# Optimizing a Trainium2 kernel written in Bass

```python
import numpy as np
import jax
import jax.numpy as jnp

def _softmax(x, axis=-1):
    return jax.nn.softmax(x, axis=axis)

def _gelu(x):
    return jax.nn.gelu(x, approximate=True)

def _silu(x):
    return jax.nn.silu(x)

def _sigmoid(x):
    return jax.nn.sigmoid(x)

def _layernorm(x, axis=-1, eps=1e-05):
    m = jnp.mean(x, axis=axis, keepdims=True)
    v = jnp.var(x, axis=axis, keepdims=True)
    return (x - m) / jnp.sqrt(v + eps)

def _scatter_add(tgt, idx, src, axis=0):
    return tgt.at[idx].add(src)

def _segment_sum(src, seg, n):
    return jax.ops.segment_sum(src, seg, n)
kernel_name = 'mk_gnn_resnorm_d2_gnn_r32_c86465'

def setup_inputs(seed: int=0):
    np.random.seed(seed)
    _w = jnp.asarray

    def _rec_inputs():
        import jax
        import jax.numpy as jnp
        _gk = jax.random.key(seed)
        x = -0.000202 + 1 * jax.random.normal(jax.random.fold_in(_gk, 1), (50000, 128), jnp.float32)
        src = jax.random.randint(jax.random.fold_in(_gk, 2), (25000,), 0, 50000, jnp.int32)
        dst = jnp.minimum((50000 * jax.random.uniform(jax.random.fold_in(_gk, 3), (25000,)) ** 2.0).astype(jnp.int32), 49999)
        _o = jnp.argsort(dst, stable=True)
        src = src[_o]
        dst = dst[_o]
        edge_attr_64 = -9.77346e-05 + 0.999888 * jax.random.normal(jax.random.fold_in(_gk, 11), (25000, 64), jnp.float32)
        return (x, src, dst, edge_attr_64)
    x, src, dst, edge_attr_64 = _rec_inputs()

    def _L0_gnn_setup():
        import jax, jax.numpy as jnp
        import numpy as np
        N_NODES = 50000
        N_EDGES = 18750
        D_IN = 128
        D_OUT = 128
        N_LAYERS = 3

        def _gin_conv(h, src, dst, eps, W1, b1, W2, b2):
            agg = jax.ops.segment_sum(h[src], dst, num_segments=N_NODES)
            z = (1.0 + eps) * h + agg
            z = jax.nn.relu(z @ W1 + b1) @ W2 + b2
            return z
        key = jax.random.key(seed)
        ks = jax.random.split(key, 16)
        s = 1.0 / np.sqrt(D_IN)
        x = jax.random.normal(ks[0], (N_NODES, D_IN), dtype=jnp.float32)
        edge_index = jax.random.randint(ks[1], (2, N_EDGES), 0, N_NODES, dtype=jnp.int64)
        W1 = jax.random.normal(ks[2], (N_LAYERS, D_IN, D_OUT), dtype=jnp.float32) * s
        b1 = jnp.zeros((N_LAYERS, D_OUT), dtype=jnp.float32)
        W2 = jax.random.normal(ks[3], (N_LAYERS, D_OUT, D_OUT), dtype=jnp.float32) * s
        b2 = jnp.zeros((N_LAYERS, D_OUT), dtype=jnp.float32)
        eps = jnp.zeros((N_LAYERS,), dtype=jnp.float32)
        d_cat = D_IN + N_LAYERS * D_OUT
        Wf = jax.random.normal(ks[4], (d_cat, D_OUT), dtype=jnp.float32) * (1.0 / np.sqrt(d_cat))
        bf = jnp.zeros((D_OUT,), dtype=jnp.float32)
        return {'x': x, 'edge_index': edge_index, 'eps': eps, 'W1': W1, 'b1': b1, 'W2': W2, 'b2': b2, 'Wf': Wf, 'bf': bf}
    _L0_gnn_all = _L0_gnn_setup()
    _L0_gnn_in = {k: v for k, v in _L0_gnn_all.items() if k in ('eps', 'W1', 'b1', 'W2', 'b2', 'Wf', 'bf')}
    del _L0_gnn_all

    def _L1_gnn_setup():
        import jax, jax.numpy as jnp
        import numpy as np
        N = 50000
        NE = 25000
        D = 128
        ED = 64
        H = 8
        HD = D // H
        key = jax.random.key(seed)
        ks = jax.random.split(key, 12)
        g = lambda k, shp: jax.random.normal(k, shp, jnp.float32) * 0.05
        return {'V': jax.random.normal(ks[0], (N, D), jnp.float32), 'E': jax.random.normal(ks[1], (NE, ED), jnp.float32), 'edge_index': jax.random.randint(ks[2], (2, NE), 0, N, jnp.int32), 'Wq': g(ks[3], (D, D)), 'bq': jnp.zeros((D,), jnp.float32), 'Wk': g(ks[4], (D, D)), 'bk': jnp.zeros((D,), jnp.float32), 'Wv': g(ks[5], (D, D)), 'bv': jnp.zeros((D,), jnp.float32), 'Wb': g(ks[6], (ED, 1)), 'bb': jnp.zeros((1,), jnp.float32), 'Wo': g(ks[7], (D, D)), 'bo': jnp.zeros((D,), jnp.float32)}
    _L1_gnn_all = _L1_gnn_setup()
    _L1_gnn_in = {k: v for k, v in _L1_gnn_all.items() if k in ('Wq', 'bq', 'Wk', 'bk', 'Wv', 'bv', 'Wb', 'bb', 'Wo', 'bo')}
    del _L1_gnn_all
    return {'x': x, 'src': src, 'dst': dst, 'edge_attr_64': edge_attr_64, 'L0_gnn_eps': _L0_gnn_in['eps'], 'L0_gnn_W1': _L0_gnn_in['W1'], 'L0_gnn_b1': _L0_gnn_in['b1'], 'L0_gnn_W2': _L0_gnn_in['W2'], 'L0_gnn_b2': _L0_gnn_in['b2'], 'L0_gnn_Wf': _L0_gnn_in['Wf'], 'L0_gnn_bf': _L0_gnn_in['bf'], 'L1_gnn_Wq': _L1_gnn_in['Wq'], 'L1_gnn_bq': _L1_gnn_in['bq'], 'L1_gnn_Wk': _L1_gnn_in['Wk'], 'L1_gnn_bk': _L1_gnn_in['bk'], 'L1_gnn_Wv': _L1_gnn_in['Wv'], 'L1_gnn_bv': _L1_gnn_in['bv'], 'L1_gnn_Wb': _L1_gnn_in['Wb'], 'L1_gnn_bb': _L1_gnn_in['bb'], 'L1_gnn_Wo': _L1_gnn_in['Wo'], 'L1_gnn_bo': _L1_gnn_in['bo']}

def reference(x, src, dst, edge_attr_64, L0_gnn_eps, L0_gnn_W1, L0_gnn_b1, L0_gnn_W2, L0_gnn_b2, L0_gnn_Wf, L0_gnn_bf, L1_gnn_Wq, L1_gnn_bq, L1_gnn_Wk, L1_gnn_bk, L1_gnn_Wv, L1_gnn_bv, L1_gnn_Wb, L1_gnn_bb, L1_gnn_Wo, L1_gnn_bo):
    import jax
    import jax.numpy as jnp

    def _L0_gnn_ref(x, edge_index, eps, W1, b1, W2, b2, Wf, bf):
        import jax, jax.numpy as jnp
        import numpy as np
        N_NODES = 50000
        N_EDGES = 18750
        D_IN = 128
        D_OUT = 128
        N_LAYERS = 3

        def _gin_conv(h, src, dst, eps, W1, b1, W2, b2):
            agg = jax.ops.segment_sum(h[src], dst, num_segments=N_NODES)
            z = (1.0 + eps) * h + agg
            z = jax.nn.relu(z @ W1 + b1) @ W2 + b2
            return z
        src, dst = (edge_index[0], edge_index[1])
        xs = [x]
        h = x
        for l in range(N_LAYERS):
            h = _gin_conv(h, src, dst, eps[l], W1[l], b1[l], W2[l], b2[l])
            xs.append(h)
        out = jnp.concatenate(xs, axis=-1)
        out = out @ Wf + bf
        return out

    def _L1_gnn_ref(V, E, edge_index, Wq, bq, Wk, bk, Wv, bv, Wb, bb, Wo, bo):
        import jax, jax.numpy as jnp
        import numpy as np
        N = 50000
        NE = 25000
        D = 128
        ED = 64
        H = 8
        HD = D // H
        src, dest = (edge_index[0], edge_index[1])
        Q = (V[src] @ Wq + bq).reshape(-1, H, HD)
        K = (V[dest] @ Wk + bk).reshape(-1, H, HD)
        Vv = (V[dest] @ Wv + bv).reshape(-1, H, HD)
        bias = E @ Wb + bb
        scores = jnp.einsum('ehd,ehd->eh', Q, K) / np.float32(np.sqrt(HD)) + bias
        m = jax.ops.segment_max(scores, dest, num_segments=N)
        ex = jnp.exp(scores - m[dest])
        den = jax.ops.segment_sum(ex, dest, num_segments=N)
        alpha = ex / den[dest]
        Hagg = jax.ops.segment_sum(alpha[..., None] * Vv, dest, num_segments=N)
        O = Hagg.reshape(N, H * HD) @ Wo + bo
        return O
    edge_index = jnp.stack([src, dst])
    x = _layernorm(x + _L0_gnn_ref(x, edge_index, L0_gnn_eps, L0_gnn_W1, L0_gnn_b1, L0_gnn_W2, L0_gnn_b2, L0_gnn_Wf, L0_gnn_bf), axis=-1)
    x = _layernorm(x + _L1_gnn_ref(x, edge_attr_64, edge_index, L1_gnn_Wq, L1_gnn_bq, L1_gnn_Wk, L1_gnn_bk, L1_gnn_Wv, L1_gnn_bv, L1_gnn_Wb, L1_gnn_bb, L1_gnn_Wo, L1_gnn_bo), axis=-1)
    return x

_drawn_inputs = setup_inputs


def setup_inputs(seed=0):
    import zlib

    import numpy as np

    out = dict(_drawn_inputs(seed))
    spreads = {'L0_gnn_eps': (0.0, 0.269),
     'L0_gnn_b1': (0.0, 0.1),
     'L0_gnn_b2': (0.0, 0.1),
     'L0_gnn_bf': (0.0, 0.1),
     'L1_gnn_bq': (0.0, 2.0),
     'L1_gnn_bk': (0.0, 2.0),
     'L1_gnn_bv': (0.0, 0.1),
     'L1_gnn_bo': (0.0, 0.1)}
    factors = {'edge_attr_64': 200.0, 'L1_gnn_Wq': 200.0, 'L1_gnn_Wk': 200.0, 'L1_gnn_Wb': 200.0}
    for name, (base, spread) in spreads.items():
        noise = np.random.default_rng([zlib.crc32(name.encode()), seed]).standard_normal(out[name].shape)
        drawn = base * np.exp(spread * noise) if base else spread * noise
        out[name] = jnp.asarray(drawn.astype(out[name].dtype))
    for name, factor in factors.items():
        out[name] = (out[name] * factor).astype(out[name].dtype)
    return out
```

```python
from contextlib import ExitStack

import concourse.bass as bass
from concourse import mybir

F32 = mybir.dt.float32
I32 = mybir.dt.int32
U8 = mybir.dt.uint8
ALU = mybir.AluOpType
ACT = mybir.ActivationFunctionType

P = 128
N = 50000
E = 25000
D = 128
ED = 64
H = 8
HD = D // H
LAYERS = 3
NR = 4
NT = NR * P
ER = 2
ET = ER * P
STEPS = -(-E // (2 * ET))
EP = STEPS * 2 * ET
TILES = EP // P
CHUNK = 2 * ER
LAST_NODE = N - NT
ROWS = N + EP
PAD_DST = 1 << 20
EDGE_OF_LIST = PAD_DST + 1
SKIP = 1 << 21
LN_EPS = 1e-5
FAR = 1e30

assert (2 * STEPS - 1) * NT < N <= 2 * STEPS * NT and E > EP - P




def settle(eng, passed):
    eng.sem_inc(passed, 1)


def reuse(eng, sem, count):
    if not isinstance(count, int) or count > 0:
        eng.wait_ge(sem, count)


class Memory:
    pass


def lay_out(nc, ctx):
    m = Memory()

    def sb(name, shape, dt=F32):
        return ctx.enter_context(nc.sbuf_tensor(name, shape, dt))

    m.y1_table = nc.dram_tensor("y1_table", (ROWS, D), F32).ap()
    m.y2_table = nc.dram_tensor("y2_table", (ROWS, D), F32).ap()
    m.x1_table = nc.dram_tensor("x1_table", (ROWS, D), F32).ap()
    m.skip_rows = nc.dram_tensor("skip_rows", (EP, D), F32).ap()
    m.row_of_node = nc.dram_tensor("row_of_node", (N, 1), I32).ap()
    m.dst_list = nc.dram_tensor("dst_list", (EP + 2, 1), I32).ap()
    m.src_list = nc.dram_tensor("src_list", (EP, 1), I32).ap()

    m.W1_0 = sb("W1_0", [P, P])
    m.W0f = sb("W0f", [P, P])
    m.G3 = sb("G3", [P, P])
    m.Wq = sb("Wq", [P, P])
    m.Wk = sb("Wk", [P, P])
    m.Wv = sb("Wv", [P, P])
    m.Wo = sb("Wo", [P, P])
    m.ident = sb("ident", [P, P])
    m.MG1 = sb("MG1", [P, 2 * P])
    m.MG2 = sb("MG2", [P, 2 * P])
    m.b1 = sb("b1", [P, LAYERS])
    m.scale = sb("scale", [P, LAYERS])
    m.c = sb("c", [P, 2])
    m.c_row = sb("c_row", [1, 2, P])
    m.beta = sb("beta", [P, 2])
    m.ones_row = sb("ones_row", [1, P])
    m.cf = sb("cf", [P, NR, P])
    m.bo = sb("bo", [P, NR, P])
    m.bqkv = sb("bqkv", [P, 3])
    m.Wb8 = sb("Wb8", [ED, H])
    m.bb8 = sb("bb8", [H, 1])
    m.head_sum = sb("head_sum", [P, H])
    m.head_spread = sb("head_spread", [H, P])
    m.minus_half = sb("minus_half", [P, NR])

    m.src_idx = sb("src_idx", [P, TILES], I32)
    m.dst_idx = sb("dst_idx", [P, TILES], I32)
    m.slot_to = sb("slot_to", [P, TILES], I32)
    m.final_to = sb("final_to", [P, TILES], I32)
    m.slot_row = sb("slot_row", [P, TILES], I32)
    m.src_row = sb("src_row", [P, TILES], I32)

    m.same = sb("same", [P, EP + 1], U8)
    m.slots = sb("slots", [P, EP])
    return m


def sem_maker(nc, ctx, phase):
    made = []

    def give_back():
        nc.clear_and_free_semaphores(made)
        nc.all_engine_barrier()

    ctx.callback(give_back)

    def sem(name):
        made.append(nc.alloc_semaphore(f"{phase}_{name}"))
        return made[-1]

    def pair(name):
        return [sem(f"{name}{h}") for h in range(2)]

    return sem, pair



def prepare(nc, m, a):
    with ExitStack() as ctx:
        sem, pair = sem_maker(nc, ctx, "prep")

        def sb(name, shape, dt=F32):
            return ctx.enter_context(nc.sbuf_tensor(name, shape, dt))

        def ps(name, shape):
            return ctx.enter_context(nc.psum_tensor(name, shape, F32))

        HI = P
        LO = TILES - P
        pads = EP - E
        fill = sb("fill", [1, 3 * P], I32)
        own = sb("own", [125, N // 125], I32)
        rows_i = sb("rows_i", [P, 4, 2, P], I32)
        rows_f = sb("rows_f", [P, 4, 2, P])
        cols = sb("cols", [P, 4, TILES])
        eq = sb("eq", [P, 2, TILES])
        W1 = sb("W1", [P, 2, P])
        W2 = sb("W2", [P, LAYERS, P])
        W2T = sb("W2T", [P, LAYERS, P])
        Wf = sb("Wf", [P, LAYERS + 1, P])
        WW = sb("WW", [P, 2, 2, P])
        b2 = sb("b2", [P, LAYERS])
        b2_wide = sb("b2_wide", [P, LAYERS, P])
        bf = sb("bf", [P, P])
        bo1 = sb("bo1", [P, P])
        pT = [ps(f"pT{q}", [P, 512]) for q in range(4)]
        pW = ps("pW", [P, LAYERS, P])
        pG = ps("pG", [P, 512])
        pC = ps("pC", [P, 512])

        filled = sem("filled")
        owned = sem("owned")
        lists = sem("lists")
        own_out = sem("own_out")
        index_in = sem("index_in")
        floats = sem("floats")
        turned = sem("turned")
        cols_ready = sem("cols_ready")
        eq_ready = sem("eq_ready")
        idx_done = sem("idx_done")
        w_in = sem("w_in")
        id_made = sem("id_made")
        iota_done = sem("iota_done")
        heads = sem("heads")
        w2_turned = sem("w2_turned")
        w2T_ready = sem("w2T_ready")
        wide_ready = sem("wide_ready")
        products = sem("products")
        prod_out = sem("prod_out")
        small = sem("small")
        consts = sem("consts")
        block = ctx.enter_context(nc.Block())

        @block.sync
        def _(sp):
            sp.wait_ge(filled, 3)
            sp.dma_start(m.dst_list[0:1, :], fill[0:1, 0:1]).then_inc(lists, 16)
            sp.dma_start(m.dst_list[1:1 + E, :].rearrange("(a b) c -> a (b c)", b=E // 40),
                         a["dst"].rearrange("(a b) -> a b", b=E // 40)).then_inc(lists, 16)
            sp.dma_start(m.dst_list[1 + E:1 + EP, :].rearrange("a c -> c a"),
                         fill[0:1, P:P + pads]).then_inc(lists, 16)
            sp.dma_start(m.dst_list[1 + EP:2 + EP, :], fill[0:1, 0:1]).then_inc(lists, 16)
            sp.dma_start(m.src_list[0:E, :].rearrange("(a b) c -> a (b c)", b=E // 40),
                         a["src"].rearrange("(a b) -> a b", b=E // 40)).then_inc(lists, 16)
            sp.dma_start(m.src_list[E:EP, :].rearrange("a c -> c a"),
                         fill[0:1, 2 * P:2 * P + pads]).then_inc(lists, 16)
            sp.wait_ge(owned, 1)
            sp.dma_start(m.row_of_node.rearrange("(p n) c -> p (n c)", p=125), own[:, :]).then_inc(own_out, 16)
            sp.wait_ge(lists, 96)
            for q, (lst, off) in enumerate(((m.dst_list, 1), (m.dst_list, 0), (m.dst_list, 2), (m.src_list, 0))):
                sp.dma_start(rows_i[:, q, 0, :],
                             lst[off:off + HI * P, :].rearrange("(t p) c -> t (p c)", p=P)).then_inc(index_in, 16)
                sp.dma_start(rows_i[0:LO, q, 1, :],
                             lst[off + HI * P:off + EP, :].rearrange("(t p) c -> t (p c)", p=P)
                             ).then_inc(index_in, 16)
            sp.wait_ge(own_out, 16)

        loads = [
            (m.W1_0[:, :], a["W1"][0]), (W1[:, 0, :], a["W1"][1]), (W1[:, 1, :], a["W1"][2]),
            (W2[:, :, :], a["W2"].rearrange("l k n -> k l n")),
            (Wf[:, :, :], a["Wf"].rearrange("(l k) n -> k l n", k=P)),
            (m.Wq[:, :], a["Wq"]), (m.Wk[:, :], a["Wk"]), (m.Wv[:, :], a["Wv"]), (m.Wo[:, :], a["Wo"]),
            (m.b1[:, :], a["b1"].rearrange("l k -> k l")),
            (b2[:, :], a["b2"].rearrange("l k -> k l")),
            (m.scale[:, :], a["eps"].rearrange("(o l) -> o l", o=1).to_broadcast([P, LAYERS])),
            (bf[:, :], a["bf"].rearrange("(o n) -> o n", o=1).to_broadcast([P, P])),
            (bo1[:, :], a["bo"].rearrange("(o n) -> o n", o=1).to_broadcast([P, P])),
            (m.bqkv[:, 0:1], a["bq"].rearrange("(n o) -> n o", o=1)),
            (m.bqkv[:, 1:2], a["bk"].rearrange("(n o) -> n o", o=1)),
            (m.bqkv[:, 2:3], a["bv"].rearrange("(n o) -> n o", o=1)),
            (m.Wb8[:, 0:1], a["Wb"]),
            (m.bb8[:, :], a["bb"].rearrange("(o n) -> o n", o=1).to_broadcast([H, 1])),
        ]
        W_DMAS = len(loads)

        @block.scalar
        def _(act):
            with nc.allow_non_contiguous_dma(reason="a few hundred bias values, once"):
                for dst, src in loads:
                    act.dma_start(dst, src).then_inc(w_in, 16)

        @block.gpsimd
        def _(pool):
            nc.gpsimd.iota(own[:, :], pattern=[[1, N // 125]], base=0, channel_multiplier=N // 125
                           ).then_inc(owned, 1)
            nc.gpsimd.iota(m.slot_row[:, :], pattern=[[P, TILES]], base=N, channel_multiplier=1
                           ).then_inc(iota_done, 1)
            nc.gpsimd.memset(m.ident[:, :], 0.0).then_inc(id_made, 1)
            pool.wait_ge(id_made, 1)
            nc.gpsimd.affine_select(out=m.ident[:, :], in_=m.ident[:, :], compare_op=ALU.not_equal, fill=1.0,
                                    base=0, pattern=[[-1, P]], channel_multiplier=1).then_inc(id_made, 1)
            nc.gpsimd.memset(m.head_sum[:, :], float(HD) ** -0.5).then_inc(heads, 1)
            nc.gpsimd.memset(m.head_spread[:, :], 1.0).then_inc(heads, 1)
            pool.wait_ge(heads, 2)
            nc.gpsimd.affine_select(out=m.head_sum[:, :], in_=m.head_sum[:, :], compare_op=ALU.is_ge, fill=0.0,
                                    base=0, pattern=[[-HD, H]], channel_multiplier=1).then_inc(heads, 1)
            nc.gpsimd.affine_select(out=m.head_spread[:, :], in_=m.head_spread[:, :], compare_op=ALU.is_ge,
                                    fill=0.0, base=0, pattern=[[1, P]], channel_multiplier=-HD).then_inc(heads, 1)
            pool.wait_ge(heads, 4)
            nc.gpsimd.affine_select(out=m.head_sum[:, :], in_=m.head_sum[:, :], compare_op=ALU.is_ge, fill=0.0,
                                    base=HD - 1, pattern=[[HD, H]], channel_multiplier=-1).then_inc(heads, 1)
            nc.gpsimd.affine_select(out=m.head_spread[:, :], in_=m.head_spread[:, :], compare_op=ALU.is_ge,
                                    fill=0.0, base=HD - 1, pattern=[[-1, P]], channel_multiplier=HD
                                    ).then_inc(heads, 1)

        @block.tensor
        def _(pe):
            pe.wait_ge(id_made, 2)
            pe.wait_ge(w_in, 16 * W_DMAS)
            for l in range(LAYERS):
                last = nc.tensor.transpose(pW[:, l, :], W2[:, l, :], m.ident[:, :])
            last.then_inc(w2_turned, 1)
            pe.wait_ge(floats, 4)
            for q in range(4):
                nc.tensor.transpose(pT[q][:, 0:P], rows_f[:, q, 0, :], m.ident[:, :])
                last = nc.tensor.transpose(pT[q][:, P:TILES], rows_f[0:LO, q, 1, :], m.ident[0:LO, 0:LO])
                last.then_inc(turned, 1)
            pe.wait_ge(w2T_ready, 1)
            pe.wait_ge(wide_ready, 3)
            nc.tensor.matmul(pG[:, 0:2 * P], W2T[:, 0, :], WW[:, 0].rearrange("p a b -> p (a b)"),
                             start=True, stop=True)
            last = nc.tensor.matmul(pG[:, 2 * P:4 * P], W2T[:, 1, :], WW[:, 1].rearrange("p a b -> p (a b)"),
                                    start=True, stop=True)
            last.then_inc(products, 1)
            pe.wait_ge(cols_ready, 4)
            nc.tensor.matmul(pT[0][:, 0:P], W2T[:, 2, :], Wf[:, 3, :], start=True, stop=True)
            nc.tensor.matmul(pT[1][0:1, 0:P], b2[:, 0:1], W1[:, 0, :], start=True, stop=True)
            nc.tensor.matmul(pT[1][0:1, P:2 * P], b2[:, 1:2], W1[:, 1, :], start=True, stop=True)
            nc.tensor.matmul(pT[2][:, 0:1], W1[:, 0, :], b2[:, 0:1], start=True, stop=True)
            nc.tensor.matmul(pT[2][:, 1:2], W1[:, 1, :], b2[:, 1:2], start=True, stop=True)
            for l in range(LAYERS):
                last = nc.tensor.matmul(pC[:, 0:P], b2_wide[:, l, :], Wf[:, l + 1, :],
                                        start=(l == 0), stop=(l == LAYERS - 1))
            last.then_inc(products, 1)

        @block.vector
        def _(dve):
            nc.vector.memset(fill[:, 0:P], EDGE_OF_LIST).then_inc(filled, 1)
            nc.vector.memset(fill[:, P:2 * P], PAD_DST).then_inc(filled, 1)
            nc.vector.memset(fill[:, 2 * P:3 * P], 0).then_inc(filled, 1)
            nc.vector.memset(m.ones_row[:, :], 1.0).then_inc(consts, 1)
            nc.vector.memset(m.minus_half[:, :], -0.5).then_inc(consts, 1)
            nc.vector.memset(m.same[:, EP:EP + 1], 0).then_inc(consts, 1)
            dve.wait_ge(w_in, 16 * W_DMAS)
            nc.vector.tensor_copy(WW[:, :, 0, :], W1[:, :, :]).then_inc(wide_ready, 1)
            nc.vector.tensor_copy(WW[:, :, 1, :], Wf[:, 1:3, :]).then_inc(wide_ready, 1)
            nc.vector.tensor_copy(b2_wide[:, :, :], b2[:, :].unsqueeze(2).to_broadcast([P, LAYERS, P])
                                  ).then_inc(wide_ready, 1)
            nc.vector.tensor_copy(m.bo[:, :, :], bo1[:, :].unsqueeze(1).to_broadcast([P, NR, P])
                                  ).then_inc(consts, 1)
            nc.vector.tensor_copy(m.Wb8[:, 1:H], m.Wb8[:, 0:1].to_broadcast([ED, H - 1])).then_inc(consts, 1)
            nc.vector.tensor_scalar(m.scale[:, :], m.scale[:, :], 1.0, None, ALU.add).then_inc(small, 1)
            dve.wait_ge(w2_turned, 1)
            nc.vector.tensor_copy(W2T[:, :, :], pW[:, :, :]).then_inc(w2T_ready, 1)
            dve.wait_ge(id_made, 2)
            nc.vector.tensor_tensor(m.W0f[:, :], Wf[:, 0, :], m.ident[:, :], ALU.add).then_inc(consts, 1)
            dve.wait_ge(index_in, 128)
            for q in range(4):
                nc.vector.tensor_copy(rows_f[:, q, 0, :], rows_i[:, q, 0, :])
                nc.vector.tensor_copy(rows_f[0:LO, q, 1, :], rows_i[0:LO, q, 1, :]).then_inc(floats, 1)
            for q in range(4):
                dve.wait_ge(turned, q + 1)
                nc.vector.tensor_copy(cols[:, q, :], pT[q][:, 0:TILES]).then_inc(cols_ready, 1)
            dve.wait_ge(cols_ready, 4)
            nc.vector.tensor_tensor(eq[:, 0, :], cols[:, 0, :], cols[:, 1, :], ALU.is_equal).then_inc(eq_ready, 1)
            nc.vector.tensor_tensor(eq[:, 1, :], cols[:, 0, :], cols[:, 2, :], ALU.is_equal).then_inc(eq_ready, 1)
            nc.vector.tensor_copy(m.src_idx[:, :], cols[:, 3, :]).then_inc(idx_done, 1)
            nc.vector.tensor_scalar(m.dst_idx[:, :], cols[:, 0, :], float(N - 1), None, ALU.min
                                    ).then_inc(idx_done, 1)
            dve.wait_ge(eq_ready, 2)
            nc.vector.scalar_tensor_tensor(out=m.final_to[:, :], in0=eq[:, 0, :], scalar=float(SKIP),
                                           in1=cols[:, 0, :], op0=ALU.mult, op1=ALU.add).then_inc(idx_done, 1)
            nc.vector.scalar_tensor_tensor(out=m.slot_to[:, :], in0=eq[:, 1, :], scalar=float(SKIP),
                                           in1=cols[:, 0, :], op0=ALU.mult, op1=ALU.add).then_inc(idx_done, 1)
            dve.wait_ge(products, 2)
            nc.vector.tensor_copy(m.MG1[:, :], pG[:, 0:2 * P]).then_inc(prod_out, 1)
            nc.vector.tensor_copy(m.MG2[:, :], pG[:, 2 * P:4 * P]).then_inc(prod_out, 1)
            nc.vector.tensor_copy(m.G3[:, :], pT[0][:, 0:P]).then_inc(prod_out, 1)
            nc.vector.tensor_copy(m.c_row[:, :, :], pT[1][0:1, 0:2 * P].rearrange("o (a b) -> o a b", a=2)
                                  ).then_inc(prod_out, 1)
            nc.vector.tensor_copy(m.c[:, :], pT[2][:, 0:2]).then_inc(prod_out, 1)
            nc.vector.tensor_tensor(m.cf[:, 0, :], pC[:, 0:P], bf[:, :], ALU.add).then_inc(prod_out, 1)
            dve.wait_ge(prod_out, 6)
            dve.wait_ge(small, 1)
            nc.vector.tensor_copy(m.cf[:, 1:NR, :], m.cf[:, 0:1, :].to_broadcast([P, NR - 1, P])
                                  ).then_inc(consts, 1)
            nc.vector.tensor_tensor(m.beta[:, :], m.c[:, :], m.scale[:, 1:3], ALU.mult).then_inc(small, 1)
            dve.wait_ge(small, 2)
            nc.vector.tensor_tensor(m.beta[:, :], m.beta[:, :], m.b1[:, 1:3], ALU.add).then_inc(consts, 1)



def node_rows(t, start):
    return t[bass.DynSlice(start, NT), :].rearrange("(p j) d -> p (j d)", j=NR)


def edge_rows(t, start):
    return t[bass.DynSlice(start, ET), :].rearrange("(j p) d -> p j d", p=P)


def nodes_and_first_layer(nc, m, a, out):
    with ExitStack() as ctx:
        sem, pair = sem_maker(nc, ctx, "nodes")

        def sb2(name, shape, dt=F32):
            return [ctx.enter_context(nc.sbuf_tensor(f"{name}{h}", shape, dt)) for h in range(2)]

        def sb(name, shape, dt=F32):
            return ctx.enter_context(nc.sbuf_tensor(name, shape, dt))

        def ps(name, shape):
            return ctx.enter_context(nc.psum_tensor(name, shape, F32))

        x_in = sb2("x_in", [P, NT])
        xT = sb2("xT", [P, NT])
        r1 = sb2("r1", [P, NT])
        r2 = sb2("r2", [P, NT])
        r3 = sb2("r3", [P, NT])
        y1s = sb2("y1s", [P, NT])
        y2s = sb2("y2s", [P, NT])
        u = sb2("u", [P, NR, P])
        x1s = sb2("x1s", [P, NR, P])
        fins = sb2("fins", [P, NR, P])
        stats = sb2("stats", [P, 2, NR, 6])
        mv = sb2("mv", [P, 2, NR, 2])
        vare = sb2("vare", [P, 2, NR])
        rstd = sb2("rstd", [P, 2, NR])
        dst_wide = sb("dst_wide", [P, 2 * ET + 1], I32)
        stage = sb("stage", [P, 2 * CHUNK], I32)
        slot_stage = sb("slot_stage", [P, 4, CHUNK], I32)
        found = sb("found", [P, 2 * CHUNK], I32)
        gs = sb2("gs", [P, ER, P])
        gd = sb2("gd", [P, ER, P])
        xdT = sb2("xdT", [P, ET])
        agg = sb2("agg", [P, ET])
        z = sb2("z", [P, ET])
        re = sb2("re", [P, ET])
        rows_s = sb2("rows_s", [P, ER, 2 * P])

        chain = [ps(f"chain{h}", [P, NT]) for h in range(2)]
        yb = [ps(f"yb{h}", [P, NT]) for h in range(2)]
        ob = ps("ob", [P, NR, P])
        e0 = ps("e0", [P, 2, ET])
        e1 = ps("e1", [P, 2, ET])
        e2 = ps("e2", [P, ER, 2 * P])

        x_loaded = pair("x_loaded")
        t_done = pair("t_done")
        xT_ready = pair("xT_ready")
        l1_done = pair("l1_done")
        r1_ready = pair("r1_ready")
        l2_done = pair("l2_done")
        r2_ready = pair("r2_ready")
        l3_done = pair("l3_done")
        r3_ready = pair("r3_ready")
        y1_done = pair("y1_done")
        y1_out = pair("y1_out")
        y1_stored = pair("y1_stored")
        y2_done = pair("y2_done")
        y2_out = pair("y2_out")
        y2_stored = pair("y2_stored")
        o_done = pair("o_done")
        u_ready = pair("u_ready")
        stats_ready = [pair(f"stats_ready{n}") for n in range(2)]
        mv_ready = [pair(f"mv_ready{n}") for n in range(2)]
        var_ready = [pair(f"var_ready{n}") for n in range(2)]
        rstd_ready = [pair(f"rstd_ready{n}") for n in range(2)]
        x1_ready = pair("x1_ready")
        x1_stored = pair("x1_stored")
        v_ready = pair("v_ready")
        fin_ready = pair("fin_ready")
        fin_stored = pair("fin_stored")
        dst_loaded = sem("dst_loaded")
        mask_ready = sem("mask_ready")
        carry_ready = sem("carry_ready")
        staged = sem("staged")
        slots_staged = sem("slots_staged")
        slots_put = sem("slots_put")
        rows_found = sem("rows_found")
        found_kept = sem("found_kept")
        gathered = pair("gathered")
        te_done = pair("te_done")
        xdT_ready = pair("xdT_ready")
        agg_ready = pair("agg_ready")
        z_ready = pair("z_ready")
        le_done = pair("le_done")
        re_ready = pair("re_ready")
        me_done = pair("me_done")
        slot_ready = pair("slot_ready")
        rows_done = pair("rows_done")
        rows_out = pair("rows_out")
        rows_stored = pair("rows_stored")
        passed_pool = sem("passed_pool")
        passed_dve = sem("passed_dve")
        block = ctx.enter_context(nc.Block())

        @block.sync
        def _(sp):
            def load(i, last=False):
                for h in range(2):
                    reuse(sp, t_done[h], i)
                    start = LAST_NODE if last and h == 1 else (2 * i + h) * NT
                    sp.dma_start(x_in[h][:, :], node_rows(a["x"], start)).then_inc(x_loaded[h], 16)
                reuse(sp, mask_ready, i)
                sp.dma_start(dst_wide[:, :],
                             m.dst_list[bass.DynSlice(i * 2 * ET, 2 * ET + 1), :].rearrange("n o -> o n")
                             .to_broadcast([P, 2 * ET + 1])).then_inc(dst_loaded, 16)

            def store(i, last=False):
                for h in range(2):
                    start = LAST_NODE if last and h == 1 else (2 * i + h) * NT
                    if last and h == 1:
                        sp.wait_ge(y1_stored[0], 16 * STEPS)
                        sp.wait_ge(y2_stored[0], 16 * STEPS)
                        sp.wait_ge(x1_stored[0], 16 * STEPS)
                        sp.wait_ge(fin_stored[0], 16 * STEPS)
                    sp.wait_ge(y1_out[h], i + 1)
                    sp.dma_start(node_rows(m.y1_table, start), y1s[h][:, :]).then_inc(y1_stored[h], 16)
                    sp.wait_ge(y2_out[h], i + 1)
                    sp.dma_start(node_rows(m.y2_table, start), y2s[h][:, :]).then_inc(y2_stored[h], 16)
                    sp.wait_ge(rows_out[h], i + 1)
                    edge = (2 * i + h) * ET
                    sp.dma_start(edge_rows(m.y1_table, edge + N), rows_s[h][:, :, 0:P]
                                 ).then_inc(rows_stored[h], 16)
                    sp.dma_start(edge_rows(m.skip_rows, edge), rows_s[h][:, :, P:2 * P]
                                 ).then_inc(rows_stored[h], 16)
                    sp.wait_ge(x1_ready[h], i + 1)
                    sp.dma_start(node_rows(m.x1_table, start), x1s[h].rearrange("p j d -> p (j d)")
                                 ).then_inc(x1_stored[h], 16)
                    sp.wait_ge(fin_ready[h], i + 1)
                    sp.dma_start(node_rows(out, start), fins[h].rearrange("p j d -> p (j d)")
                                 ).then_inc(fin_stored[h], 16)

            load(0)
            load(1)
            store(0)
            with sp.Fori(1, STEPS - 2) as i:
                load(i + 1)
                store(i)
            load(STEPS - 1, last=True)
            store(STEPS - 2)
            store(STEPS - 1, last=True)
            for h in range(2):
                for s in (y1_stored, y2_stored, x1_stored, fin_stored):
                    sp.wait_ge(s[h], 16 * STEPS)
                sp.wait_ge(rows_stored[h], 32 * STEPS)

        @block.tensor
        def _(pe):
            def node_turn(i, h):
                pe.wait_ge(x_loaded[h], 16 * (i + 1))
                reuse(pe, r3_ready[h], i)
                for j in range(NR):
                    last = nc.tensor.transpose(chain[h][:, j * P:(j + 1) * P], x_in[h][:, j * P:(j + 1) * P],
                                               m.ident[:, :])
                last.then_inc(t_done[h], 1)

            def layer(i, h, ready, w, src, done):
                pe.wait_ge(ready[h], i + 1)
                nc.tensor.matmul(chain[h][:, :], w, src[h][:, :], start=True, stop=True).then_inc(done[h], 1)

            def y_rows(i, h, free, count, w, src, done):
                pe.wait_ge(free[h], count)
                for j in range(NR):
                    last = nc.tensor.matmul(yb[h][:, j * P:(j + 1) * P], src[h][:, j * P:(j + 1) * P], w,
                                            start=True, stop=True)
                last.then_inc(done[h], 1)

            def out_rows(i, h):
                pe.wait_ge(r3_ready[h], i + 1)
                reuse(pe, u_ready[1 - h], i + h)
                for j in range(NR):
                    cut = slice(j * P, (j + 1) * P)
                    nc.tensor.matmul(ob[:, j, :], xT[h][:, cut], m.W0f[:, :], start=True, stop=False)
                    nc.tensor.matmul(ob[:, j, :], r1[h][:, cut], m.MG1[:, P:2 * P], start=False, stop=False)
                    nc.tensor.matmul(ob[:, j, :], r2[h][:, cut], m.MG2[:, P:2 * P], start=False, stop=False)
                    last = nc.tensor.matmul(ob[:, j, :], r3[h][:, cut], m.G3[:, :], start=False, stop=True)
                last.then_inc(o_done[h], 1)

            def edge_turn(i, h):
                pe.wait_ge(gathered[h], 64 * (i + 1))
                reuse(pe, agg_ready[1 - h], i + h)
                reuse(pe, xdT_ready[1 - h], i + h)
                for j in range(ER):
                    nc.tensor.transpose(e0[:, 0, j * P:(j + 1) * P], gs[h][:, j, :], m.ident[:, :])
                for j in range(ER):
                    last = nc.tensor.transpose(e0[:, 1, j * P:(j + 1) * P], gd[h][:, j, :], m.ident[:, :])
                last.then_inc(te_done[h], 1)

            def edge_layer(i, h):
                pe.wait_ge(z_ready[h], i + 1)
                reuse(pe, slot_ready[1 - h], i + h)
                nc.tensor.matmul(e1[:, 0, :], m.W1_0[:, :], z[h][:, :], start=True, stop=True
                                 ).then_inc(le_done[h], 1)

            def edge_rows_out(i, h):
                pe.wait_ge(re_ready[h], i + 1)
                nc.tensor.matmul(e1[:, 1, :], m.MG1[:, 0:P], re[h][:, :], start=True, stop=True
                                 ).then_inc(me_done[h], 1)
                pe.wait_ge(xdT_ready[h], i + 1)
                reuse(pe, rows_out[1 - h], i + h)
                for j in range(ER):
                    cut = slice(j * P, (j + 1) * P)
                    nc.tensor.matmul(e2[:, j, :], re[h][:, cut], m.MG1[:, :], start=True, stop=True,
                                     skip_group_check=True)
                    last = nc.tensor.matmul(e2[:, j, P:2 * P], xdT[h][:, cut], m.W0f[:, :], start=False,
                                            stop=True, skip_group_check=True)
                last.then_inc(rows_done[h], 1)

            def step(i):
                node_turn(i, 0)
                node_turn(i, 1)
                layer(i, 0, xT_ready, m.W1_0[:, :], xT, l1_done)
                layer(i, 1, xT_ready, m.W1_0[:, :], xT, l1_done)
                edge_turn(i, 0)
                for h in range(2):
                    layer(i, h, r1_ready, m.MG1[:, 0:P], r1, l2_done)
                    y_rows(i, h, y2_out, i, m.MG1[:, 0:P], r1, y1_done)
                edge_layer(i, 0)
                edge_turn(i, 1)
                for h in range(2):
                    layer(i, h, r2_ready, m.MG2[:, 0:P], r2, l3_done)
                    y_rows(i, h, y1_out, i + 1, m.MG2[:, 0:P], r2, y2_done)
                edge_rows_out(i, 0)
                edge_layer(i, 1)
                out_rows(i, 0)
                edge_rows_out(i, 1)
                out_rows(i, 1)

            step(0)
            with pe.Fori(1, STEPS) as i:
                step(i)

        @block.scalar
        def _(act):
            def turn_out(i, h):
                act.wait_ge(t_done[h], i + 1)
                reuse(act, o_done[h], i)
                nc.scalar.activation(xT[h][:, :], chain[h][:, :], ACT.Copy).then_inc(xT_ready[h], 1)

            def relu(i, h, done, scale, bias, dst, ready):
                act.wait_ge(done[h], i + 1)
                nc.scalar.activation(dst[h][:, :], chain[h][:, :], ACT.Relu, bias=bias, scale=scale
                                     ).then_inc(ready[h], 1)

            def y_out(i, h, done, stored, dst, copied):
                act.wait_ge(done[h], i + 1)
                reuse(act, stored[h], 16 * i)
                nc.scalar.activation(dst[h][:, :], yb[h][:, :], ACT.Copy).then_inc(copied[h], 1)

            def edge_turn_out(i, h):
                act.wait_ge(te_done[h], i + 1)
                reuse(act, rows_done[h], i)
                reuse(act, z_ready[h], i)
                nc.scalar.activation(xdT[h][:, :], e0[:, 1, :], ACT.Copy).then_inc(xdT_ready[h], 1)

            def edge_relu(i, h):
                act.wait_ge(le_done[h], i + 1)
                reuse(act, rows_done[h], i)
                nc.scalar.activation(re[h][:, :], e1[:, 0, :], ACT.Relu, bias=m.b1[:, 0:1]
                                     ).then_inc(re_ready[h], 1)

            def edge_out(i, h):
                act.wait_ge(me_done[h], i + 1)
                nc.scalar.activation(m.slots[:, bass.DynSlice((2 * i + h) * ET, ET)], e1[:, 1, :],
                                     ACT.Identity, bias=m.c[:, 0:1]).then_inc(slot_ready[h], 1)
                act.wait_ge(rows_done[h], i + 1)
                reuse(act, rows_stored[h], 32 * i)
                nc.scalar.activation(rows_s[h][:, :, :], e2[:, :, :], ACT.Copy).then_inc(rows_out[h], 1)

            def step(i):
                turn_out(i, 0)
                turn_out(i, 1)
                relu(i, 0, l1_done, m.scale[:, 0:1], m.b1[:, 0:1], r1, r1_ready)
                relu(i, 1, l1_done, m.scale[:, 0:1], m.b1[:, 0:1], r1, r1_ready)
                edge_turn_out(i, 0)
                for h in range(2):
                    relu(i, h, l2_done, m.scale[:, 1:2], m.beta[:, 0:1], r2, r2_ready)
                    y_out(i, h, y1_done, y1_stored, y1s, y1_out)
                edge_relu(i, 0)
                edge_turn_out(i, 1)
                for h in range(2):
                    relu(i, h, l3_done, m.scale[:, 2:3], m.beta[:, 1:2], r3, r3_ready)
                    y_out(i, h, y2_done, y2_stored, y2s, y2_out)
                edge_out(i, 0)
                edge_relu(i, 1)
                edge_out(i, 1)

            step(0)
            with act.Fori(1, STEPS) as i:
                step(i)

        @block.vector
        def _(dve):
            nc.vector.memset(agg[1][:, :], 0.0).then_inc(carry_ready, 1)
            dve.wait_ge(carry_ready, 1)

            def mask(i):
                dve.wait_ge(dst_loaded, 16 * (i + 1))
                nc.vector.tensor_tensor(m.same[:, bass.DynSlice(i * 2 * ET, 2 * ET)], dst_wide[:, 1:2 * ET + 1],
                                        dst_wide[:, 0:2 * ET], ALU.is_equal).then_inc(mask_ready, 1)
                dve.wait_ge(mask_ready, i + 1)

            def sums(i, h):
                dve.wait_ge(xdT_ready[h], i + 1)
                reuse(dve, agg_ready[1 - h], i + h)
                nc.vector.tensor_tensor_scan(agg[h][:, :], m.same[:, bass.DynSlice((2 * i + h) * ET, ET)],
                                             e0[:, 0, :], agg[1 - h][:, ET - 1:ET], ALU.mult, ALU.add
                                             ).then_inc(agg_ready[h], 1)
                dve.wait_ge(agg_ready[h], i + 1)
                reuse(dve, le_done[h], i)
                nc.vector.scalar_tensor_tensor(out=z[h][:, :], in0=xdT[h][:, :], scalar=m.scale[:, 0:1],
                                               in1=agg[h][:, :], op0=ALU.mult, op1=ALU.add
                                               ).then_inc(z_ready[h], 1)

            def moments(i, h, n, src, src_ready):
                dve.wait_ge(src_ready[h], i + 1)
                for j in range(NR):
                    nc.vector.bn_stats(stats[h][:, n, j, :], src[h][:, j, :]).then_inc(stats_ready[n][h], 1)
                dve.wait_ge(stats_ready[n][h], NR * (i + 1))
                settle(dve, passed_dve)
                for j in range(NR):
                    nc.vector.bn_aggr(mv[h][:, n, j, :], stats[h][:, n, j, :]).then_inc(mv_ready[n][h], 1)
                dve.wait_ge(mv_ready[n][h], NR * (i + 1))
                nc.vector.tensor_scalar(vare[h][:, n, :], mv[h][:, n, :, 1], LN_EPS, None, ALU.add
                                        ).then_inc(var_ready[n][h], 1)

            def step(i):
                mask(i)
                sums(i, 0)
                sums(i, 1)
                for h in range(2):
                    dve.wait_ge(o_done[h], i + 1)
                    nc.vector.tensor_tensor(u[h][:, :, :], ob[:, :, :], m.cf[:, :, :], ALU.add
                                            ).then_inc(u_ready[h], 1)
                    moments(i, h, 0, u, u_ready)
                for h in range(2):
                    dve.wait_ge(rstd_ready[0][h], i + 1)
                    reuse(dve, x1_stored[h], 16 * i)
                    for j in range(NR):
                        last = nc.vector.tensor_scalar(x1s[h][:, j, :], u[h][:, j, :], mv[h][:, 0, j, 0:1],
                                                       rstd[h][:, 0, j:j + 1], ALU.subtract, ALU.mult)
                    last.then_inc(x1_ready[h], 1)
                    dve.wait_ge(x1_ready[h], i + 1)
                    nc.vector.tensor_tensor(u[h][:, :, :], x1s[h][:, :, :], m.bo[:, :, :], ALU.add
                                            ).then_inc(v_ready[h], 1)
                    moments(i, h, 1, u, v_ready)
                for h in range(2):
                    dve.wait_ge(rstd_ready[1][h], i + 1)
                    reuse(dve, fin_stored[h], 16 * i)
                    for j in range(NR):
                        last = nc.vector.tensor_scalar(fins[h][:, j, :], u[h][:, j, :], mv[h][:, 1, j, 0:1],
                                                       rstd[h][:, 1, j:j + 1], ALU.subtract, ALU.mult)
                    last.then_inc(fin_ready[h], 1)

            step(0)
            with dve.Fori(1, STEPS) as i:
                step(i)

        @block.gpsimd
        def _(pool):
            def gather(i):
                for h in range(2):
                    reuse(pool, te_done[h], i)
                nc.gpsimd.tensor_copy(stage[:, 0:CHUNK], m.src_idx[:, bass.DynSlice(i * CHUNK, CHUNK)]
                                      ).then_inc(staged, 1)
                nc.gpsimd.tensor_copy(stage[:, CHUNK:2 * CHUNK], m.dst_idx[:, bass.DynSlice(i * CHUNK, CHUNK)]
                                      ).then_inc(staged, 1)
                pool.wait_ge(staged, 2 * (i + 1))
                settle(pool, passed_pool)
                for h in range(2):
                    for j in range(ER):
                        for c, g in ((0, gs), (CHUNK, gd)):
                            col = c + h * ER + j
                            nc.gpsimd.indirect_dma_start(
                                out=g[h][:, j, :], out_offset=None, in_=a["x"],
                                in_offset=bass.IndirectOffsetOnAxis(ap=stage[:, col:col + 1], axis=0),
                            ).then_inc(gathered[h], 16)

            def put_slots(n):
                reuse(pool, slots_put, 16 * CHUNK * n)
                nc.gpsimd.tensor_copy(slot_stage[:, 0, :], m.slot_to[:, bass.DynSlice(n * CHUNK, CHUNK)]
                                      ).then_inc(slots_staged, 1)
                nc.gpsimd.tensor_copy(slot_stage[:, 1, :], m.slot_row[:, bass.DynSlice(n * CHUNK, CHUNK)]
                                      ).then_inc(slots_staged, 1)
                pool.wait_ge(slots_staged, 2 * (n + 1))
                settle(pool, passed_pool)
                for j in range(CHUNK):
                    nc.gpsimd.indirect_dma_start(
                        out=m.row_of_node, in_=slot_stage[:, 1, j:j + 1], in_offset=None,
                        out_offset=bass.IndirectOffsetOnAxis(ap=slot_stage[:, 0, j:j + 1], axis=0),
                        bounds_check=N - 1, oob_is_err=False,
                    ).then_inc(slots_put, 16)

            def find_rows(n):
                reuse(pool, found_kept, n)
                nc.gpsimd.tensor_copy(slot_stage[:, 2, :], m.src_idx[:, bass.DynSlice(n * CHUNK, CHUNK)]
                                      ).then_inc(slots_staged, 1)
                pool.wait_ge(slots_staged, 2 * STEPS + n + 1)
                settle(pool, passed_pool)
                for j in range(CHUNK):
                    nc.gpsimd.indirect_dma_start(
                        out=found[:, j:j + 1], out_offset=None, in_=m.row_of_node,
                        in_offset=bass.IndirectOffsetOnAxis(ap=slot_stage[:, 2, j:j + 1], axis=0),
                    ).then_inc(rows_found, 16)
                pool.wait_ge(rows_found, 16 * CHUNK * (n + 1))
                nc.gpsimd.tensor_copy(m.src_row[:, bass.DynSlice(n * CHUNK, CHUNK)], found[:, 0:CHUNK]
                                      ).then_inc(found_kept, 1)

            def roots(i):
                for n in range(2):
                    for h in range(2):
                        pool.wait_ge(var_ready[n][h], i + 1)
                        nc.gpsimd.tensor_tensor(rstd[h][:, n, :], vare[h][:, n, :], m.minus_half[:, :], ALU.pow
                                                ).then_inc(rstd_ready[n][h], 1)

            half = STEPS // 2
            def putting_step(i):
                gather(i + 1)
                put_slots(2 * i)
                put_slots(2 * i + 1)
                roots(i)

            def finding_step(i, n):
                gather(i + 1)
                find_rows(n)
                find_rows(n + 1)
                roots(i)

            gather(0)
            putting_step(0)
            with pool.Fori(1, half) as i:
                putting_step(i)
            put_slots(2 * half)
            pool.wait_ge(slots_put, 16 * TILES)
            finding_step(half, 0)
            with pool.Fori(half + 1, STEPS - 1) as i:
                finding_step(i, 2 * i - 2 * half)
            find_rows(2 * half)
            roots(STEPS - 1)



def edge_layer(nc, m, l):
    final = l == 2
    src_table = m.y2_table if final else m.y1_table
    with ExitStack() as ctx:
        sem, pair = sem_maker(nc, ctx, f"layer{l}")

        def sb2(name, shape, dt=F32):
            return [ctx.enter_context(nc.sbuf_tensor(f"{name}_l{l}{h}", shape, dt)) for h in range(2)]

        def ps2(name, shape):
            return [ctx.enter_context(nc.psum_tensor(f"{name}_l{l}{h}", shape, F32)) for h in range(2)]

        stage = ctx.enter_context(nc.sbuf_tensor(f"stage_l{l}", [P, CHUNK], I32))
        gs = sb2("gs", [P, ER, P])
        agg = sb2("agg", [P, ET])
        pre = sb2("pre", [P, ET])
        re = sb2("re", [P, ET])
        skip_in = sb2("skip_in", [P, ER, P])
        y_out = sb2("y_out", [P, ER, P])
        s_out = sb2("s_out", [P, ER, P])
        stats = sb2("stats", [P, ER, 6])
        mv = sb2("mv", [P, ER, 2])
        vare = sb2("vare", [P, ER])
        rstd = sb2("rstd", [P, ER])
        pt = ps2("pt", [P, ET])
        pm = ps2("pm", [P, 512])
        pr = ps2("pr", [P, ER, 2 * P])

        staged = sem("staged")
        gathered = pair("gathered")
        skip_loaded = pair("skip_loaded")
        t_done = pair("t_done")
        agg_ready = pair("agg_ready")
        pre_ready = pair("pre_ready")
        re_ready = pair("re_ready")
        m_done = pair("m_done")
        slot_ready = pair("slot_ready")
        rows_done = pair("rows_done")
        y_ready = pair("y_ready")
        sum_ready = pair("sum_ready")
        sum2_ready = pair("sum2_ready")
        stored = pair("stored")
        stats_ready = pair("stats_ready")
        mv_ready = pair("mv_ready")
        var_ready = pair("var_ready")
        rstd_ready = pair("rstd_ready")
        x1_ready = pair("x1_ready")
        x1_turned = pair("x1_turned")
        carry_ready = sem("carry_ready")
        passed_pool = sem("passed_pool")
        passed_dve = sem("passed_dve")
        block = ctx.enter_context(nc.Block())

        def skewed(eng, front, back):
            front(0, 0)
            front(0, 1)
            back(0, 0)
            with eng.Fori(1, STEPS) as i:
                front(i, 0)
                back(i - 1, 1)
                front(i, 1)
                back(i, 0)
            back(STEPS - 1, 1)

        @block.sync
        def _(sp):
            def front(i, h):
                reuse(sp, sum_ready[h], i)
                sp.dma_start(skip_in[h][:, :, :], edge_rows(m.skip_rows, (2 * i + h) * ET)
                             ).then_inc(skip_loaded[h], 16)

            def back(i, h):
                edge = (2 * i + h) * ET
                if final:
                    sp.wait_ge(x1_ready[h], i + 1)
                    sp.dma_start(edge_rows(m.x1_table, edge + N), s_out[h][:, :, :]).then_inc(stored[h], 16)
                else:
                    sp.wait_ge(y_ready[h], i + 1)
                    sp.dma_start(edge_rows(m.y2_table, edge + N), y_out[h][:, :, :]).then_inc(stored[h], 16)
                    sp.wait_ge(sum_ready[h], i + 1)
                    sp.dma_start(edge_rows(m.skip_rows, edge), s_out[h][:, :, :]).then_inc(stored[h], 16)

            skewed(sp, front, back)
            for h in range(2):
                sp.wait_ge(stored[h], (16 if final else 32) * STEPS)

        @block.gpsimd
        def _(pool):
            def gather(i):
                for h in range(2):
                    reuse(pool, t_done[h], i)
                nc.gpsimd.tensor_copy(stage[:, :], m.src_row[:, bass.DynSlice(i * CHUNK, CHUNK)]
                                      ).then_inc(staged, 1)
                pool.wait_ge(staged, i + 1)
                settle(pool, passed_pool)
                for h in range(2):
                    for j in range(ER):
                        col = h * ER + j
                        nc.gpsimd.indirect_dma_start(
                            out=gs[h][:, j, :], out_offset=None, in_=src_table,
                            in_offset=bass.IndirectOffsetOnAxis(ap=stage[:, col:col + 1], axis=0),
                        ).then_inc(gathered[h], 16)

            def root(i, h):
                pool.wait_ge(var_ready[h], i + 1)
                nc.gpsimd.tensor_tensor(rstd[h][:, :], vare[h][:, :], m.minus_half[:, 0:ER], ALU.pow
                                        ).then_inc(rstd_ready[h], 1)

            if final:
                gather(0)
                with pool.Fori(0, STEPS - 1) as i:
                    gather(i + 1)
                    root(i, 0)
                    root(i, 1)
                root(STEPS - 1, 0)
                root(STEPS - 1, 1)
            else:
                gather(0)
                with pool.Fori(1, STEPS) as i:
                    gather(i)

        @block.tensor
        def _(pe):
            def front(i, h):
                pe.wait_ge(gathered[h], 32 * (i + 1))
                reuse(pe, agg_ready[h], i)
                for j in range(ER):
                    cut = slice(j * P, (j + 1) * P)
                    nc.tensor.matmul(pt[h][:, cut], m.c_row[0:1, l - 1, :], m.ones_row[0:1, :],
                                     start=True, stop=False)
                    last = nc.tensor.matmul(pt[h][:, cut], gs[h][:, j, :], m.ident[:, :],
                                            start=False, stop=True)
                last.then_inc(t_done[h], 1)

            def back(i, h):
                pe.wait_ge(re_ready[h], i + 1)
                if not final:
                    reuse(pe, slot_ready[h], i)
                    nc.tensor.matmul(pm[h][:, 0:ET], m.MG2[:, 0:P], re[h][:, :], start=True, stop=True
                                     ).then_inc(m_done[h], 1)
                    reuse(pe, y_ready[h], i)
                reuse(pe, sum_ready[h], i)
                for j in range(ER):
                    w = m.G3[:, :] if final else m.MG2[:, :]
                    last = nc.tensor.matmul(pr[h][:, j, 0:P] if final else pr[h][:, j, :],
                                            re[h][:, j * P:(j + 1) * P], w, start=True, stop=True)
                last.then_inc(rows_done[h], 1)
                if final:
                    reuse(pe, slot_ready[h], i)
                    pe.wait_ge(x1_ready[h], i + 1)
                    for j in range(ER):
                        last = nc.tensor.transpose(pm[h][:, j * P:(j + 1) * P], s_out[h][:, j, :], m.ident[:, :])
                    last.then_inc(x1_turned[h], 1)

            skewed(pe, front, back)

        @block.scalar
        def _(act):
            def front(i, h):
                act.wait_ge(pre_ready[h], i + 1)
                reuse(act, rows_done[h], i)
                nc.scalar.activation(re[h][:, :], pre[h][:, :], ACT.Relu, bias=m.b1[:, l:l + 1]
                                     ).then_inc(re_ready[h], 1)

            def back(i, h):
                if not final:
                    act.wait_ge(m_done[h], i + 1)
                    nc.scalar.activation(m.slots[:, bass.DynSlice((2 * i + h) * ET, ET)], pm[h][:, 0:ET],
                                         ACT.Identity, bias=m.c[:, 1:2]).then_inc(slot_ready[h], 1)
                    act.wait_ge(rows_done[h], i + 1)
                    reuse(act, stored[h], 32 * i)
                    nc.scalar.activation(y_out[h][:, :, :], pr[h][:, :, 0:P], ACT.Copy).then_inc(y_ready[h], 1)

            skewed(act, front, back)

        @block.vector
        def _(dve):
            nc.vector.memset(agg[1][:, :], 0.0).then_inc(carry_ready, 1)
            dve.wait_ge(carry_ready, 1)

            def front(i, h):
                dve.wait_ge(t_done[h], i + 1)
                reuse(dve, agg_ready[1 - h], i + h)
                nc.vector.tensor_tensor_scan(agg[h][:, :], m.same[:, bass.DynSlice((2 * i + h) * ET, ET)],
                                             pt[h][:, :], agg[1 - h][:, ET - 1:ET], ALU.mult, ALU.add
                                             ).then_inc(agg_ready[h], 1)
                dve.wait_ge(agg_ready[h], i + 1)
                reuse(dve, re_ready[h], i)
                nc.vector.scalar_tensor_tensor(out=pre[h][:, :], in0=m.slots[:, bass.DynSlice((2 * i + h) * ET, ET)],
                                               scalar=m.scale[:, l:l + 1], in1=agg[h][:, :],
                                               op0=ALU.mult, op1=ALU.add).then_inc(pre_ready[h], 1)

            def back(i, h):
                dve.wait_ge(rows_done[h], i + 1)
                dve.wait_ge(skip_loaded[h], 16 * (i + 1))
                if not final:
                    dve.wait_ge(y_ready[h], i + 1)
                    reuse(dve, stored[h], 32 * i)
                    nc.vector.tensor_tensor(s_out[h][:, :, :], pr[h][:, :, P:2 * P], skip_in[h][:, :, :], ALU.add
                                            ).then_inc(sum_ready[h], 1)
                    return
                nc.vector.tensor_tensor(y_out[h][:, :, :], pr[h][:, :, 0:P], skip_in[h][:, :, :], ALU.add
                                        ).then_inc(sum_ready[h], 1)
                dve.wait_ge(sum_ready[h], i + 1)
                nc.vector.tensor_tensor(y_out[h][:, :, :], y_out[h][:, :, :], m.cf[:, 0:ER, :], ALU.add
                                        ).then_inc(sum2_ready[h], 1)
                dve.wait_ge(sum2_ready[h], i + 1)
                for j in range(ER):
                    nc.vector.bn_stats(stats[h][:, j, :], y_out[h][:, j, :]).then_inc(stats_ready[h], 1)
                dve.wait_ge(stats_ready[h], ER * (i + 1))
                settle(dve, passed_dve)
                for j in range(ER):
                    nc.vector.bn_aggr(mv[h][:, j, :], stats[h][:, j, :]).then_inc(mv_ready[h], 1)
                dve.wait_ge(mv_ready[h], ER * (i + 1))
                nc.vector.tensor_scalar(vare[h][:, :], mv[h][:, :, 1], LN_EPS, None, ALU.add
                                        ).then_inc(var_ready[h], 1)
                dve.wait_ge(rstd_ready[h], i + 1)
                reuse(dve, stored[h], 16 * i)
                for j in range(ER):
                    last = nc.vector.tensor_scalar(s_out[h][:, j, :], y_out[h][:, j, :], mv[h][:, j, 0:1],
                                                   rstd[h][:, j:j + 1], ALU.subtract, ALU.mult)
                last.then_inc(x1_ready[h], 1)
                dve.wait_ge(x1_turned[h], i + 1)
                nc.vector.scalar_tensor_tensor(out=m.slots[:, bass.DynSlice((2 * i + h) * ET, ET)],
                                               in0=m.same[:, bass.DynSlice((2 * i + h) * ET + 1, ET)], scalar=0.0,
                                               in1=pm[h][:, 0:ET], op0=ALU.is_equal, op1=ALU.mult
                                               ).then_inc(slot_ready[h], 1)

            skewed(dve, front, back)



def attention(nc, m, a, out):
    with ExitStack() as ctx:
        sem, pair = sem_maker(nc, ctx, "attn")

        def sb2(name, shape, dt=F32):
            return [ctx.enter_context(nc.sbuf_tensor(f"{name}_at{h}", shape, dt)) for h in range(2)]

        def ps2(name, shape):
            return [ctx.enter_context(nc.psum_tensor(f"{name}_at{h}", shape, F32)) for h in range(2)]

        def ps(name, shape):
            return ctx.enter_context(nc.psum_tensor(f"{name}_at", shape, F32))

        stage = ctx.enter_context(nc.sbuf_tensor("stage_at", [P, CHUNK], I32))
        to_stage = sb2("to_stage", [P, ER], I32)
        gs = sb2("gs", [P, ER, P])
        ein = sb2("ein", [P, ER, ED])
        ends = sb2("ends", [P, ET])
        goes_on = sb2("goes_on", [P, ET], U8)
        xs = sb2("xs", [P, ET])
        eT = sb2("eT", [ED, ET])
        xd = sb2("xd", [P, ET])
        q = sb2("q", [P, ET])
        v = sb2("v", [P, ET])
        prod = sb2("prod", [P, ET])
        sc = sb2("sc", [H, ET])
        pen = sb2("pen", [H, ET])
        mx = sb2("mx", [H, ET + 1])
        arg = sb2("arg", [H, 2, ET])
        tmp = sb2("tmp", [H, ET])
        ex = sb2("ex", [H, 2, ET])
        den = sb2("den", [H, ET])
        rden = sb2("rden", [H, ET])
        al = sb2("al", [H, ET])
        va = sb2("va", [P, ET])
        u = sb2("u", [P, ER, P])
        fin = sb2("fin", [P, ER, P])
        stats = sb2("stats", [P, ER, 6])
        mv = sb2("mv", [P, ER, 2])
        vare = sb2("vare", [P, ER])
        rstd = sb2("rstd", [P, ER])
        a0 = ps2("a0", [P, 512])
        a1 = ps2("a1", [P, 512])
        a2 = ps("a2", [P, ET])
        a3 = ps("a3", [P, 512])
        a4 = ps2("a4", [P, ER, P])

        staged = sem("staged")
        gathered = pair("gathered")
        e_loaded = pair("e_loaded")
        e_clear = sem("e_clear")
        slots_in = pair("slots_in")
        init = sem("init")
        t_done = pair("t_done")
        xs_ready = pair("xs_ready")
        eT_ready = pair("eT_ready")
        xd_ready = pair("xd_ready")
        qk_done = pair("qk_done")
        v_done = pair("v_done")
        q_ready = pair("q_ready")
        v_ready = pair("v_ready")
        prod_ready = pair("prod_ready")
        sc_done = pair("sc_done")
        sc_ready = pair("sc_ready")
        pen_ready = pair("pen_ready")
        tail_ready = pair("tail_ready")
        mx_ready = pair("mx_ready")
        tmp_ready = pair("tmp_ready")
        arg_ready = pair("arg_ready")
        ex_ready = pair("ex_ready")
        den_ready = pair("den_ready")
        rden_ready = pair("rden_ready")
        al_ready = pair("al_ready")
        spread_done = pair("spread_done")
        va_ready = pair("va_ready")
        o_done = pair("o_done")
        u_ready = pair("u_ready")
        stats_ready = pair("stats_ready")
        mv_ready = pair("mv_ready")
        var_ready = pair("var_ready")
        rstd_ready = pair("rstd_ready")
        fin_ready = pair("fin_ready")
        to_staged = pair("to_staged")
        scattered = pair("scattered")
        passed_pool = sem("passed_pool")
        passed_dve = sem("passed_dve")
        block = ctx.enter_context(nc.Block())

        def first_edge(i, h):
            return (2 * STEPS - 1 - h) * ET - 2 * ET * i

        def skewed(eng, front, back):
            front(0, 0)
            front(0, 1)
            back(0, 0)
            with eng.Fori(1, STEPS) as i:
                front(i, 0)
                back(i - 1, 1)
                front(i, 1)
                back(i, 0)
            back(STEPS - 1, 1)

        @block.sync
        def _(sp):
            whole = (E - (EP - ET)) // P
            rest = E - (EP - ET) - whole * P
            assert whole == 1 and rest > 0
            def slots(i, h):
                first = first_edge(i, h)
                sp.wait_ge(init, 3)
                reuse(sp, xd_ready[h], i)
                reuse(sp, pen_ready[h], i)
                sp.dma_start(ends[h][:, :], m.slots[:, bass.DynSlice(first, ET)]).then_inc(slots_in[h], 16)
                sp.dma_start(goes_on[h][:, :], m.same[:, bass.DynSlice(first + 1, ET)]).then_inc(slots_in[h], 16)

            slots(0, 0)
            slots(0, 1)
            sp.wait_ge(e_clear, 1)
            sp.dma_start(ein[0][:, 0, :], a["edge"][EP - ET:EP - ET + P, :]).then_inc(e_loaded[0], 16)
            sp.dma_start(ein[0][0:rest, 1, :], a["edge"][EP - P:E, :]).then_inc(e_loaded[0], 16)
            sp.dma_start(ein[1][:, :, :], edge_rows(a["edge"], first_edge(0, 1))).then_inc(e_loaded[1], 16)
            with sp.Fori(1, STEPS) as i:
                for h in range(2):
                    slots(i, h)
                    reuse(sp, t_done[h], i)
                    sp.dma_start(ein[h][:, :, :], edge_rows(a["edge"], first_edge(i, h))
                                 ).then_inc(e_loaded[h], 16)

        @block.gpsimd
        def _(pool):
            def gather(i):
                for h in range(2):
                    reuse(pool, t_done[h], i)
                nc.gpsimd.tensor_copy(stage[:, :], m.src_row[:, bass.DynSlice((STEPS - 1) * CHUNK - i * CHUNK, CHUNK)]
                                      ).then_inc(staged, 1)
                pool.wait_ge(staged, i + 1)
                settle(pool, passed_pool)
                for h in range(2):
                    for j in range(ER):
                        col = (1 - h) * ER + j
                        nc.gpsimd.indirect_dma_start(
                            out=gs[h][:, j, :], out_offset=None, in_=m.x1_table,
                            in_offset=bass.IndirectOffsetOnAxis(ap=stage[:, col:col + 1], axis=0),
                        ).then_inc(gathered[h], 16)

            def root(i, h):
                pool.wait_ge(var_ready[h], i + 1)
                nc.gpsimd.tensor_tensor(rstd[h][:, :], vare[h][:, :], m.minus_half[:, 0:ER], ALU.pow
                                        ).then_inc(rstd_ready[h], 1)

            def scatter(i, h):
                reuse(pool, scattered[h], 32 * i)
                settle(pool, passed_pool)
                nc.gpsimd.tensor_copy(to_stage[h][:, :],
                                      m.final_to[:, bass.DynSlice((2 * STEPS - 1 - h) * ER - 2 * ER * i, ER)]
                                      ).then_inc(to_staged[h], 1)
                pool.wait_ge(to_staged[h], i + 1)
                pool.wait_ge(fin_ready[h], i + 1)
                settle(pool, passed_pool)
                for j in range(ER):
                    nc.gpsimd.indirect_dma_start(
                        out=out, in_=fin[h][:, j, :], in_offset=None,
                        out_offset=bass.IndirectOffsetOnAxis(ap=to_stage[h][:, j:j + 1], axis=0),
                        bounds_check=N - 1, oob_is_err=False,
                    ).then_inc(scattered[h], 16)

            def step(i):
                gather(i + 1)
                for h in range(2):
                    root(i, h)
                    scatter(i, h)

            gather(0)
            step(0)
            with pool.Fori(1, STEPS - 1) as i:
                step(i)
            for h in range(2):
                root(STEPS - 1, h)
                scatter(STEPS - 1, h)
            for h in range(2):
                pool.wait_ge(scattered[h], 32 * STEPS)

        @block.tensor
        def _(pe):
            def front(i, h):
                pe.wait_ge(gathered[h], 32 * (i + 1))
                pe.wait_ge(e_loaded[h], 16 * (i + 1) + (16 if h == 0 else 0))
                reuse(pe, xs_ready[h], i)
                reuse(pe, eT_ready[h], i)
                for j in range(ER):
                    nc.tensor.transpose(a0[h][:, j * P:(j + 1) * P], gs[h][:, j, :], m.ident[:, :])
                for j in range(ER):
                    last = nc.tensor.transpose(a0[h][0:ED, ET + j * P:ET + (j + 1) * P], ein[h][:, j, :],
                                               m.ident[:, :])
                last.then_inc(t_done[h], 1)
                pe.wait_ge(xd_ready[h], i + 1)
                reuse(pe, prod_ready[h], i)
                nc.tensor.matmul(a1[h][:, ET:2 * ET], m.Wk[:, :], xd[h][:, :], start=True, stop=True)
                pe.wait_ge(xs_ready[h], i + 1)
                nc.tensor.matmul(a1[h][:, 0:ET], m.Wq[:, :], xs[h][:, :], start=True, stop=True
                                 ).then_inc(qk_done[h], 1)
                reuse(pe, sc_ready[1 - h], i + h)
                nc.tensor.matmul(a3[:, 0:ET], m.Wv[:, :], xd[h][:, :], start=True, stop=True
                                 ).then_inc(v_done[h], 1)
                pe.wait_ge(prod_ready[h], i + 1)
                pe.wait_ge(eT_ready[h], i + 1)
                pe.wait_ge(v_ready[h], i + 1)
                nc.tensor.matmul(a3[0:H, ET:2 * ET], m.head_sum[:, :], prod[h][:, :], start=True, stop=False)
                nc.tensor.matmul(a3[0:H, ET:2 * ET], m.Wb8[:, :], eT[h][:, :], start=False, stop=True
                                 ).then_inc(sc_done[h], 1)

            def back(i, h):
                pe.wait_ge(al_ready[h], i + 1)
                reuse(pe, va_ready[1 - h], i + h)
                nc.tensor.matmul(a2[:, :], m.head_spread[:, :], al[h][:, :], start=True, stop=True
                                 ).then_inc(spread_done[h], 1)
                pe.wait_ge(va_ready[h], i + 1)
                reuse(pe, u_ready[h], i)
                for j in range(ER):
                    cut = slice(j * P, (j + 1) * P)
                    nc.tensor.matmul(a4[h][:, j, :], xd[h][:, cut], m.ident[:, :], start=True, stop=False)
                    last = nc.tensor.matmul(a4[h][:, j, :], va[h][:, cut], m.Wo[:, :], start=False, stop=True)
                last.then_inc(o_done[h], 1)

            skewed(pe, front, back)

        @block.scalar
        def _(act):
            def front(i, h):
                act.wait_ge(t_done[h], i + 1)
                reuse(act, qk_done[h], i)
                nc.scalar.activation(xs[h][:, :], a0[h][:, 0:ET], ACT.Copy).then_inc(xs_ready[h], 1)
                act.wait_ge(qk_done[h], i + 1)
                reuse(act, prod_ready[h], i)
                nc.scalar.activation(q[h][:, :], a1[h][:, 0:ET], ACT.Identity, bias=m.bqkv[:, 0:1]
                                     ).then_inc(q_ready[h], 1)
                act.wait_ge(v_done[h], i + 1)
                reuse(act, va_ready[h], i)
                nc.scalar.activation(v[h][:, :], a3[:, 0:ET], ACT.Identity, bias=m.bqkv[:, 2:3]
                                     ).then_inc(v_ready[h], 1)
                act.wait_ge(sc_done[h], i + 1)
                reuse(act, arg_ready[h], i)
                nc.scalar.activation(sc[h][:, :], a3[0:H, ET:2 * ET], ACT.Identity, bias=m.bb8[:, 0:1]
                                     ).then_inc(sc_ready[h], 1)

            def back(i, h):
                act.wait_ge(arg_ready[h], i + 1)
                reuse(act, den_ready[h], i)
                nc.scalar.activation(ex[h][:, :, :], arg[h][:, :, :], ACT.Exp).then_inc(ex_ready[h], 1)

            skewed(act, front, back)

        @block.vector
        def _(dve):
            nc.vector.memset(ein[0][:, :, :], 0.0).then_inc(e_clear, 1)
            nc.vector.memset(xd[1][:, :], 0.0).then_inc(init, 1)
            nc.vector.memset(mx[1][:, :], 0.0).then_inc(init, 1)
            nc.vector.memset(den[1][:, :], 1.0).then_inc(init, 1)
            dve.wait_ge(init, 3)

            def front(i, h):
                reuse(dve, xd_ready[1 - h], i + h)
                reuse(dve, o_done[h], i)
                dve.wait_ge(slots_in[h], 32 * (i + 1))
                nc.vector.tensor_tensor_scan(xd[h][:, ::-1], goes_on[h][:, ::-1], ends[h][:, ::-1],
                                             xd[1 - h][:, 0:1], ALU.mult, ALU.add).then_inc(xd_ready[h], 1)
                reuse(dve, tmp_ready[h], i)
                nc.vector.tensor_scalar(pen[h][:, :], goes_on[h][0:H, :], -1.0, FAR,
                                        ALU.add, ALU.mult).then_inc(pen_ready[h], 1)
                dve.wait_ge(xs_ready[h], i + 1)
                reuse(dve, sc_done[h], i)
                nc.vector.tensor_copy(eT[h][:, :], a0[h][0:ED, ET:2 * ET]).then_inc(eT_ready[h], 1)
                dve.wait_ge(q_ready[h], i + 1)
                nc.vector.scalar_tensor_tensor(out=prod[h][:, :], in0=a1[h][:, ET:2 * ET],
                                               scalar=m.bqkv[:, 1:2], in1=q[h][:, :],
                                               op0=ALU.add, op1=ALU.mult).then_inc(prod_ready[h], 1)

            def back(i, h):
                reuse(dve, mx_ready[1 - h], i + h)
                nc.vector.tensor_copy(mx[h][:, ET:ET + 1], mx[1 - h][:, 0:1]).then_inc(tail_ready[h], 1)
                dve.wait_ge(tail_ready[h], i + 1)
                dve.wait_ge(pen_ready[h], i + 1)
                dve.wait_ge(sc_ready[h], i + 1)
                nc.vector.tensor_tensor_scan(mx[h][:, 0:ET][:, ::-1], pen[h][:, ::-1], sc[h][:, ::-1],
                                             mx[h][:, ET:ET + 1], ALU.add, ALU.max).then_inc(mx_ready[h], 1)
                dve.wait_ge(mx_ready[h], i + 1)
                nc.vector.tensor_tensor(tmp[h][:, :], mx[h][:, 1:ET + 1], pen[h][:, :], ALU.add
                                        ).then_inc(tmp_ready[h], 1)
                dve.wait_ge(tmp_ready[h], i + 1)
                reuse(dve, ex_ready[h], i)
                nc.vector.tensor_tensor(arg[h][:, 0, :], tmp[h][:, :], mx[h][:, 0:ET], ALU.subtract)
                nc.vector.tensor_tensor(arg[h][:, 1, :], sc[h][:, :], mx[h][:, 0:ET], ALU.subtract
                                        ).then_inc(arg_ready[h], 1)
                dve.wait_ge(ex_ready[h], i + 1)
                reuse(dve, den_ready[1 - h], i + h)
                nc.vector.tensor_tensor_scan(den[h][:, ::-1], ex[h][:, 0, ::-1], ex[h][:, 1, ::-1],
                                             den[1 - h][:, 0:1], ALU.mult, ALU.add).then_inc(den_ready[h], 1)
                dve.wait_ge(den_ready[h], i + 1)
                nc.vector.reciprocal(rden[h][:, :], den[h][:, :]).then_inc(rden_ready[h], 1)
                dve.wait_ge(rden_ready[h], i + 1)
                reuse(dve, spread_done[h], i)
                nc.vector.tensor_tensor(al[h][:, :], den[h][:, :], rden[h][:, :], ALU.mult
                                        ).then_inc(al_ready[h], 1)
                dve.wait_ge(spread_done[h], i + 1)
                dve.wait_ge(v_ready[h], i + 1)
                reuse(dve, o_done[h], i)
                nc.vector.tensor_tensor(va[h][:, :], a2[:, :], v[h][:, :], ALU.mult
                                        ).then_inc(va_ready[h], 1)
                dve.wait_ge(o_done[h], i + 1)
                nc.vector.tensor_tensor(u[h][:, :, :], a4[h][:, :, :], m.bo[:, 0:ER, :], ALU.add
                                        ).then_inc(u_ready[h], 1)
                dve.wait_ge(u_ready[h], i + 1)
                for j in range(ER):
                    nc.vector.bn_stats(stats[h][:, j, :], u[h][:, j, :]).then_inc(stats_ready[h], 1)
                dve.wait_ge(stats_ready[h], ER * (i + 1))
                settle(dve, passed_dve)
                for j in range(ER):
                    nc.vector.bn_aggr(mv[h][:, j, :], stats[h][:, j, :]).then_inc(mv_ready[h], 1)
                dve.wait_ge(mv_ready[h], ER * (i + 1))
                nc.vector.tensor_scalar(vare[h][:, :], mv[h][:, :, 1], LN_EPS, None, ALU.add
                                        ).then_inc(var_ready[h], 1)
                dve.wait_ge(rstd_ready[h], i + 1)
                reuse(dve, scattered[h], 32 * i)
                for j in range(ER):
                    last = nc.vector.tensor_scalar(fin[h][:, j, :], u[h][:, j, :], mv[h][:, j, 0:1],
                                                   rstd[h][:, j:j + 1], ALU.subtract, ALU.mult)
                last.then_inc(fin_ready[h], 1)

            skewed(dve, front, back)


def program(nc, a, out):
    with ExitStack() as ctx:
        m = lay_out(nc, ctx)
        prepare(nc, m, a)
        nodes_and_first_layer(nc, m, a, out)
        edge_layer(nc, m, 1)
        edge_layer(nc, m, 2)
        attention(nc, m, a, out)


_INS = {"x": "x", "src": "src", "dst": "dst", "edge_attr_64": "edge",
        "L0_gnn_eps": "eps", "L0_gnn_W1": "W1", "L0_gnn_b1": "b1", "L0_gnn_W2": "W2", "L0_gnn_b2": "b2",
        "L0_gnn_Wf": "Wf", "L0_gnn_bf": "bf",
        "L1_gnn_Wq": "Wq", "L1_gnn_bq": "bq", "L1_gnn_Wk": "Wk", "L1_gnn_bk": "bk", "L1_gnn_Wv": "Wv",
        "L1_gnn_bv": "bv", "L1_gnn_Wb": "Wb", "L1_gnn_bb": "bb", "L1_gnn_Wo": "Wo", "L1_gnn_bo": "bo"}


def kernel(**inputs):
    import numpy as _np
    import concourse.bacc as _bacc
    from concourse import mybir as _mybir
    from concourse.bass_utils import run_bass_kernel_spmd as _run

    nc = _bacc.Bacc("TRN2", target_bir_lowering=False, num_devices=1)
    arrays, args = {}, {}
    for name, short in _INS.items():
        v = _np.ascontiguousarray(inputs[name])
        arrays[f"in_{name}_dram"] = v
        args[short] = nc.dram_tensor(f"in_{name}_dram", v.shape, _mybir.dt.from_np(v.dtype),
                                     kind="ExternalInput").ap()
    out = nc.dram_tensor("out_0_dram", (N, D), _mybir.dt.float32, kind="ExternalOutput").ap()
    program(nc, args, out)
    r = _run(nc, [arrays], core_ids=[0])
    return r.results[0]["out_0_dram"]
```

```python
from contextlib import ExitStack

import concourse.bass as bass
from concourse import mybir

F32 = mybir.dt.float32
I32 = mybir.dt.int32
U8 = mybir.dt.uint8
ALU = mybir.AluOpType
ACT = mybir.ActivationFunctionType

P = 128
N = 50000
E = 25000
D = 128
ED = 64
H = 8
HD = D // H
LAYERS = 3
NR = 4
NT = NR * P
ER = 2
ET = ER * P
STEPS = -(-E // (2 * ET))
EP = STEPS * 2 * ET
TILES = EP // P
CHUNK = 2 * ER
UNITS = 2 * STEPS
RING = 4
LAST_NODE = N - NT
ROWS = N + EP
PAD_DST = 1 << 20
EDGE_OF_LIST = PAD_DST + 1
SKIP = 1 << 21
LN_EPS = 1e-5
FAR = 1e30

assert (2 * STEPS - 1) * NT < N <= 2 * STEPS * NT and E > EP - P




def use(n, q):
    return (n - q) // RING + 1


def uses(q):
    return len(range(q, UNITS, RING))


def settle(eng, passed):
    eng.sem_inc(passed, 1)


def reuse(eng, sem, count):
    if not isinstance(count, int) or count > 0:
        eng.wait_ge(sem, count)


class Memory:
    pass


def lay_out(nc, ctx):
    m = Memory()

    def sb(name, shape, dt=F32):
        return ctx.enter_context(nc.sbuf_tensor(name, shape, dt))

    m.y1_table = nc.dram_tensor("y1_table", (ROWS, D), F32).ap()
    m.y2_table = nc.dram_tensor("y2_table", (ROWS, D), F32).ap()
    m.x1_table = nc.dram_tensor("x1_table", (ROWS, D), F32).ap()
    m.skip_rows = nc.dram_tensor("skip_rows", (EP, D), F32).ap()
    m.row_of_node = nc.dram_tensor("row_of_node", (N, 1), I32).ap()
    m.dst_list = nc.dram_tensor("dst_list", (EP + 2, 1), I32).ap()
    m.src_list = nc.dram_tensor("src_list", (EP, 1), I32).ap()

    m.W1_0 = sb("W1_0", [P, P])
    m.W0f = sb("W0f", [P, P])
    m.G3 = sb("G3", [P, P])
    m.Wq = sb("Wq", [P, P])
    m.Wk = sb("Wk", [P, P])
    m.Wv = sb("Wv", [P, P])
    m.Wo = sb("Wo", [P, P])
    m.ident = sb("ident", [P, P])
    m.MG1 = sb("MG1", [P, 2 * P])
    m.MG2 = sb("MG2", [P, 2 * P])
    m.b1 = sb("b1", [P, LAYERS])
    m.scale = sb("scale", [P, LAYERS])
    m.c = sb("c", [P, 2])
    m.c_row = sb("c_row", [1, 2, P])
    m.beta = sb("beta", [P, 2])
    m.ones_row = sb("ones_row", [1, P])
    m.eps = sb("eps", [P, 1])
    m.cf = sb("cf", [P, NR, P])
    m.bo = sb("bo", [P, NR, P])
    m.bqkv = sb("bqkv", [P, 3])
    m.Wb8 = sb("Wb8", [ED, H])
    m.bb8 = sb("bb8", [H, 1])
    m.head_sum = sb("head_sum", [P, H])
    m.head_spread = sb("head_spread", [H, P])
    m.minus_half = sb("minus_half", [P, NR])

    m.src_idx = sb("src_idx", [P, TILES], I32)
    m.dst_idx = sb("dst_idx", [P, TILES], I32)
    m.slot_to = sb("slot_to", [P, TILES], I32)
    m.final_to = sb("final_to", [P, TILES], I32)
    m.slot_row = sb("slot_row", [P, TILES], I32)
    m.src_row = sb("src_row", [P, TILES], I32)

    m.same = sb("same", [P, EP + 1], U8)
    m.slots = sb("slots", [P, EP])
    return m


def sem_maker(nc, ctx, phase, count=RING):
    made = []

    def give_back():
        nc.clear_and_free_semaphores(made)
        nc.all_engine_barrier()

    ctx.callback(give_back)

    def sem(name):
        made.append(nc.alloc_semaphore(f"{phase}_{name}"))
        return made[-1]

    def several(name):
        return [sem(f"{name}{q}") for q in range(count)]

    return sem, several



def prepare(nc, m, a):
    with ExitStack() as ctx:
        sem, pair = sem_maker(nc, ctx, "prep", 2)

        def sb(name, shape, dt=F32):
            return ctx.enter_context(nc.sbuf_tensor(name, shape, dt))

        def ps(name, shape):
            return ctx.enter_context(nc.psum_tensor(name, shape, F32))

        HI = P
        LO = TILES - P
        pads = EP - E
        fill = sb("fill", [1, 3 * P], I32)
        own = sb("own", [125, N // 125], I32)
        rows_i = sb("rows_i", [P, 4, 2, P], I32)
        rows_f = sb("rows_f", [P, 4, 2, P])
        cols = sb("cols", [P, 4, TILES])
        eq = sb("eq", [P, 2, TILES])
        W1 = sb("W1", [P, 2, P])
        W2 = sb("W2", [P, LAYERS, P])
        W2T = sb("W2T", [P, LAYERS, P])
        Wf = sb("Wf", [P, LAYERS + 1, P])
        WW = sb("WW", [P, 2, 2, P])
        b2 = sb("b2", [P, LAYERS])
        b2_wide = sb("b2_wide", [P, LAYERS, P])
        bf = sb("bf", [P, P])
        bo1 = sb("bo1", [P, P])
        pT = [ps(f"pT{q}", [P, 512]) for q in range(4)]
        pW = ps("pW", [P, LAYERS, P])
        pG = ps("pG", [P, 512])
        pC = ps("pC", [P, 512])

        filled = sem("filled")
        owned = sem("owned")
        lists = sem("lists")
        own_out = sem("own_out")
        index_in = sem("index_in")
        floats = sem("floats")
        turned = sem("turned")
        cols_ready = sem("cols_ready")
        eq_ready = sem("eq_ready")
        idx_done = sem("idx_done")
        w_in = sem("w_in")
        id_made = sem("id_made")
        iota_done = sem("iota_done")
        heads = sem("heads")
        w2_turned = sem("w2_turned")
        w2T_ready = sem("w2T_ready")
        wide_ready = sem("wide_ready")
        products = sem("products")
        prod_out = sem("prod_out")
        small = sem("small")
        consts = sem("consts")
        block = ctx.enter_context(nc.Block())

        @block.sync
        def _(sp):
            sp.wait_ge(filled, 3)
            sp.dma_start(m.dst_list[0:1, :], fill[0:1, 0:1]).then_inc(lists, 16)
            sp.dma_start(m.dst_list[1:1 + E, :].rearrange("(a b) c -> a (b c)", b=E // 40),
                         a["dst"].rearrange("(a b) -> a b", b=E // 40)).then_inc(lists, 16)
            sp.dma_start(m.dst_list[1 + E:1 + EP, :].rearrange("a c -> c a"),
                         fill[0:1, P:P + pads]).then_inc(lists, 16)
            sp.dma_start(m.dst_list[1 + EP:2 + EP, :], fill[0:1, 0:1]).then_inc(lists, 16)
            sp.dma_start(m.src_list[0:E, :].rearrange("(a b) c -> a (b c)", b=E // 40),
                         a["src"].rearrange("(a b) -> a b", b=E // 40)).then_inc(lists, 16)
            sp.dma_start(m.src_list[E:EP, :].rearrange("a c -> c a"),
                         fill[0:1, 2 * P:2 * P + pads]).then_inc(lists, 16)
            sp.wait_ge(owned, 1)
            sp.dma_start(m.row_of_node.rearrange("(p n) c -> p (n c)", p=125), own[:, :]).then_inc(own_out, 16)
            sp.wait_ge(lists, 96)
            for q, (lst, off) in enumerate(((m.dst_list, 1), (m.dst_list, 0), (m.dst_list, 2), (m.src_list, 0))):
                sp.dma_start(rows_i[:, q, 0, :],
                             lst[off:off + HI * P, :].rearrange("(t p) c -> t (p c)", p=P)).then_inc(index_in, 16)
                sp.dma_start(rows_i[0:LO, q, 1, :],
                             lst[off + HI * P:off + EP, :].rearrange("(t p) c -> t (p c)", p=P)
                             ).then_inc(index_in, 16)
            sp.wait_ge(own_out, 16)

        loads = [
            (m.W1_0[:, :], a["W1"][0]), (W1[:, 0, :], a["W1"][1]), (W1[:, 1, :], a["W1"][2]),
            (W2[:, :, :], a["W2"].rearrange("l k n -> k l n")),
            (Wf[:, :, :], a["Wf"].rearrange("(l k) n -> k l n", k=P)),
            (m.Wq[:, :], a["Wq"]), (m.Wk[:, :], a["Wk"]), (m.Wv[:, :], a["Wv"]), (m.Wo[:, :], a["Wo"]),
            (m.b1[:, :], a["b1"].rearrange("l k -> k l")),
            (b2[:, :], a["b2"].rearrange("l k -> k l")),
            (m.scale[:, :], a["eps"].rearrange("(o l) -> o l", o=1).to_broadcast([P, LAYERS])),
            (bf[:, :], a["bf"].rearrange("(o n) -> o n", o=1).to_broadcast([P, P])),
            (bo1[:, :], a["bo"].rearrange("(o n) -> o n", o=1).to_broadcast([P, P])),
            (m.bqkv[:, 0:1], a["bq"].rearrange("(n o) -> n o", o=1)),
            (m.bqkv[:, 1:2], a["bk"].rearrange("(n o) -> n o", o=1)),
            (m.bqkv[:, 2:3], a["bv"].rearrange("(n o) -> n o", o=1)),
            (m.Wb8[:, 0:1], a["Wb"]),
            (m.bb8[:, :], a["bb"].rearrange("(o n) -> o n", o=1).to_broadcast([H, 1])),
        ]
        W_DMAS = len(loads)

        @block.scalar
        def _(act):
            with nc.allow_non_contiguous_dma(reason="a few hundred bias values, once"):
                for dst, src in loads:
                    act.dma_start(dst, src).then_inc(w_in, 16)

        @block.gpsimd
        def _(pool):
            nc.gpsimd.iota(own[:, :], pattern=[[1, N // 125]], base=0, channel_multiplier=N // 125
                           ).then_inc(owned, 1)
            nc.gpsimd.iota(m.slot_row[:, :], pattern=[[P, TILES]], base=N, channel_multiplier=1
                           ).then_inc(iota_done, 1)
            nc.gpsimd.memset(m.ident[:, :], 0.0).then_inc(id_made, 1)
            pool.wait_ge(id_made, 1)
            nc.gpsimd.affine_select(out=m.ident[:, :], in_=m.ident[:, :], compare_op=ALU.not_equal, fill=1.0,
                                    base=0, pattern=[[-1, P]], channel_multiplier=1).then_inc(id_made, 1)
            nc.gpsimd.memset(m.head_sum[:, :], float(HD) ** -0.5).then_inc(heads, 1)
            nc.gpsimd.memset(m.head_spread[:, :], 1.0).then_inc(heads, 1)
            pool.wait_ge(heads, 2)
            nc.gpsimd.affine_select(out=m.head_sum[:, :], in_=m.head_sum[:, :], compare_op=ALU.is_ge, fill=0.0,
                                    base=0, pattern=[[-HD, H]], channel_multiplier=1).then_inc(heads, 1)
            nc.gpsimd.affine_select(out=m.head_spread[:, :], in_=m.head_spread[:, :], compare_op=ALU.is_ge,
                                    fill=0.0, base=0, pattern=[[1, P]], channel_multiplier=-HD).then_inc(heads, 1)
            pool.wait_ge(heads, 4)
            nc.gpsimd.affine_select(out=m.head_sum[:, :], in_=m.head_sum[:, :], compare_op=ALU.is_ge, fill=0.0,
                                    base=HD - 1, pattern=[[HD, H]], channel_multiplier=-1).then_inc(heads, 1)
            nc.gpsimd.affine_select(out=m.head_spread[:, :], in_=m.head_spread[:, :], compare_op=ALU.is_ge,
                                    fill=0.0, base=HD - 1, pattern=[[-1, P]], channel_multiplier=HD
                                    ).then_inc(heads, 1)

        @block.tensor
        def _(pe):
            pe.wait_ge(id_made, 2)
            pe.wait_ge(w_in, 16 * W_DMAS)
            for l in range(LAYERS):
                last = nc.tensor.transpose(pW[:, l, :], W2[:, l, :], m.ident[:, :])
            last.then_inc(w2_turned, 1)
            pe.wait_ge(floats, 4)
            for q in range(4):
                nc.tensor.transpose(pT[q][:, 0:P], rows_f[:, q, 0, :], m.ident[:, :])
                last = nc.tensor.transpose(pT[q][:, P:TILES], rows_f[0:LO, q, 1, :], m.ident[0:LO, 0:LO])
                last.then_inc(turned, 1)
            pe.wait_ge(w2T_ready, 1)
            pe.wait_ge(wide_ready, 3)
            nc.tensor.matmul(pG[:, 0:2 * P], W2T[:, 0, :], WW[:, 0].rearrange("p a b -> p (a b)"),
                             start=True, stop=True)
            last = nc.tensor.matmul(pG[:, 2 * P:4 * P], W2T[:, 1, :], WW[:, 1].rearrange("p a b -> p (a b)"),
                                    start=True, stop=True)
            last.then_inc(products, 1)
            pe.wait_ge(cols_ready, 4)
            nc.tensor.matmul(pT[0][:, 0:P], W2T[:, 2, :], Wf[:, 3, :], start=True, stop=True)
            nc.tensor.matmul(pT[1][0:1, 0:P], b2[:, 0:1], W1[:, 0, :], start=True, stop=True)
            nc.tensor.matmul(pT[1][0:1, P:2 * P], b2[:, 1:2], W1[:, 1, :], start=True, stop=True)
            nc.tensor.matmul(pT[2][:, 0:1], W1[:, 0, :], b2[:, 0:1], start=True, stop=True)
            nc.tensor.matmul(pT[2][:, 1:2], W1[:, 1, :], b2[:, 1:2], start=True, stop=True)
            for l in range(LAYERS):
                last = nc.tensor.matmul(pC[:, 0:P], b2_wide[:, l, :], Wf[:, l + 1, :],
                                        start=(l == 0), stop=(l == LAYERS - 1))
            last.then_inc(products, 1)

        @block.vector
        def _(dve):
            nc.vector.memset(fill[:, 0:P], EDGE_OF_LIST).then_inc(filled, 1)
            nc.vector.memset(fill[:, P:2 * P], PAD_DST).then_inc(filled, 1)
            nc.vector.memset(fill[:, 2 * P:3 * P], 0).then_inc(filled, 1)
            nc.vector.memset(m.ones_row[:, :], 1.0).then_inc(consts, 1)
            nc.vector.memset(m.minus_half[:, :], -0.5).then_inc(consts, 1)
            nc.vector.memset(m.eps[:, :], LN_EPS).then_inc(consts, 1)
            nc.vector.memset(m.same[:, EP:EP + 1], 0).then_inc(consts, 1)
            dve.wait_ge(w_in, 16 * W_DMAS)
            nc.vector.tensor_copy(WW[:, :, 0, :], W1[:, :, :]).then_inc(wide_ready, 1)
            nc.vector.tensor_copy(WW[:, :, 1, :], Wf[:, 1:3, :]).then_inc(wide_ready, 1)
            nc.vector.tensor_copy(b2_wide[:, :, :], b2[:, :].unsqueeze(2).to_broadcast([P, LAYERS, P])
                                  ).then_inc(wide_ready, 1)
            nc.vector.tensor_copy(m.bo[:, :, :], bo1[:, :].unsqueeze(1).to_broadcast([P, NR, P])
                                  ).then_inc(consts, 1)
            nc.vector.tensor_copy(m.Wb8[:, 1:H], m.Wb8[:, 0:1].to_broadcast([ED, H - 1])).then_inc(consts, 1)
            nc.vector.tensor_scalar(m.scale[:, :], m.scale[:, :], 1.0, None, ALU.add).then_inc(small, 1)
            dve.wait_ge(w2_turned, 1)
            nc.vector.tensor_copy(W2T[:, :, :], pW[:, :, :]).then_inc(w2T_ready, 1)
            dve.wait_ge(id_made, 2)
            nc.vector.tensor_tensor(m.W0f[:, :], Wf[:, 0, :], m.ident[:, :], ALU.add).then_inc(consts, 1)
            dve.wait_ge(index_in, 128)
            for q in range(4):
                nc.vector.tensor_copy(rows_f[:, q, 0, :], rows_i[:, q, 0, :])
                nc.vector.tensor_copy(rows_f[0:LO, q, 1, :], rows_i[0:LO, q, 1, :]).then_inc(floats, 1)
            for q in range(4):
                dve.wait_ge(turned, q + 1)
                nc.vector.tensor_copy(cols[:, q, :], pT[q][:, 0:TILES]).then_inc(cols_ready, 1)
            dve.wait_ge(cols_ready, 4)
            nc.vector.tensor_tensor(eq[:, 0, :], cols[:, 0, :], cols[:, 1, :], ALU.is_equal).then_inc(eq_ready, 1)
            nc.vector.tensor_tensor(eq[:, 1, :], cols[:, 0, :], cols[:, 2, :], ALU.is_equal).then_inc(eq_ready, 1)
            nc.vector.tensor_copy(m.src_idx[:, :], cols[:, 3, :]).then_inc(idx_done, 1)
            nc.vector.tensor_scalar(m.dst_idx[:, :], cols[:, 0, :], float(N - 1), None, ALU.min
                                    ).then_inc(idx_done, 1)
            dve.wait_ge(eq_ready, 2)
            nc.vector.scalar_tensor_tensor(out=m.final_to[:, :], in0=eq[:, 0, :], scalar=float(SKIP),
                                           in1=cols[:, 0, :], op0=ALU.mult, op1=ALU.add).then_inc(idx_done, 1)
            nc.vector.scalar_tensor_tensor(out=m.slot_to[:, :], in0=eq[:, 1, :], scalar=float(SKIP),
                                           in1=cols[:, 0, :], op0=ALU.mult, op1=ALU.add).then_inc(idx_done, 1)
            dve.wait_ge(products, 2)
            nc.vector.tensor_copy(m.MG1[:, :], pG[:, 0:2 * P]).then_inc(prod_out, 1)
            nc.vector.tensor_copy(m.MG2[:, :], pG[:, 2 * P:4 * P]).then_inc(prod_out, 1)
            nc.vector.tensor_copy(m.G3[:, :], pT[0][:, 0:P]).then_inc(prod_out, 1)
            nc.vector.tensor_copy(m.c_row[:, :, :], pT[1][0:1, 0:2 * P].rearrange("o (a b) -> o a b", a=2)
                                  ).then_inc(prod_out, 1)
            nc.vector.tensor_copy(m.c[:, :], pT[2][:, 0:2]).then_inc(prod_out, 1)
            nc.vector.tensor_tensor(m.cf[:, 0, :], pC[:, 0:P], bf[:, :], ALU.add).then_inc(prod_out, 1)
            dve.wait_ge(prod_out, 6)
            dve.wait_ge(small, 1)
            nc.vector.tensor_copy(m.cf[:, 1:NR, :], m.cf[:, 0:1, :].to_broadcast([P, NR - 1, P])
                                  ).then_inc(consts, 1)
            nc.vector.tensor_tensor(m.beta[:, :], m.c[:, :], m.scale[:, 1:3], ALU.mult).then_inc(small, 1)
            dve.wait_ge(small, 2)
            nc.vector.tensor_tensor(m.beta[:, :], m.beta[:, :], m.b1[:, 1:3], ALU.add).then_inc(consts, 1)



def node_rows(t, start):
    return t[bass.DynSlice(start, NT), :].rearrange("(p j) d -> p (j d)", j=NR)


def edge_rows(t, start):
    return t[bass.DynSlice(start, ET), :].rearrange("(j p) d -> p j d", p=P)


def nodes_and_first_layer(nc, m, a, out):
    with ExitStack() as ctx:
        sem, pair = sem_maker(nc, ctx, "nodes", 2)

        def sb2(name, shape, dt=F32):
            return [ctx.enter_context(nc.sbuf_tensor(f"{name}{h}", shape, dt)) for h in range(2)]

        def sb(name, shape, dt=F32):
            return ctx.enter_context(nc.sbuf_tensor(name, shape, dt))

        def ps(name, shape):
            return ctx.enter_context(nc.psum_tensor(name, shape, F32))

        x_in = sb2("x_in", [P, NT])
        xT = sb2("xT", [P, NT])
        r1 = sb2("r1", [P, NT])
        r2 = sb2("r2", [P, NT])
        r3 = sb2("r3", [P, NT])
        y1s = sb2("y1s", [P, NT])
        y2s = sb2("y2s", [P, NT])
        u = sb2("u", [P, NR, P])
        x1s = sb2("x1s", [P, NR, P])
        fins = sb2("fins", [P, NR, P])
        stats = sb2("stats", [P, 2, NR, 6])
        mv = sb2("mv", [P, 2, NR, 2])
        std = sb2("std", [P, 2, NR])
        rstd = sb2("rstd", [P, 2, NR])
        dst_wide = sb("dst_wide", [P, 2 * ET + 1], I32)
        stage = sb("stage", [P, 2 * CHUNK], I32)
        to_put = sb2("to_put", [P, CHUNK], I32)
        put_rows = sb2("put_rows", [P, CHUNK], I32)
        to_find = sb2("to_find", [P, CHUNK], I32)
        found = sb2("found", [P, CHUNK], I32)
        gs = sb2("gs", [P, ER, P])
        gd = sb2("gd", [P, ER, P])
        xdT = sb2("xdT", [P, ET])
        agg = sb2("agg", [P, ET])
        z = sb2("z", [P, ET])
        re = sb2("re", [P, ET])
        rows_s = sb2("rows_s", [P, ER, 2 * P])

        chain = [ps(f"chain{h}", [P, NT]) for h in range(2)]
        yb = [ps(f"yb{h}", [P, NT]) for h in range(2)]
        ob = ps("ob", [P, NR, P])
        e0 = ps("e0", [P, 2, ET])
        e1 = ps("e1", [P, 2, ET])
        e2 = ps("e2", [P, ER, 2 * P])

        x_loaded = pair("x_loaded")
        t_done = pair("t_done")
        xT_ready = pair("xT_ready")
        l1_done = pair("l1_done")
        r1_ready = pair("r1_ready")
        l2_done = pair("l2_done")
        r2_ready = pair("r2_ready")
        l3_done = pair("l3_done")
        r3_ready = pair("r3_ready")
        y1_done = pair("y1_done")
        y1_out = pair("y1_out")
        y1_stored = pair("y1_stored")
        y2_done = pair("y2_done")
        y2_out = pair("y2_out")
        y2_stored = pair("y2_stored")
        o_done = pair("o_done")
        u_ready = pair("u_ready")
        stats_ready = [pair(f"stats_ready{n}") for n in range(2)]
        mv_ready = [pair(f"mv_ready{n}") for n in range(2)]
        std_ready = [pair(f"std_ready{n}") for n in range(2)]
        rstd_ready = [pair(f"rstd_ready{n}") for n in range(2)]
        x1_ready = pair("x1_ready")
        x1_stored = pair("x1_stored")
        v_ready = pair("v_ready")
        fin_ready = pair("fin_ready")
        fin_stored = pair("fin_stored")
        dst_loaded = sem("dst_loaded")
        mask_ready = sem("mask_ready")
        carry_ready = sem("carry_ready")
        staged = sem("staged")
        slots_staged = sem("slots_staged")
        slots_put = pair("slots_put")
        finds_staged = sem("finds_staged")
        rows_found = pair("rows_found")
        found_kept = sem("found_kept")
        gathered = pair("gathered")
        te_done = pair("te_done")
        xdT_ready = pair("xdT_ready")
        agg_ready = pair("agg_ready")
        z_ready = pair("z_ready")
        le_done = pair("le_done")
        re_ready = pair("re_ready")
        me_done = pair("me_done")
        slot_ready = pair("slot_ready")
        rows_done = pair("rows_done")
        rows_out = pair("rows_out")
        rows_stored = pair("rows_stored")
        passed_pool = sem("passed_pool")
        passed_dve = sem("passed_dve")
        block = ctx.enter_context(nc.Block())

        @block.sync
        def _(sp):
            def load(i, last=False):
                for h in range(2):
                    reuse(sp, t_done[h], i)
                    start = LAST_NODE if last and h == 1 else (2 * i + h) * NT
                    sp.dma_start(x_in[h][:, :], node_rows(a["x"], start)).then_inc(x_loaded[h], 16)
                reuse(sp, mask_ready, i)
                sp.dma_start(dst_wide[:, :],
                             m.dst_list[bass.DynSlice(i * 2 * ET, 2 * ET + 1), :].rearrange("n o -> o n")
                             .to_broadcast([P, 2 * ET + 1])).then_inc(dst_loaded, 16)

            def store(i, last=False):
                for h in range(2):
                    start = LAST_NODE if last and h == 1 else (2 * i + h) * NT
                    if last and h == 1:
                        sp.wait_ge(y1_stored[0], 16 * STEPS)
                        sp.wait_ge(y2_stored[0], 16 * STEPS)
                    sp.wait_ge(y1_out[h], i + 1)
                    sp.dma_start(node_rows(m.y1_table, start), y1s[h][:, :]).then_inc(y1_stored[h], 16)
                    sp.wait_ge(y2_out[h], i + 1)
                    sp.dma_start(node_rows(m.y2_table, start), y2s[h][:, :]).then_inc(y2_stored[h], 16)
                    sp.wait_ge(rows_out[h], i + 1)
                    edge = (2 * i + h) * ET
                    sp.dma_start(edge_rows(m.y1_table, edge + N), rows_s[h][:, :, 0:P]
                                 ).then_inc(rows_stored[h], 16)
                    sp.dma_start(edge_rows(m.skip_rows, edge), rows_s[h][:, :, P:2 * P]
                                 ).then_inc(rows_stored[h], 16)

            def store_norms(i, last=False):
                for h in range(2):
                    start = LAST_NODE if last and h == 1 else (2 * i + h) * NT
                    if last and h == 1:
                        sp.wait_ge(x1_stored[0], 16 * STEPS)
                        sp.wait_ge(fin_stored[0], 16 * STEPS)
                    sp.wait_ge(x1_ready[h], i + 1)
                    sp.dma_start(node_rows(m.x1_table, start), x1s[h].rearrange("p j d -> p (j d)")
                                 ).then_inc(x1_stored[h], 16)
                    sp.wait_ge(fin_ready[h], i + 1)
                    sp.dma_start(node_rows(out, start), fins[h].rearrange("p j d -> p (j d)")
                                 ).then_inc(fin_stored[h], 16)

            load(0)
            load(1)
            store(0)
            with sp.Fori(1, STEPS - 2) as i:
                load(i + 1)
                store_norms(i - 1)
                store(i)
            load(STEPS - 1, last=True)
            store_norms(STEPS - 3)
            store(STEPS - 2)
            store_norms(STEPS - 2)
            store(STEPS - 1, last=True)
            store_norms(STEPS - 1, last=True)
            for h in range(2):
                for s in (y1_stored, y2_stored, x1_stored, fin_stored):
                    sp.wait_ge(s[h], 16 * STEPS)
                sp.wait_ge(rows_stored[h], 32 * STEPS)

        @block.tensor
        def _(pe):
            def node_turn(i, h):
                pe.wait_ge(x_loaded[h], 16 * (i + 1))
                reuse(pe, r3_ready[h], i)
                for j in range(NR):
                    last = nc.tensor.transpose(chain[h][:, j * P:(j + 1) * P], x_in[h][:, j * P:(j + 1) * P],
                                               m.ident[:, :])
                last.then_inc(t_done[h], 1)

            def layer(i, h, ready, w, src, done):
                pe.wait_ge(ready[h], i + 1)
                nc.tensor.matmul(chain[h][:, :], w, src[h][:, :], start=True, stop=True).then_inc(done[h], 1)

            def y_rows(i, h, free, count, w, src, done):
                pe.wait_ge(free[h], count)
                for j in range(NR):
                    last = nc.tensor.matmul(yb[h][:, j * P:(j + 1) * P], src[h][:, j * P:(j + 1) * P], w,
                                            start=True, stop=True)
                last.then_inc(done[h], 1)

            def out_rows(i, h):
                pe.wait_ge(r3_ready[h], i + 1)
                reuse(pe, u_ready[1 - h], i + h)
                for j in range(NR):
                    cut = slice(j * P, (j + 1) * P)
                    nc.tensor.matmul(ob[:, j, :], xT[h][:, cut], m.W0f[:, :], start=True, stop=False)
                    nc.tensor.matmul(ob[:, j, :], r1[h][:, cut], m.MG1[:, P:2 * P], start=False, stop=False)
                    nc.tensor.matmul(ob[:, j, :], r2[h][:, cut], m.MG2[:, P:2 * P], start=False, stop=False)
                    last = nc.tensor.matmul(ob[:, j, :], r3[h][:, cut], m.G3[:, :], start=False, stop=True)
                last.then_inc(o_done[h], 1)

            def edge_turn(i, h):
                pe.wait_ge(gathered[h], 64 * (i + 1))
                reuse(pe, agg_ready[1 - h], i + h)
                reuse(pe, xdT_ready[1 - h], i + h)
                for j in range(ER):
                    nc.tensor.transpose(e0[:, 0, j * P:(j + 1) * P], gs[h][:, j, :], m.ident[:, :])
                for j in range(ER):
                    last = nc.tensor.transpose(e0[:, 1, j * P:(j + 1) * P], gd[h][:, j, :], m.ident[:, :])
                last.then_inc(te_done[h], 1)

            def edge_layer(i, h):
                pe.wait_ge(z_ready[h], i + 1)
                reuse(pe, slot_ready[1 - h], i + h)
                nc.tensor.matmul(e1[:, 0, :], m.W1_0[:, :], z[h][:, :], start=True, stop=True
                                 ).then_inc(le_done[h], 1)

            def edge_rows_out(i, h):
                pe.wait_ge(re_ready[h], i + 1)
                nc.tensor.matmul(e1[:, 1, :], m.MG1[:, 0:P], re[h][:, :], start=True, stop=True
                                 ).then_inc(me_done[h], 1)
                pe.wait_ge(xdT_ready[h], i + 1)
                reuse(pe, rows_out[1 - h], i + h)
                for j in range(ER):
                    cut = slice(j * P, (j + 1) * P)
                    nc.tensor.matmul(e2[:, j, :], re[h][:, cut], m.MG1[:, :], start=True, stop=True,
                                     skip_group_check=True)
                    last = nc.tensor.matmul(e2[:, j, P:2 * P], xdT[h][:, cut], m.W0f[:, :], start=False,
                                            stop=True, skip_group_check=True)
                last.then_inc(rows_done[h], 1)

            def step(i):
                node_turn(i, 0)
                node_turn(i, 1)
                layer(i, 0, xT_ready, m.W1_0[:, :], xT, l1_done)
                layer(i, 1, xT_ready, m.W1_0[:, :], xT, l1_done)
                edge_turn(i, 0)
                for h in range(2):
                    layer(i, h, r1_ready, m.MG1[:, 0:P], r1, l2_done)
                    y_rows(i, h, y2_out, i, m.MG1[:, 0:P], r1, y1_done)
                edge_layer(i, 0)
                edge_turn(i, 1)
                for h in range(2):
                    layer(i, h, r2_ready, m.MG2[:, 0:P], r2, l3_done)
                    y_rows(i, h, y1_out, i + 1, m.MG2[:, 0:P], r2, y2_done)
                edge_rows_out(i, 0)
                edge_layer(i, 1)
                out_rows(i, 0)
                edge_rows_out(i, 1)
                out_rows(i, 1)

            step(0)
            with pe.Fori(1, STEPS) as i:
                step(i)

        @block.scalar
        def _(act):
            def turn_out(i, h):
                act.wait_ge(t_done[h], i + 1)
                reuse(act, o_done[h], i)
                nc.scalar.activation(xT[h][:, :], chain[h][:, :], ACT.Copy).then_inc(xT_ready[h], 1)

            def relu(i, h, done, scale, bias, dst, ready):
                act.wait_ge(done[h], i + 1)
                nc.scalar.activation(dst[h][:, :], chain[h][:, :], ACT.Relu, bias=bias, scale=scale
                                     ).then_inc(ready[h], 1)

            def y_out(i, h, done, stored, dst, copied):
                act.wait_ge(done[h], i + 1)
                reuse(act, stored[h], 16 * i)
                nc.scalar.activation(dst[h][:, :], yb[h][:, :], ACT.Copy).then_inc(copied[h], 1)

            def edge_turn_out(i, h):
                act.wait_ge(te_done[h], i + 1)
                reuse(act, rows_done[h], i)
                reuse(act, z_ready[h], i)
                nc.scalar.activation(xdT[h][:, :], e0[:, 1, :], ACT.Copy).then_inc(xdT_ready[h], 1)

            def edge_relu(i, h):
                act.wait_ge(le_done[h], i + 1)
                reuse(act, rows_done[h], i)
                nc.scalar.activation(re[h][:, :], e1[:, 0, :], ACT.Relu, bias=m.b1[:, 0:1]
                                     ).then_inc(re_ready[h], 1)

            def edge_out(i, h):
                act.wait_ge(me_done[h], i + 1)
                nc.scalar.activation(m.slots[:, bass.DynSlice((2 * i + h) * ET, ET)], e1[:, 1, :],
                                     ACT.Identity, bias=m.c[:, 0:1]).then_inc(slot_ready[h], 1)
                act.wait_ge(rows_done[h], i + 1)
                reuse(act, rows_stored[h], 32 * i)
                nc.scalar.activation(rows_s[h][:, :, :], e2[:, :, :], ACT.Copy).then_inc(rows_out[h], 1)

            def root(i, h, n):
                act.wait_ge(mv_ready[n][h], NR * (i + 1))
                reuse(act, rstd_ready[n][h], i)
                nc.scalar.activation(std[h][:, n, :], mv[h][:, n, :, 1], ACT.Sqrt, bias=m.eps[:, 0:1]
                                     ).then_inc(std_ready[n][h], 1)

            def step(i, norms=True):
                turn_out(i, 0)
                turn_out(i, 1)
                relu(i, 0, l1_done, m.scale[:, 0:1], m.b1[:, 0:1], r1, r1_ready)
                relu(i, 1, l1_done, m.scale[:, 0:1], m.b1[:, 0:1], r1, r1_ready)
                if norms:
                    root(i - 1, 0, 0)
                    root(i - 1, 1, 0)
                edge_turn_out(i, 0)
                for h in range(2):
                    relu(i, h, l2_done, m.scale[:, 1:2], m.beta[:, 0:1], r2, r2_ready)
                    y_out(i, h, y1_done, y1_stored, y1s, y1_out)
                edge_relu(i, 0)
                edge_turn_out(i, 1)
                if norms:
                    root(i - 1, 0, 1)
                    root(i - 1, 1, 1)
                for h in range(2):
                    relu(i, h, l3_done, m.scale[:, 2:3], m.beta[:, 1:2], r3, r3_ready)
                    y_out(i, h, y2_done, y2_stored, y2s, y2_out)
                edge_out(i, 0)
                edge_relu(i, 1)
                edge_out(i, 1)

            step(0, norms=False)
            step(1)
            with act.Fori(2, STEPS) as i:
                step(i)
            for n in range(2):
                for h in range(2):
                    root(STEPS - 1, h, n)

        @block.vector
        def _(dve):
            nc.vector.memset(agg[1][:, :], 0.0).then_inc(carry_ready, 1)
            dve.wait_ge(carry_ready, 1)

            def mask(i):
                dve.wait_ge(dst_loaded, 16 * (i + 1))
                nc.vector.tensor_tensor(m.same[:, bass.DynSlice(i * 2 * ET, 2 * ET)], dst_wide[:, 1:2 * ET + 1],
                                        dst_wide[:, 0:2 * ET], ALU.is_equal).then_inc(mask_ready, 1)
                dve.wait_ge(mask_ready, i + 1)

            def sums(i, h):
                dve.wait_ge(xdT_ready[h], i + 1)
                reuse(dve, agg_ready[1 - h], i + h)
                nc.vector.tensor_tensor_scan(agg[h][:, :], m.same[:, bass.DynSlice((2 * i + h) * ET, ET)],
                                             e0[:, 0, :], agg[1 - h][:, ET - 1:ET], ALU.mult, ALU.add
                                             ).then_inc(agg_ready[h], 1)
                dve.wait_ge(agg_ready[h], i + 1)
                reuse(dve, le_done[h], i)
                nc.vector.scalar_tensor_tensor(out=z[h][:, :], in0=xdT[h][:, :], scalar=m.scale[:, 0:1],
                                               in1=agg[h][:, :], op0=ALU.mult, op1=ALU.add
                                               ).then_inc(z_ready[h], 1)

            def moments(i, h, n, src, src_ready):
                dve.wait_ge(src_ready[h], i + 1)
                for j in range(NR):
                    nc.vector.bn_stats(stats[h][:, n, j, :], src[h][:, j, :]).then_inc(stats_ready[n][h], 1)
                dve.wait_ge(stats_ready[n][h], NR * (i + 1))
                settle(dve, passed_dve)
                for j in range(NR):
                    nc.vector.bn_aggr(mv[h][:, n, j, :], stats[h][:, n, j, :]).then_inc(mv_ready[n][h], 1)

            def inverse(i, h, n):
                dve.wait_ge(std_ready[n][h], i + 1)
                nc.vector.reciprocal(rstd[h][:, n, :], std[h][:, n, :]).then_inc(rstd_ready[n][h], 1)

            def normed(i, h, n, dst, stored, ready):
                dve.wait_ge(rstd_ready[n][h], i + 1)
                reuse(dve, stored[h], 16 * i)
                for j in range(NR):
                    last = nc.vector.tensor_scalar(dst[h][:, j, :], u[h][:, j, :], mv[h][:, n, j, 0:1],
                                                   rstd[h][:, n, j:j + 1], ALU.subtract, ALU.mult)
                last.then_inc(ready[h], 1)

            def first_norm(i):
                for h in range(2):
                    inverse(i, h, 0)
                for h in range(2):
                    normed(i, h, 0, x1s, x1_stored, x1_ready)
                for h in range(2):
                    dve.wait_ge(x1_ready[h], i + 1)
                    nc.vector.tensor_tensor(u[h][:, :, :], x1s[h][:, :, :], m.bo[:, :, :], ALU.add
                                            ).then_inc(v_ready[h], 1)
                    moments(i, h, 1, u, v_ready)

            def second_norm(i):
                for h in range(2):
                    inverse(i, h, 1)
                for h in range(2):
                    normed(i, h, 1, fins, fin_stored, fin_ready)

            def add_constant(i, h):
                dve.wait_ge(o_done[h], i + 1)
                reuse(dve, fin_ready[h], i)
                nc.vector.tensor_tensor(u[h][:, :, :], ob[:, :, :], m.cf[:, :, :], ALU.add
                                        ).then_inc(u_ready[h], 1)
                moments(i, h, 0, u, u_ready)

            def step(i, norms=True):
                mask(i)
                if norms:
                    first_norm(i - 1)
                sums(i, 0)
                sums(i, 1)
                if norms:
                    second_norm(i - 1)
                add_constant(i, 0)
                add_constant(i, 1)

            step(0, norms=False)
            step(1)
            with dve.Fori(2, STEPS) as i:
                step(i)
            first_norm(STEPS - 1)
            second_norm(STEPS - 1)

        @block.gpsimd
        def _(pool):
            def gather(i):
                for h in range(2):
                    reuse(pool, te_done[h], i)
                nc.gpsimd.tensor_copy(stage[:, 0:CHUNK], m.src_idx[:, bass.DynSlice(i * CHUNK, CHUNK)]
                                      ).then_inc(staged, 1)
                nc.gpsimd.tensor_copy(stage[:, CHUNK:2 * CHUNK], m.dst_idx[:, bass.DynSlice(i * CHUNK, CHUNK)]
                                      ).then_inc(staged, 1)
                pool.wait_ge(staged, 2 * (i + 1))
                settle(pool, passed_pool)
                for h in range(2):
                    for j in range(ER):
                        for c, g in ((0, gs), (CHUNK, gd)):
                            col = c + h * ER + j
                            nc.gpsimd.indirect_dma_start(
                                out=g[h][:, j, :], out_offset=None, in_=a["x"],
                                in_offset=bass.IndirectOffsetOnAxis(ap=stage[:, col:col + 1], axis=0),
                            ).then_inc(gathered[h], 16)

            def put_slots(n, q):
                reuse(pool, slots_put[q], 16 * CHUNK * ((n - q) // 2))
                nc.gpsimd.tensor_copy(to_put[q][:, :], m.slot_to[:, bass.DynSlice(n * CHUNK, CHUNK)]
                                      ).then_inc(slots_staged, 1)
                nc.gpsimd.tensor_copy(put_rows[q][:, :], m.slot_row[:, bass.DynSlice(n * CHUNK, CHUNK)]
                                      ).then_inc(slots_staged, 1)
                pool.wait_ge(slots_staged, 2 * n + 2)
                settle(pool, passed_pool)
                for j in range(CHUNK):
                    nc.gpsimd.indirect_dma_start(
                        out=m.row_of_node, in_=put_rows[q][:, j:j + 1], in_offset=None,
                        out_offset=bass.IndirectOffsetOnAxis(ap=to_put[q][:, j:j + 1], axis=0),
                        bounds_check=N - 1, oob_is_err=False,
                    ).then_inc(slots_put[q], 16)

            def find_rows(n, q):
                reuse(pool, found_kept, n - 1)
                nc.gpsimd.tensor_copy(to_find[q][:, :], m.src_idx[:, bass.DynSlice(n * CHUNK, CHUNK)]
                                      ).then_inc(finds_staged, 1)
                pool.wait_ge(finds_staged, n + 1)
                settle(pool, passed_pool)
                for j in range(CHUNK):
                    nc.gpsimd.indirect_dma_start(
                        out=found[q][:, j:j + 1], out_offset=None, in_=m.row_of_node,
                        in_offset=bass.IndirectOffsetOnAxis(ap=to_find[q][:, j:j + 1], axis=0),
                    ).then_inc(rows_found[q], 16)

            def keep_rows(n, q):
                pool.wait_ge(rows_found[q], 16 * CHUNK * ((n - q) // 2 + 1))
                nc.gpsimd.tensor_copy(m.src_row[:, bass.DynSlice(n * CHUNK, CHUNK)], found[q][:, :]
                                      ).then_inc(found_kept, 1)

            half = STEPS // 2

            def putting_step(i):
                gather(i + 1)
                put_slots(2 * i, 0)
                put_slots(2 * i + 1, 1)

            def finding_step(i, n, first=False):
                gather(i + 1)
                find_rows(n, 0)
                if not first:
                    keep_rows(n - 1, 1)
                find_rows(n + 1, 1)
                keep_rows(n, 0)

            gather(0)
            putting_step(0)
            with pool.Fori(1, half) as i:
                putting_step(i)
            put_slots(2 * half, 0)
            pool.wait_ge(slots_put[0], 16 * CHUNK * (half + 1))
            pool.wait_ge(slots_put[1], 16 * CHUNK * half)
            finding_step(half, 0, first=True)
            with pool.Fori(half + 1, STEPS - 1) as i:
                finding_step(i, 2 * i - 2 * half)
            find_rows(2 * half, 0)
            keep_rows(2 * half - 1, 1)
            keep_rows(2 * half, 0)



def pipeline(eng, units, stages):
    lags = [lag for _, lag in stages]
    first = -(-(max(lags) + RING) // RING)
    last = (units + min(lags)) // RING

    def single(s):
        for stage, lag in stages:
            if 0 <= s - lag < units:
                stage(s - lag, (s - lag) % RING)

    for s in range(min(0, min(lags)), RING * first):
        single(s)
    with eng.Fori(first, last) as i:
        for r in range(RING):
            for stage, lag in stages:
                stage(RING * i + r - lag, (r - lag) % RING)
    for s in range(RING * last, units + max(lags)):
        single(s)


def edge_layer(nc, m, l):
    final = l == 2
    src_table = m.y2_table if final else m.y1_table
    with ExitStack() as ctx:
        sem, ring_of_sems = sem_maker(nc, ctx, f"layer{l}")

        def ring(name, shape, dt=F32):
            return [ctx.enter_context(nc.sbuf_tensor(f"{name}_l{l}{q}", shape, dt)) for q in range(RING)]

        def banks(name, shape):
            return [ctx.enter_context(nc.psum_tensor(f"{name}_l{l}{q}", shape, F32)) for q in range(2)]

        stage = ring("stage", [P, ER], I32)
        gs = ring("gs", [P, ER, P])
        agg = ring("agg", [P, ET])
        pre = ring("pre", [P, ET])
        re = ring("re", [P, ET])
        skip_in = ring("skip_in", [P, ER, P])
        y_out = ring("y_out", [P, ER, P])
        s_out = ring("s_out", [P, ER, P])
        stats = ring("stats", [P, ER, 6])
        mv = ring("mv", [P, ER, 2])
        std = ring("std", [P, ER])
        rstd = ring("rstd", [P, ER])
        pt = banks("pt", [P, ET])
        pm = banks("pm", [P, 512])
        pr = banks("pr", [P, ER, 2 * P])

        gathered = ring_of_sems("gathered")
        skip_loaded = ring_of_sems("skip_loaded")
        stored = ring_of_sems("stored")
        staged = sem("staged")
        t_done = sem("t_done")
        agg_ready = sem("agg_ready")
        pre_ready = sem("pre_ready")
        re_ready = sem("re_ready")
        m_done = sem("m_done")
        slot_ready = sem("slot_ready")
        rows_done = sem("rows_done")
        y_ready = sem("y_ready")
        sum_ready = sem("sum_ready")
        sum2_ready = sem("sum2_ready")
        stats_ready = sem("stats_ready")
        mv_ready = sem("mv_ready")
        std_ready = sem("std_ready")
        rstd_ready = sem("rstd_ready")
        x1_ready = sem("x1_ready")
        x1_turned = sem("x1_turned")
        carry_ready = sem("carry_ready")
        passed_pool = sem("passed_pool")
        passed_dve = sem("passed_dve")
        block = ctx.enter_context(nc.Block())

        @block.sync
        def _(sp):
            def load_skip(n, q):
                reuse(sp, sum_ready, n - RING + 1)
                sp.dma_start(skip_in[q][:, :, :], edge_rows(m.skip_rows, n * ET)).then_inc(skip_loaded[q], 16)

            def store(n, q):
                if final:
                    sp.wait_ge(x1_ready, n + 1)
                    sp.dma_start(edge_rows(m.x1_table, n * ET + N), s_out[q][:, :, :]).then_inc(stored[q], 16)
                else:
                    sp.wait_ge(y_ready, n + 1)
                    sp.dma_start(edge_rows(m.y2_table, n * ET + N), y_out[q][:, :, :]).then_inc(stored[q], 16)
                    sp.wait_ge(sum_ready, n + 1)
                    sp.dma_start(edge_rows(m.skip_rows, n * ET), s_out[q][:, :, :]).then_inc(stored[q], 16)

            pipeline(sp, UNITS, [(load_skip, -1), (store, 4 if final else 3)])
            for q in range(RING):
                sp.wait_ge(stored[q], (16 if final else 32) * uses(q))

        @block.gpsimd
        def _(pool):
            def gather(n, q):
                reuse(pool, t_done, n - RING + 1)
                nc.gpsimd.tensor_copy(stage[q][:, :], m.src_row[:, bass.DynSlice(n * ER, ER)]
                                      ).then_inc(staged, 1)
                pool.wait_ge(staged, n + 1)
                settle(pool, passed_pool)
                for j in range(ER):
                    nc.gpsimd.indirect_dma_start(
                        out=gs[q][:, j, :], out_offset=None, in_=src_table,
                        in_offset=bass.IndirectOffsetOnAxis(ap=stage[q][:, j:j + 1], axis=0),
                    ).then_inc(gathered[q], 16)

            pipeline(pool, UNITS, [(gather, 0)])

        @block.tensor
        def _(pe):
            def turn(n, q):
                pe.wait_ge(gathered[q], 32 * use(n, q))
                reuse(pe, agg_ready, n - 1)
                for j in range(ER):
                    cut = slice(j * P, (j + 1) * P)
                    nc.tensor.matmul(pt[q % 2][:, cut], m.c_row[0:1, l - 1, :], m.ones_row[0:1, :],
                                     start=True, stop=False)
                    last = nc.tensor.matmul(pt[q % 2][:, cut], gs[q][:, j, :], m.ident[:, :],
                                            start=False, stop=True)
                last.then_inc(t_done, 1)

            def products(n, q):
                pe.wait_ge(re_ready, n + 1)
                reuse(pe, sum_ready, n - 1)
                if final:
                    for j in range(ER):
                        last = nc.tensor.matmul(pr[q % 2][:, j, 0:P], re[q][:, j * P:(j + 1) * P], m.G3[:, :],
                                                start=True, stop=True)
                    last.then_inc(rows_done, 1)
                    return
                reuse(pe, slot_ready, n - 1)
                nc.tensor.matmul(pm[q % 2][:, 0:ET], m.MG2[:, 0:P], re[q][:, :], start=True, stop=True
                                 ).then_inc(m_done, 1)
                for j in range(ER):
                    last = nc.tensor.matmul(pr[q % 2][:, j, :], re[q][:, j * P:(j + 1) * P], m.MG2[:, :],
                                            start=True, stop=True)
                last.then_inc(rows_done, 1)

            def turn_back(n, q):
                pe.wait_ge(x1_ready, n + 1)
                reuse(pe, slot_ready, n - 1)
                for j in range(ER):
                    last = nc.tensor.transpose(pm[q % 2][:, j * P:(j + 1) * P], s_out[q][:, j, :], m.ident[:, :])
                last.then_inc(x1_turned, 1)

            pipeline(pe, UNITS, [(turn, 0), (products, 1)] + [(turn_back, 4)] * final)

        @block.scalar
        def _(act):
            def relu(n, q):
                act.wait_ge(pre_ready, n + 1)
                reuse(act, rows_done, n - RING + 1)
                nc.scalar.activation(re[q][:, :], pre[q][:, :], ACT.Relu, bias=m.b1[:, l:l + 1]
                                     ).then_inc(re_ready, 1)

            def take(n, q):
                act.wait_ge(m_done, n + 1)
                nc.scalar.activation(m.slots[:, bass.DynSlice(n * ET, ET)], pm[q % 2][:, 0:ET],
                                     ACT.Identity, bias=m.c[:, 1:2]).then_inc(slot_ready, 1)
                act.wait_ge(rows_done, n + 1)
                reuse(act, stored[q], 32 * (use(n, q) - 1))
                nc.scalar.activation(y_out[q][:, :, :], pr[q % 2][:, :, 0:P], ACT.Copy).then_inc(y_ready, 1)

            def root(n, q):
                act.wait_ge(mv_ready, ER * n + ER)
                reuse(act, rstd_ready, n - RING + 1)
                nc.scalar.activation(std[q][:, :], mv[q][:, :, 1], ACT.Sqrt, bias=m.eps[:, 0:1]
                                     ).then_inc(std_ready, 1)

            pipeline(act, UNITS, [(relu, 0), (root, 2)] if final else [(take, 1), (relu, 0)])

        @block.vector
        def _(dve):
            nc.vector.memset(agg[RING - 1][:, :], 0.0).then_inc(carry_ready, 1)
            dve.wait_ge(carry_ready, 1)

            def sums(n, q):
                dve.wait_ge(t_done, n + 1)
                reuse(dve, agg_ready, n)
                nc.vector.tensor_tensor_scan(agg[q][:, :], m.same[:, bass.DynSlice(n * ET, ET)],
                                             pt[q % 2][:, :], agg[q - 1][:, ET - 1:ET], ALU.mult, ALU.add
                                             ).then_inc(agg_ready, 1)
                dve.wait_ge(agg_ready, n + 1)
                reuse(dve, re_ready, n - RING + 1)
                nc.vector.scalar_tensor_tensor(out=pre[q][:, :], in0=m.slots[:, bass.DynSlice(n * ET, ET)],
                                               scalar=m.scale[:, l:l + 1], in1=agg[q][:, :],
                                               op0=ALU.mult, op1=ALU.add).then_inc(pre_ready, 1)

            def add_skip(n, q):
                dve.wait_ge(rows_done, n + 1)
                dve.wait_ge(skip_loaded[q], 16 * use(n, q))
                if not final:
                    dve.wait_ge(y_ready, n + 1)
                    reuse(dve, stored[q], 32 * (use(n, q) - 1))
                    nc.vector.tensor_tensor(s_out[q][:, :, :], pr[q % 2][:, :, P:2 * P], skip_in[q][:, :, :],
                                            ALU.add).then_inc(sum_ready, 1)
                    return
                nc.vector.tensor_tensor(y_out[q][:, :, :], pr[q % 2][:, :, 0:P], skip_in[q][:, :, :], ALU.add
                                        ).then_inc(sum_ready, 1)
                dve.wait_ge(sum_ready, n + 1)
                nc.vector.tensor_tensor(y_out[q][:, :, :], y_out[q][:, :, :], m.cf[:, 0:ER, :], ALU.add
                                        ).then_inc(sum2_ready, 1)
                dve.wait_ge(sum2_ready, n + 1)
                for j in range(ER):
                    nc.vector.bn_stats(stats[q][:, j, :], y_out[q][:, j, :]).then_inc(stats_ready, 1)
                dve.wait_ge(stats_ready, ER * n + ER)
                settle(dve, passed_dve)
                for j in range(ER):
                    nc.vector.bn_aggr(mv[q][:, j, :], stats[q][:, j, :]).then_inc(mv_ready, 1)

            def norm(n, q):
                dve.wait_ge(std_ready, n + 1)
                nc.vector.reciprocal(rstd[q][:, :], std[q][:, :]).then_inc(rstd_ready, 1)
                dve.wait_ge(rstd_ready, n + 1)
                reuse(dve, stored[q], 16 * (use(n, q) - 1))
                for j in range(ER):
                    last = nc.vector.tensor_scalar(s_out[q][:, j, :], y_out[q][:, j, :], mv[q][:, j, 0:1],
                                                   rstd[q][:, j:j + 1], ALU.subtract, ALU.mult)
                last.then_inc(x1_ready, 1)

            def keep_ends(n, q):
                dve.wait_ge(x1_turned, n + 1)
                nc.vector.scalar_tensor_tensor(out=m.slots[:, bass.DynSlice(n * ET, ET)],
                                               in0=m.same[:, bass.DynSlice(n * ET + 1, ET)], scalar=0.0,
                                               in1=pm[q % 2][:, 0:ET], op0=ALU.is_equal, op1=ALU.mult
                                               ).then_inc(slot_ready, 1)

            pipeline(dve, UNITS, [(sums, 0), (add_skip, 2)] + [(norm, 3), (keep_ends, 5)] * final)



def attention(nc, m, a, out):
    with ExitStack() as ctx:
        sem, ring_of_sems = sem_maker(nc, ctx, "attn")

        def ring(name, shape, dt=F32, size=RING):
            return [ctx.enter_context(nc.sbuf_tensor(f"{name}_at{q}", shape, dt)) for q in range(size)]

        def bank(name, shape):
            return ctx.enter_context(nc.psum_tensor(f"{name}_at", shape, F32))

        stage = ring("stage", [P, ER], I32)
        to_stage = ring("to_stage", [P, ER], I32)
        gs = ring("gs", [P, ER, P])
        ein = ring("ein", [P, ER, ED])
        ends = ring("ends", [P, ET])
        goes_on = ring("goes_on", [P, ET], U8)
        xs = ring("xs", [P, ET], size=2)
        eT = ring("eT", [ED, ET], size=2)
        xd = ring("xd", [P, ET])
        qh = ring("qh", [P, ET], size=2)
        v = ring("v", [P, ET])
        prod = ring("prod", [P, ET], size=2)
        sc = ring("sc", [H, ET], size=2)
        pen = ring("pen", [H, ET], size=2)
        mx = ring("mx", [H, ET + 1], size=2)
        tmp = ring("tmp", [H, ET], size=2)
        arg = ring("arg", [H, 2, ET], size=2)
        ex = ring("ex", [H, 2, ET], size=2)
        den = ring("den", [H, ET], size=2)
        rden = ring("rden", [H, ET], size=2)
        al = ring("al", [H, ET], size=2)
        va = ring("va", [P, ET], size=2)
        u = ring("u", [P, ER, P], size=2)
        fin = ring("fin", [P, ER, P])
        stats = ring("stats", [P, ER, 6])
        mv = ring("mv", [P, ER, 2])
        vare = ring("vare", [P, ER])
        rstd = ring("rstd", [P, ER])
        far = ctx.enter_context(nc.sbuf_tensor("far", [H, 1], F32))
        turned = bank("turned", [P, 512])
        qk = [bank(f"qk{q}", [P, 512]) for q in range(2)]
        vs = [bank(f"vs{q}", [P, 512]) for q in range(2)]
        spread = bank("spread", [P, ET])
        rows = [bank(f"rows{q}", [P, ER, P]) for q in range(2)]

        gathered = ring_of_sems("gathered")
        e_loaded = ring_of_sems("e_loaded")
        slots_in = ring_of_sems("slots_in")
        scattered = ring_of_sems("scattered")
        staged = sem("staged")
        to_staged = sem("to_staged")
        init = sem("init")
        e_clear = sem("e_clear")
        t_done = sem("t_done")
        xs_ready = sem("xs_ready")
        eT_ready = sem("eT_ready")
        xd_ready = sem("xd_ready")
        qk_done = sem("qk_done")
        v_done = sem("v_done")
        q_ready = sem("q_ready")
        v_ready = sem("v_ready")
        prod_ready = sem("prod_ready")
        sc_done = sem("sc_done")
        sc_ready = sem("sc_ready")
        pen_ready = sem("pen_ready")
        tail_ready = sem("tail_ready")
        mx_ready = sem("mx_ready")
        tmp_ready = sem("tmp_ready")
        arg_ready = sem("arg_ready")
        ex_ready = sem("ex_ready")
        den_ready = sem("den_ready")
        rden_ready = sem("rden_ready")
        al_ready = sem("al_ready")
        spread_done = sem("spread_done")
        va_ready = sem("va_ready")
        o_done = sem("o_done")
        u_ready = sem("u_ready")
        stats_ready = sem("stats_ready")
        mv_ready = sem("mv_ready")
        var_ready = sem("var_ready")
        rstd_ready = sem("rstd_ready")
        fin_ready = sem("fin_ready")
        passed_pool = sem("passed_pool")
        passed_dve = sem("passed_dve")
        passed_sp = sem("passed_sp")
        block = ctx.enter_context(nc.Block())

        def first_edge(n):
            return (UNITS - 1) * ET - n * ET

        @block.sync
        def _(sp):
            def load(n, q):
                first = first_edge(n)
                reuse(sp, xd_ready, n - RING + 1)
                reuse(sp, pen_ready, n - RING + 1)
                settle(sp, passed_sp)
                sp.dma_start(ends[q][:, :], m.slots[:, bass.DynSlice(first, ET)]).then_inc(slots_in[q], 16)
                sp.dma_start(goes_on[q][:, :], m.same[:, bass.DynSlice(first + 1, ET)]
                             ).then_inc(slots_in[q], 16)
                reuse(sp, t_done, n - RING + 1)
                settle(sp, passed_sp)
                if isinstance(n, int) and n == 0:
                    rest = E - (EP - P)
                    assert 0 < rest < P
                    sp.wait_ge(e_clear, 1)
                    sp.dma_start(ein[0][:, 0, :], a["edge"][EP - ET:EP - P, :]).then_inc(e_loaded[0], 16)
                    sp.dma_start(ein[0][0:rest, 1, :], a["edge"][EP - P:E, :]).then_inc(e_loaded[0], 16)
                else:
                    sp.dma_start(ein[q][:, :, :], edge_rows(a["edge"], first)).then_inc(e_loaded[q], 16)

            pipeline(sp, UNITS, [(load, -1)])

        @block.gpsimd
        def _(pool):
            def gather(n, q):
                reuse(pool, t_done, n - RING + 1)
                nc.gpsimd.tensor_copy(stage[q][:, :], m.src_row[:, bass.DynSlice((UNITS - 1) * ER - n * ER, ER)]
                                      ).then_inc(staged, 1)
                pool.wait_ge(staged, n + 1)
                settle(pool, passed_pool)
                for j in range(ER):
                    nc.gpsimd.indirect_dma_start(
                        out=gs[q][:, j, :], out_offset=None, in_=m.x1_table,
                        in_offset=bass.IndirectOffsetOnAxis(ap=stage[q][:, j:j + 1], axis=0),
                    ).then_inc(gathered[q], 16)

            def root(n, q):
                pool.wait_ge(var_ready, n + 1)
                nc.gpsimd.tensor_tensor(rstd[q][:, :], vare[q][:, :], m.minus_half[:, 0:ER], ALU.pow
                                        ).then_inc(rstd_ready, 1)

            def scatter(n, q):
                reuse(pool, scattered[q], 32 * (use(n, q) - 1))
                settle(pool, passed_pool)
                nc.gpsimd.tensor_copy(to_stage[q][:, :],
                                      m.final_to[:, bass.DynSlice((UNITS - 1) * ER - n * ER, ER)]
                                      ).then_inc(to_staged, 1)
                pool.wait_ge(to_staged, n + 1)
                pool.wait_ge(fin_ready, n + 1)
                settle(pool, passed_pool)
                for j in range(ER):
                    nc.gpsimd.indirect_dma_start(
                        out=out, in_=fin[q][:, j, :], in_offset=None,
                        out_offset=bass.IndirectOffsetOnAxis(ap=to_stage[q][:, j:j + 1], axis=0),
                        bounds_check=N - 1, oob_is_err=False,
                    ).then_inc(scattered[q], 16)

            pipeline(pool, UNITS, [(scatter, 5), (gather, -2), (root, 3)])
            for q in range(RING):
                pool.wait_ge(scattered[q], 32 * uses(q))

        @block.tensor
        def _(pe):
            def spread_weights(n, q):
                pe.wait_ge(al_ready, n + 1)
                reuse(pe, va_ready, n)
                nc.tensor.matmul(spread[:, :], m.head_spread[:, :], al[q % 2][:, :], start=True, stop=True
                                 ).then_inc(spread_done, 1)

            def scores(n, q):
                pe.wait_ge(prod_ready, n + 1)
                pe.wait_ge(eT_ready, n + 1)
                pe.wait_ge(v_ready, n + 1)
                nc.tensor.matmul(vs[q % 2][0:H, ET:2 * ET], m.head_sum[:, :], prod[q % 2][:, :],
                                 start=True, stop=False)
                nc.tensor.matmul(vs[q % 2][0:H, ET:2 * ET], m.Wb8[:, :], eT[q % 2][:, :], start=False, stop=True
                                 ).then_inc(sc_done, 1)

            def turn(n, q):
                pe.wait_ge(gathered[q], 32 * use(n, q))
                pe.wait_ge(e_loaded[q], 16 * use(n, q) + (16 if q == 0 else 0))
                reuse(pe, eT_ready, n)
                for j in range(ER):
                    nc.tensor.transpose(turned[:, j * P:(j + 1) * P], gs[q][:, j, :], m.ident[:, :])
                for j in range(ER):
                    last = nc.tensor.transpose(turned[0:ED, ET + j * P:ET + (j + 1) * P], ein[q][:, j, :],
                                               m.ident[:, :])
                last.then_inc(t_done, 1)

            def project(n, q):
                pe.wait_ge(xd_ready, n + 1)
                reuse(pe, prod_ready, n - 1)
                nc.tensor.matmul(qk[q % 2][:, ET:2 * ET], m.Wk[:, :], xd[q][:, :], start=True, stop=True)
                pe.wait_ge(xs_ready, n + 1)
                nc.tensor.matmul(qk[q % 2][:, 0:ET], m.Wq[:, :], xs[q % 2][:, :], start=True, stop=True
                                 ).then_inc(qk_done, 1)
                reuse(pe, sc_ready, n - 1)
                nc.tensor.matmul(vs[q % 2][:, 0:ET], m.Wv[:, :], xd[q][:, :], start=True, stop=True
                                 ).then_inc(v_done, 1)

            def out_rows(n, q):
                pe.wait_ge(va_ready, n + 1)
                reuse(pe, u_ready, n - 1)
                for j in range(ER):
                    cut = slice(j * P, (j + 1) * P)
                    nc.tensor.matmul(rows[q % 2][:, j, :], xd[q][:, cut], m.ident[:, :], start=True, stop=False)
                    last = nc.tensor.matmul(rows[q % 2][:, j, :], va[q % 2][:, cut], m.Wo[:, :],
                                            start=False, stop=True)
                last.then_inc(o_done, 1)

            pipeline(pe, UNITS, [(spread_weights, 2), (turn, 0), (scores, 1), (project, 0), (out_rows, 2)])

        @block.scalar
        def _(act):
            def take_turned(n, q):
                act.wait_ge(t_done, n + 1)
                reuse(act, qk_done, n - 1)
                nc.scalar.activation(xs[q % 2][:, :], turned[:, 0:ET], ACT.Copy).then_inc(xs_ready, 1)
                reuse(act, sc_done, n - 1)
                nc.scalar.activation(eT[q % 2][:, :], turned[0:ED, ET:2 * ET], ACT.Copy).then_inc(eT_ready, 1)

            def take_projected(n, q):
                act.wait_ge(qk_done, n + 1)
                reuse(act, prod_ready, n - 1)
                nc.scalar.activation(qh[q % 2][:, :], qk[q % 2][:, 0:ET], ACT.Identity, bias=m.bqkv[:, 0:1]
                                     ).then_inc(q_ready, 1)
                act.wait_ge(v_done, n + 1)
                reuse(act, va_ready, n - RING + 1)
                nc.scalar.activation(v[q][:, :], vs[q % 2][:, 0:ET], ACT.Identity, bias=m.bqkv[:, 2:3]
                                     ).then_inc(v_ready, 1)

            def penalty(n, q):
                act.wait_ge(slots_in[q], 32 * use(n, q))
                act.wait_ge(init, 4)
                reuse(act, tmp_ready, n - 1)
                nc.scalar.activation(pen[q % 2][:, :], goes_on[q][0:H, :], ACT.Identity, bias=far[:, 0:1], scale=FAR
                                     ).then_inc(pen_ready, 1)

            def take_scores(n, q):
                act.wait_ge(sc_done, n + 1)
                reuse(act, arg_ready, n - 1)
                nc.scalar.activation(sc[q % 2][:, :], vs[q % 2][0:H, ET:2 * ET], ACT.Identity, bias=m.bb8[:, 0:1]
                                     ).then_inc(sc_ready, 1)

            def exps(n, q):
                act.wait_ge(arg_ready, n + 1)
                reuse(act, den_ready, n - 1)
                nc.scalar.activation(ex[q % 2][:, :, :], arg[q % 2][:, :, :], ACT.Exp).then_inc(ex_ready, 1)

            pipeline(act, UNITS, [(take_turned, 0), (take_scores, 1), (penalty, 0), (take_projected, 0), (exps, 1)])

        @block.vector
        def _(dve):
            nc.vector.memset(ein[0][:, :, :], 0.0).then_inc(e_clear, 1)
            nc.vector.memset(xd[RING - 1][:, :], 0.0).then_inc(init, 1)
            nc.vector.memset(mx[1][:, :], 0.0).then_inc(init, 1)
            nc.vector.memset(den[1][:, :], 1.0).then_inc(init, 1)
            nc.vector.memset(far[:, :], -FAR).then_inc(init, 1)
            dve.wait_ge(init, 4)

            def weights(n, q):
                dve.wait_ge(ex_ready, n + 1)
                reuse(dve, den_ready, n)
                nc.vector.tensor_tensor_scan(den[q % 2][:, ::-1], ex[q % 2][:, 0, ::-1], ex[q % 2][:, 1, ::-1],
                                             den[(q - 1) % 2][:, 0:1], ALU.mult, ALU.add).then_inc(den_ready, 1)
                dve.wait_ge(den_ready, n + 1)
                nc.vector.reciprocal(rden[q % 2][:, :], den[q % 2][:, :]).then_inc(rden_ready, 1)
                dve.wait_ge(rden_ready, n + 1)
                reuse(dve, spread_done, n - 1)
                nc.vector.tensor_tensor(al[q % 2][:, :], den[q % 2][:, :], rden[q % 2][:, :], ALU.mult
                                        ).then_inc(al_ready, 1)

            def products(n, q):
                dve.wait_ge(q_ready, n + 1)
                reuse(dve, sc_done, n - 1)
                nc.vector.scalar_tensor_tensor(out=prod[q % 2][:, :], in0=qk[q % 2][:, ET:2 * ET],
                                               scalar=m.bqkv[:, 1:2], in1=qh[q % 2][:, :],
                                               op0=ALU.add, op1=ALU.mult).then_inc(prod_ready, 1)

            def spread_features(n, q):
                dve.wait_ge(slots_in[q], 32 * use(n, q))
                reuse(dve, xd_ready, n)
                reuse(dve, o_done, n - RING + 1)
                nc.vector.tensor_tensor_scan(xd[q][:, ::-1], goes_on[q][:, ::-1], ends[q][:, ::-1],
                                             xd[q - 1][:, 0:1], ALU.mult, ALU.add).then_inc(xd_ready, 1)

            def weigh(n, q):
                dve.wait_ge(spread_done, n + 1)
                dve.wait_ge(v_ready, n + 1)
                reuse(dve, o_done, n - 1)
                nc.vector.tensor_tensor(va[q % 2][:, :], spread[:, :], v[q][:, :], ALU.mult
                                        ).then_inc(va_ready, 1)

            def maxima(n, q):
                reuse(dve, mx_ready, n)
                nc.vector.tensor_copy(mx[q % 2][:, ET:ET + 1], mx[(q - 1) % 2][:, 0:1]).then_inc(tail_ready, 1)
                dve.wait_ge(tail_ready, n + 1)
                dve.wait_ge(pen_ready, n + 1)
                dve.wait_ge(sc_ready, n + 1)
                nc.vector.tensor_tensor_scan(mx[q % 2][:, 0:ET][:, ::-1], pen[q % 2][:, ::-1], sc[q % 2][:, ::-1],
                                             mx[q % 2][:, ET:ET + 1], ALU.add, ALU.max).then_inc(mx_ready, 1)
                dve.wait_ge(mx_ready, n + 1)
                nc.vector.tensor_tensor(tmp[q % 2][:, :], mx[q % 2][:, 1:ET + 1], pen[q % 2][:, :], ALU.add
                                        ).then_inc(tmp_ready, 1)
                reuse(dve, ex_ready, n - 1)
                nc.vector.tensor_tensor(arg[q % 2][:, 1, :], sc[q % 2][:, :], mx[q % 2][:, 0:ET], ALU.subtract)
                dve.wait_ge(tmp_ready, n + 1)
                nc.vector.tensor_tensor(arg[q % 2][:, 0, :], tmp[q % 2][:, :], mx[q % 2][:, 0:ET], ALU.subtract
                                        ).then_inc(arg_ready, 1)

            def moments(n, q):
                dve.wait_ge(o_done, n + 1)
                reuse(dve, fin_ready, n - 1)
                nc.vector.tensor_tensor(u[q % 2][:, :, :], rows[q % 2][:, :, :], m.bo[:, 0:ER, :], ALU.add
                                        ).then_inc(u_ready, 1)
                dve.wait_ge(u_ready, n + 1)
                for j in range(ER):
                    nc.vector.bn_stats(stats[q][:, j, :], u[q % 2][:, j, :]).then_inc(stats_ready, 1)
                dve.wait_ge(stats_ready, ER * n + ER)
                settle(dve, passed_dve)
                for j in range(ER):
                    nc.vector.bn_aggr(mv[q][:, j, :], stats[q][:, j, :]).then_inc(mv_ready, 1)
                dve.wait_ge(mv_ready, ER * n + ER)
                reuse(dve, rstd_ready, n - RING + 1)
                nc.vector.tensor_scalar(vare[q][:, :], mv[q][:, :, 1], LN_EPS, None, ALU.add
                                        ).then_inc(var_ready, 1)

            def norm(n, q):
                dve.wait_ge(rstd_ready, n + 1)
                reuse(dve, scattered[q], 32 * (use(n, q) - 1))
                for j in range(ER):
                    last = nc.vector.tensor_scalar(fin[q][:, j, :], u[q % 2][:, j, :], mv[q][:, j, 0:1],
                                                   rstd[q][:, j:j + 1], ALU.subtract, ALU.mult)
                last.then_inc(fin_ready, 1)

            pipeline(dve, UNITS, [(weights, 2), (products, 1), (spread_features, 0), (weigh, 2), (maxima, 1),
                                  (moments, 3), (norm, 4)])


def program(nc, a, out):
    with ExitStack() as ctx:
        m = lay_out(nc, ctx)
        prepare(nc, m, a)
        nodes_and_first_layer(nc, m, a, out)
        edge_layer(nc, m, 1)
        edge_layer(nc, m, 2)
        attention(nc, m, a, out)


_INS = {"x": "x", "src": "src", "dst": "dst", "edge_attr_64": "edge",
        "L0_gnn_eps": "eps", "L0_gnn_W1": "W1", "L0_gnn_b1": "b1", "L0_gnn_W2": "W2", "L0_gnn_b2": "b2",
        "L0_gnn_Wf": "Wf", "L0_gnn_bf": "bf",
        "L1_gnn_Wq": "Wq", "L1_gnn_bq": "bq", "L1_gnn_Wk": "Wk", "L1_gnn_bk": "bk", "L1_gnn_Wv": "Wv",
        "L1_gnn_bv": "bv", "L1_gnn_Wb": "Wb", "L1_gnn_bb": "bb", "L1_gnn_Wo": "Wo", "L1_gnn_bo": "bo"}


def kernel(**inputs):
    import numpy as _np
    import concourse.bacc as _bacc
    from concourse import mybir as _mybir
    from concourse.bass_utils import run_bass_kernel_spmd as _run

    nc = _bacc.Bacc("TRN2", target_bir_lowering=False, num_devices=1)
    arrays, args = {}, {}
    for name, short in _INS.items():
        v = _np.ascontiguousarray(inputs[name])
        arrays[f"in_{name}_dram"] = v
        args[short] = nc.dram_tensor(f"in_{name}_dram", v.shape, _mybir.dt.from_np(v.dtype),
                                     kind="ExternalInput").ap()
    out = nc.dram_tensor("out_0_dram", (N, D), _mybir.dt.float32, kind="ExternalOutput").ap()
    program(nc, args, out)
    r = _run(nc, [arrays], core_ids=[0])
    return r.results[0]["out_0_dram"]
```

```python
from contextlib import ExitStack

import concourse.bass as bass
from concourse import mybir

F32 = mybir.dt.float32
I32 = mybir.dt.int32
U8 = mybir.dt.uint8
ALU = mybir.AluOpType
ACT = mybir.ActivationFunctionType

P = 128
N = 50000
E = 25000
D = 128
ED = 64
H = 8
HD = D // H
LAYERS = 3
NR = 4
NT = NR * P
ER = 2
ET = ER * P
STEPS = -(-E // (2 * ET))
EP = STEPS * 2 * ET
TILES = EP // P
CHUNK = 2 * ER
UNITS = 2 * STEPS
RING = 4
LAST_NODE = N - NT
ROWS = N + EP
PAD_DST = 1 << 20
EDGE_OF_LIST = PAD_DST + 1
SKIP = 1 << 21
LN_EPS = 1e-5
FAR = 1e30

assert UNITS % 2 == 0 and RING % 2 == 0
assert (2 * STEPS - 1) * NT < N <= 2 * STEPS * NT and E > EP - P




def use(n, q):
    return (n - q) // RING + 1


def uses(q):
    return len(range(q, UNITS, RING))


def settle(eng, passed):
    eng.sem_inc(passed, 1)


def reuse(eng, sem, count):
    if not isinstance(count, int) or count > 0:
        eng.wait_ge(sem, count)


class Memory:
    pass


def lay_out(nc, ctx):
    m = Memory()

    def sb(name, shape, dt=F32):
        return ctx.enter_context(nc.sbuf_tensor(name, shape, dt))

    m.y1_table = nc.dram_tensor("y1_table", (ROWS, D), F32).ap()
    m.y2_table = nc.dram_tensor("y2_table", (ROWS, D), F32).ap()
    m.x1_table = nc.dram_tensor("x1_table", (ROWS, D), F32).ap()
    m.skip_rows = nc.dram_tensor("skip_rows", (EP, D), F32).ap()
    m.row_of_node = nc.dram_tensor("row_of_node", (N, 1), I32).ap()
    m.dst_list = nc.dram_tensor("dst_list", (EP + 2, 1), I32).ap()
    m.src_list = nc.dram_tensor("src_list", (EP, 1), I32).ap()

    m.W1_0 = sb("W1_0", [P, P])
    m.W0f = sb("W0f", [P, P])
    m.G3 = sb("G3", [P, P])
    m.Wq = sb("Wq", [P, P])
    m.Wk = sb("Wk", [P, P])
    m.Wv = sb("Wv", [P, P])
    m.Wo = sb("Wo", [P, P])
    m.ident = sb("ident", [P, P])
    m.MG1 = sb("MG1", [P, 2 * P])
    m.MG2 = sb("MG2", [P, 2 * P])
    m.b1 = sb("b1", [P, LAYERS])
    m.scale = sb("scale", [P, LAYERS])
    m.c = sb("c", [P, 2])
    m.beta = sb("beta", [P, 2])
    m.eps = sb("eps", [P, 1])
    m.cf = sb("cf", [P, NR, P])
    m.bo = sb("bo", [P, NR, P])
    m.bqkv = sb("bqkv", [P, 3])
    m.Wb8 = sb("Wb8", [ED, H])
    m.bb8 = sb("bb8", [H, 1])
    m.head_sum = sb("head_sum", [P, H])
    m.minus_half = sb("minus_half", [P, NR])

    m.src_idx = sb("src_idx", [P, TILES], I32)
    m.dst_idx = sb("dst_idx", [P, TILES], I32)
    m.slot_to = sb("slot_to", [P, TILES], I32)
    m.final_to = sb("final_to", [P, TILES], I32)
    m.slot_row = sb("slot_row", [P, TILES], I32)
    m.src_row = sb("src_row", [P, TILES], I32)

    m.same = sb("same", [P, EP + 1], U8)
    m.slots = sb("slots", [P, EP])
    return m


def sem_maker(nc, ctx, phase, count=RING):
    made = []

    def give_back():
        nc.clear_and_free_semaphores(made)
        nc.all_engine_barrier()

    ctx.callback(give_back)

    def sem(name):
        made.append(nc.alloc_semaphore(f"{phase}_{name}"))
        return made[-1]

    def several(name):
        return [sem(f"{name}{q}") for q in range(count)]

    return sem, several



def prepare(nc, m, a):
    with ExitStack() as ctx:
        sem, pair = sem_maker(nc, ctx, "prep", 2)

        def sb(name, shape, dt=F32):
            return ctx.enter_context(nc.sbuf_tensor(name, shape, dt))

        def ps(name, shape):
            return ctx.enter_context(nc.psum_tensor(name, shape, F32))

        HI = P
        LO = TILES - P
        pads = EP - E
        fill = sb("fill", [1, 3 * P], I32)
        own = sb("own", [125, N // 125], I32)
        rows_i = sb("rows_i", [P, 4, 2, P], I32)
        rows_f = sb("rows_f", [P, 4, 2, P])
        cols = sb("cols", [P, 4, TILES])
        eq = sb("eq", [P, 2, TILES])
        W1 = sb("W1", [P, 2, P])
        W2 = sb("W2", [P, LAYERS, P])
        W2T = sb("W2T", [P, LAYERS, P])
        Wf = sb("Wf", [P, LAYERS + 1, P])
        WW = sb("WW", [P, 2, 2, P])
        b2 = sb("b2", [P, LAYERS])
        b2_wide = sb("b2_wide", [P, LAYERS, P])
        bf = sb("bf", [P, P])
        bo1 = sb("bo1", [P, P])
        pT = [ps(f"pT{q}", [P, 512]) for q in range(4)]
        pW = ps("pW", [P, LAYERS, P])
        pG = ps("pG", [P, 512])
        pC = ps("pC", [P, 512])

        filled = sem("filled")
        owned = sem("owned")
        lists = sem("lists")
        own_out = sem("own_out")
        index_in = sem("index_in")
        floats = sem("floats")
        turned = sem("turned")
        cols_ready = sem("cols_ready")
        eq_ready = sem("eq_ready")
        idx_done = sem("idx_done")
        w_in = sem("w_in")
        id_made = sem("id_made")
        iota_done = sem("iota_done")
        heads = sem("heads")
        w2_turned = sem("w2_turned")
        w2T_ready = sem("w2T_ready")
        wide_ready = sem("wide_ready")
        products = sem("products")
        prod_out = sem("prod_out")
        small = sem("small")
        consts = sem("consts")
        block = ctx.enter_context(nc.Block())

        @block.sync
        def _(sp):
            sp.wait_ge(filled, 3)
            sp.dma_start(m.dst_list[0:1, :], fill[0:1, 0:1]).then_inc(lists, 16)
            sp.dma_start(m.dst_list[1:1 + E, :].rearrange("(a b) c -> a (b c)", b=E // 40),
                         a["dst"].rearrange("(a b) -> a b", b=E // 40)).then_inc(lists, 16)
            sp.dma_start(m.dst_list[1 + E:1 + EP, :].rearrange("a c -> c a"),
                         fill[0:1, P:P + pads]).then_inc(lists, 16)
            sp.dma_start(m.dst_list[1 + EP:2 + EP, :], fill[0:1, 0:1]).then_inc(lists, 16)
            sp.dma_start(m.src_list[0:E, :].rearrange("(a b) c -> a (b c)", b=E // 40),
                         a["src"].rearrange("(a b) -> a b", b=E // 40)).then_inc(lists, 16)
            sp.dma_start(m.src_list[E:EP, :].rearrange("a c -> c a"),
                         fill[0:1, 2 * P:2 * P + pads]).then_inc(lists, 16)
            sp.wait_ge(owned, 1)
            sp.dma_start(m.row_of_node.rearrange("(p n) c -> p (n c)", p=125), own[:, :]).then_inc(own_out, 16)
            sp.wait_ge(lists, 96)
            for q, (lst, off) in enumerate(((m.dst_list, 1), (m.dst_list, 0), (m.dst_list, 2), (m.src_list, 0))):
                sp.dma_start(rows_i[:, q, 0, :],
                             lst[off:off + HI * P, :].rearrange("(t p) c -> t (p c)", p=P)).then_inc(index_in, 16)
                sp.dma_start(rows_i[0:LO, q, 1, :],
                             lst[off + HI * P:off + EP, :].rearrange("(t p) c -> t (p c)", p=P)
                             ).then_inc(index_in, 16)
            sp.wait_ge(own_out, 16)

        loads = [
            (m.W1_0[:, :], a["W1"][0]), (W1[:, 0, :], a["W1"][1]), (W1[:, 1, :], a["W1"][2]),
            (W2[:, :, :], a["W2"].rearrange("l k n -> k l n")),
            (Wf[:, :, :], a["Wf"].rearrange("(l k) n -> k l n", k=P)),
            (m.Wq[:, :], a["Wq"]), (m.Wk[:, :], a["Wk"]), (m.Wv[:, :], a["Wv"]), (m.Wo[:, :], a["Wo"]),
            (m.b1[:, :], a["b1"].rearrange("l k -> k l")),
            (b2[:, :], a["b2"].rearrange("l k -> k l")),
            (m.scale[:, :], a["eps"].rearrange("(o l) -> o l", o=1).to_broadcast([P, LAYERS])),
            (bf[:, :], a["bf"].rearrange("(o n) -> o n", o=1).to_broadcast([P, P])),
            (bo1[:, :], a["bo"].rearrange("(o n) -> o n", o=1).to_broadcast([P, P])),
            (m.bqkv[:, 0:1], a["bq"].rearrange("(n o) -> n o", o=1)),
            (m.bqkv[:, 1:2], a["bk"].rearrange("(n o) -> n o", o=1)),
            (m.bqkv[:, 2:3], a["bv"].rearrange("(n o) -> n o", o=1)),
            (m.Wb8[:, 0:1], a["Wb"]),
            (m.bb8[:, :], a["bb"].rearrange("(o n) -> o n", o=1).to_broadcast([H, 1])),
        ]
        W_DMAS = len(loads)

        @block.scalar
        def _(act):
            with nc.allow_non_contiguous_dma(reason="a few hundred bias values, once"):
                for dst, src in loads:
                    act.dma_start(dst, src).then_inc(w_in, 16)

        @block.gpsimd
        def _(pool):
            nc.gpsimd.iota(own[:, :], pattern=[[1, N // 125]], base=0, channel_multiplier=N // 125
                           ).then_inc(owned, 1)
            nc.gpsimd.iota(m.slot_row[:, :], pattern=[[P, TILES]], base=N, channel_multiplier=1
                           ).then_inc(iota_done, 1)
            nc.gpsimd.memset(m.ident[:, :], 0.0).then_inc(id_made, 1)
            pool.wait_ge(id_made, 1)
            nc.gpsimd.affine_select(out=m.ident[:, :], in_=m.ident[:, :], compare_op=ALU.not_equal, fill=1.0,
                                    base=0, pattern=[[-1, P]], channel_multiplier=1).then_inc(id_made, 1)
            nc.gpsimd.memset(m.head_sum[:, :], float(HD) ** -0.5).then_inc(heads, 1)
            pool.wait_ge(heads, 1)
            nc.gpsimd.affine_select(out=m.head_sum[:, :], in_=m.head_sum[:, :], compare_op=ALU.is_ge, fill=0.0,
                                    base=0, pattern=[[-HD, H]], channel_multiplier=1).then_inc(heads, 1)
            pool.wait_ge(heads, 2)
            nc.gpsimd.affine_select(out=m.head_sum[:, :], in_=m.head_sum[:, :], compare_op=ALU.is_ge, fill=0.0,
                                    base=HD - 1, pattern=[[HD, H]], channel_multiplier=-1).then_inc(heads, 1)

        @block.tensor
        def _(pe):
            pe.wait_ge(id_made, 2)
            pe.wait_ge(w_in, 16 * W_DMAS)
            for l in range(LAYERS):
                last = nc.tensor.transpose(pW[:, l, :], W2[:, l, :], m.ident[:, :])
            last.then_inc(w2_turned, 1)
            pe.wait_ge(floats, 4)
            for q in range(4):
                nc.tensor.transpose(pT[q][:, 0:P], rows_f[:, q, 0, :], m.ident[:, :])
                last = nc.tensor.transpose(pT[q][:, P:TILES], rows_f[0:LO, q, 1, :], m.ident[0:LO, 0:LO])
                last.then_inc(turned, 1)
            pe.wait_ge(w2T_ready, 1)
            pe.wait_ge(wide_ready, 3)
            nc.tensor.matmul(pG[:, 0:2 * P], W2T[:, 0, :], WW[:, 0].rearrange("p a b -> p (a b)"),
                             start=True, stop=True)
            last = nc.tensor.matmul(pG[:, 2 * P:4 * P], W2T[:, 1, :], WW[:, 1].rearrange("p a b -> p (a b)"),
                                    start=True, stop=True)
            last.then_inc(products, 1)
            pe.wait_ge(cols_ready, 4)
            nc.tensor.matmul(pT[0][:, 0:P], W2T[:, 2, :], Wf[:, 3, :], start=True, stop=True)
            nc.tensor.matmul(pT[2][:, 0:1], W1[:, 0, :], b2[:, 0:1], start=True, stop=True)
            nc.tensor.matmul(pT[2][:, 1:2], W1[:, 1, :], b2[:, 1:2], start=True, stop=True)
            for l in range(LAYERS):
                last = nc.tensor.matmul(pC[:, 0:P], b2_wide[:, l, :], Wf[:, l + 1, :],
                                        start=(l == 0), stop=(l == LAYERS - 1))
            last.then_inc(products, 1)

        @block.vector
        def _(dve):
            nc.vector.memset(fill[:, 0:P], EDGE_OF_LIST).then_inc(filled, 1)
            nc.vector.memset(fill[:, P:2 * P], PAD_DST).then_inc(filled, 1)
            nc.vector.memset(fill[:, 2 * P:3 * P], 0).then_inc(filled, 1)
            nc.vector.memset(m.minus_half[:, :], -0.5).then_inc(consts, 1)
            nc.vector.memset(m.eps[:, :], LN_EPS).then_inc(consts, 1)
            nc.vector.memset(m.same[:, EP:EP + 1], 0).then_inc(consts, 1)
            dve.wait_ge(w_in, 16 * W_DMAS)
            nc.vector.tensor_copy(WW[:, :, 0, :], W1[:, :, :]).then_inc(wide_ready, 1)
            nc.vector.tensor_copy(WW[:, :, 1, :], Wf[:, 1:3, :]).then_inc(wide_ready, 1)
            nc.vector.tensor_copy(b2_wide[:, :, :], b2[:, :].unsqueeze(2).to_broadcast([P, LAYERS, P])
                                  ).then_inc(wide_ready, 1)
            nc.vector.tensor_copy(m.bo[:, :, :], bo1[:, :].unsqueeze(1).to_broadcast([P, NR, P])
                                  ).then_inc(consts, 1)
            nc.vector.tensor_copy(m.Wb8[:, 1:H], m.Wb8[:, 0:1].to_broadcast([ED, H - 1])).then_inc(consts, 1)
            nc.vector.tensor_scalar(m.scale[:, :], m.scale[:, :], 1.0, None, ALU.add).then_inc(small, 1)
            dve.wait_ge(w2_turned, 1)
            nc.vector.tensor_copy(W2T[:, :, :], pW[:, :, :]).then_inc(w2T_ready, 1)
            dve.wait_ge(id_made, 2)
            nc.vector.tensor_tensor(m.W0f[:, :], Wf[:, 0, :], m.ident[:, :], ALU.add).then_inc(consts, 1)
            dve.wait_ge(index_in, 128)
            for q in range(4):
                nc.vector.tensor_copy(rows_f[:, q, 0, :], rows_i[:, q, 0, :])
                nc.vector.tensor_copy(rows_f[0:LO, q, 1, :], rows_i[0:LO, q, 1, :]).then_inc(floats, 1)
            for q in range(4):
                dve.wait_ge(turned, q + 1)
                nc.vector.tensor_copy(cols[:, q, :], pT[q][:, 0:TILES]).then_inc(cols_ready, 1)
            dve.wait_ge(cols_ready, 4)
            nc.vector.tensor_tensor(eq[:, 0, :], cols[:, 0, :], cols[:, 1, :], ALU.is_equal).then_inc(eq_ready, 1)
            nc.vector.tensor_tensor(eq[:, 1, :], cols[:, 0, :], cols[:, 2, :], ALU.is_equal).then_inc(eq_ready, 1)
            nc.vector.tensor_copy(m.src_idx[:, :], cols[:, 3, :]).then_inc(idx_done, 1)
            nc.vector.tensor_scalar(m.dst_idx[:, :], cols[:, 0, :], float(N - 1), None, ALU.min
                                    ).then_inc(idx_done, 1)
            dve.wait_ge(eq_ready, 2)
            nc.vector.scalar_tensor_tensor(out=m.final_to[:, :], in0=eq[:, 0, :], scalar=float(SKIP),
                                           in1=cols[:, 0, :], op0=ALU.mult, op1=ALU.add).then_inc(idx_done, 1)
            nc.vector.scalar_tensor_tensor(out=m.slot_to[:, :], in0=eq[:, 1, :], scalar=float(SKIP),
                                           in1=cols[:, 0, :], op0=ALU.mult, op1=ALU.add).then_inc(idx_done, 1)
            dve.wait_ge(products, 2)
            nc.vector.tensor_copy(m.MG1[:, :], pG[:, 0:2 * P]).then_inc(prod_out, 1)
            nc.vector.tensor_copy(m.MG2[:, :], pG[:, 2 * P:4 * P]).then_inc(prod_out, 1)
            nc.vector.tensor_copy(m.G3[:, :], pT[0][:, 0:P]).then_inc(prod_out, 1)
            nc.vector.tensor_copy(m.c[:, :], pT[2][:, 0:2]).then_inc(prod_out, 1)
            nc.vector.tensor_tensor(m.cf[:, 0, :], pC[:, 0:P], bf[:, :], ALU.add).then_inc(prod_out, 1)
            dve.wait_ge(prod_out, 5)
            dve.wait_ge(small, 1)
            nc.vector.tensor_copy(m.cf[:, 1:NR, :], m.cf[:, 0:1, :].to_broadcast([P, NR - 1, P])
                                  ).then_inc(consts, 1)
            nc.vector.tensor_tensor(m.beta[:, :], m.c[:, :], m.scale[:, 1:3], ALU.mult).then_inc(small, 1)
            dve.wait_ge(small, 2)
            nc.vector.tensor_tensor(m.beta[:, :], m.beta[:, :], m.b1[:, 1:3], ALU.add).then_inc(consts, 1)



def node_rows(t, start):
    return t[bass.DynSlice(start, NT), :].rearrange("(p j) d -> p (j d)", j=NR)


def edge_rows(t, start):
    return t[bass.DynSlice(start, ET), :].rearrange("(j p) d -> p j d", p=P)


def nodes_and_first_layer(nc, m, a, out):
    with ExitStack() as ctx:
        sem, pair = sem_maker(nc, ctx, "nodes", 2)

        def sb2(name, shape, dt=F32):
            return [ctx.enter_context(nc.sbuf_tensor(f"{name}{h}", shape, dt)) for h in range(2)]

        def sb(name, shape, dt=F32):
            return ctx.enter_context(nc.sbuf_tensor(name, shape, dt))

        def ps(name, shape):
            return ctx.enter_context(nc.psum_tensor(name, shape, F32))

        x_in = sb2("x_in", [P, NT])
        xT = sb2("xT", [P, NT])
        r1 = sb2("r1", [P, NT])
        r2 = sb2("r2", [P, NT])
        r3 = sb2("r3", [P, NT])
        y1s = sb2("y1s", [P, NT])
        y2s = sb2("y2s", [P, NT])
        u = sb2("u", [P, NR, P])
        x1s = sb2("x1s", [P, NR, P])
        fins = sb2("fins", [P, NR, P])
        stats = sb2("stats", [P, 2, NR, 6])
        mv = sb2("mv", [P, 2, NR, 2])
        std = sb2("std", [P, 2, NR])
        rstd = sb2("rstd", [P, 2, NR])
        dst_wide = sb("dst_wide", [P, 2 * ET + 1], I32)
        stage = sb("stage", [P, 2 * CHUNK], I32)
        to_put = sb2("to_put", [P, CHUNK], I32)
        put_rows = sb2("put_rows", [P, CHUNK], I32)
        to_find = sb2("to_find", [P, CHUNK], I32)
        found = sb2("found", [P, CHUNK], I32)
        gs = sb2("gs", [P, ER, P])
        gd = sb2("gd", [P, ER, P])
        xdT = sb2("xdT", [P, ET])
        agg = sb2("agg", [P, ET])
        z = sb2("z", [P, ET])
        re = sb2("re", [P, ET])
        rows_s = sb2("rows_s", [P, ER, 2 * P])

        chain = [ps(f"chain{h}", [P, NT]) for h in range(2)]
        yb = [ps(f"yb{h}", [P, NT]) for h in range(2)]
        ob = ps("ob", [P, NR, P])
        e0 = ps("e0", [P, 2, ET])
        e1 = ps("e1", [P, 2, ET])
        e2 = ps("e2", [P, ER, 2 * P])

        x_loaded = pair("x_loaded")
        t_done = pair("t_done")
        xT_ready = pair("xT_ready")
        l1_done = pair("l1_done")
        r1_ready = pair("r1_ready")
        l2_done = pair("l2_done")
        r2_ready = pair("r2_ready")
        l3_done = pair("l3_done")
        r3_ready = pair("r3_ready")
        y1_done = pair("y1_done")
        y1_out = pair("y1_out")
        y1_stored = pair("y1_stored")
        y2_done = pair("y2_done")
        y2_out = pair("y2_out")
        y2_stored = pair("y2_stored")
        o_done = pair("o_done")
        u_ready = pair("u_ready")
        stats_ready = [pair(f"stats_ready{n}") for n in range(2)]
        mv_ready = [pair(f"mv_ready{n}") for n in range(2)]
        std_ready = [pair(f"std_ready{n}") for n in range(2)]
        rstd_ready = [pair(f"rstd_ready{n}") for n in range(2)]
        x1_ready = pair("x1_ready")
        x1_stored = pair("x1_stored")
        v_ready = pair("v_ready")
        fin_ready = pair("fin_ready")
        fin_stored = pair("fin_stored")
        dst_loaded = sem("dst_loaded")
        mask_ready = sem("mask_ready")
        carry_ready = sem("carry_ready")
        staged = sem("staged")
        slots_staged = sem("slots_staged")
        slots_put = pair("slots_put")
        finds_staged = sem("finds_staged")
        rows_found = pair("rows_found")
        found_kept = sem("found_kept")
        gathered = pair("gathered")
        te_done = pair("te_done")
        xdT_ready = pair("xdT_ready")
        agg_ready = pair("agg_ready")
        z_ready = pair("z_ready")
        le_done = pair("le_done")
        re_ready = pair("re_ready")
        me_done = pair("me_done")
        slot_ready = pair("slot_ready")
        rows_done = pair("rows_done")
        rows_out = pair("rows_out")
        rows_stored = pair("rows_stored")
        passed_pool = sem("passed_pool")
        passed_dve = sem("passed_dve")
        block = ctx.enter_context(nc.Block())

        @block.sync
        def _(sp):
            def load(i, last=False):
                for h in range(2):
                    reuse(sp, t_done[h], i)
                    start = LAST_NODE if last and h == 1 else (2 * i + h) * NT
                    sp.dma_start(x_in[h][:, :], node_rows(a["x"], start)).then_inc(x_loaded[h], 16)
                reuse(sp, mask_ready, i)
                sp.dma_start(dst_wide[:, :],
                             m.dst_list[bass.DynSlice(i * 2 * ET, 2 * ET + 1), :].rearrange("n o -> o n")
                             .to_broadcast([P, 2 * ET + 1])).then_inc(dst_loaded, 16)

            def store(i, last=False):
                for h in range(2):
                    start = LAST_NODE if last and h == 1 else (2 * i + h) * NT
                    if last and h == 1:
                        sp.wait_ge(y1_stored[0], 16 * STEPS)
                        sp.wait_ge(y2_stored[0], 16 * STEPS)
                    sp.wait_ge(y1_out[h], i + 1)
                    sp.dma_start(node_rows(m.y1_table, start), y1s[h][:, :]).then_inc(y1_stored[h], 16)
                    sp.wait_ge(y2_out[h], i + 1)
                    sp.dma_start(node_rows(m.y2_table, start), y2s[h][:, :]).then_inc(y2_stored[h], 16)
                    sp.wait_ge(rows_out[h], i + 1)
                    edge = (2 * i + h) * ET
                    sp.dma_start(edge_rows(m.y1_table, edge + N), rows_s[h][:, :, 0:P]
                                 ).then_inc(rows_stored[h], 16)
                    sp.dma_start(edge_rows(m.skip_rows, edge), rows_s[h][:, :, P:2 * P]
                                 ).then_inc(rows_stored[h], 16)

            def store_norms(i, last=False):
                for h in range(2):
                    start = LAST_NODE if last and h == 1 else (2 * i + h) * NT
                    if last and h == 1:
                        sp.wait_ge(x1_stored[0], 16 * STEPS)
                        sp.wait_ge(fin_stored[0], 16 * STEPS)
                    sp.wait_ge(x1_ready[h], i + 1)
                    sp.dma_start(node_rows(m.x1_table, start), x1s[h].rearrange("p j d -> p (j d)")
                                 ).then_inc(x1_stored[h], 16)
                    sp.wait_ge(fin_ready[h], i + 1)
                    sp.dma_start(node_rows(out, start), fins[h].rearrange("p j d -> p (j d)")
                                 ).then_inc(fin_stored[h], 16)

            load(0)
            load(1)
            store(0)
            with sp.Fori(1, STEPS - 2) as i:
                load(i + 1)
                store_norms(i - 1)
                store(i)
            load(STEPS - 1, last=True)
            store_norms(STEPS - 3)
            store(STEPS - 2)
            store_norms(STEPS - 2)
            store(STEPS - 1, last=True)
            store_norms(STEPS - 1, last=True)
            for h in range(2):
                for s in (y1_stored, y2_stored, x1_stored, fin_stored):
                    sp.wait_ge(s[h], 16 * STEPS)
                sp.wait_ge(rows_stored[h], 32 * STEPS)

        @block.tensor
        def _(pe):
            def node_turn(i, h):
                pe.wait_ge(x_loaded[h], 16 * (i + 1))
                reuse(pe, r3_ready[h], i)
                for j in range(NR):
                    last = nc.tensor.transpose(chain[h][:, j * P:(j + 1) * P], x_in[h][:, j * P:(j + 1) * P],
                                               m.ident[:, :])
                last.then_inc(t_done[h], 1)

            def first_product(i, h):
                pe.wait_ge(xT_ready[h], i + 1)
                nc.tensor.matmul(chain[h][:, :], m.W1_0[:, :], xT[h][:, :], start=True, stop=True
                                 ).then_inc(l1_done[h], 1)

            def y_rows(i, h, ready, free, count, w, src, done):
                pe.wait_ge(ready[h], i + 1)
                reuse(pe, free[h], count)
                for j in range(NR):
                    last = nc.tensor.matmul(yb[h][:, j * P:(j + 1) * P], src[h][:, j * P:(j + 1) * P], w,
                                            start=True, stop=True)
                last.then_inc(done[h], 1)

            def y_turn(i, h, copied, y, done):
                pe.wait_ge(copied[h], i + 1)
                for j in range(NR):
                    last = nc.tensor.transpose(chain[h][:, j * P:(j + 1) * P], y[h][:, j * P:(j + 1) * P],
                                               m.ident[:, :])
                last.then_inc(done[h], 1)

            def out_rows(i, h):
                pe.wait_ge(r3_ready[h], i + 1)
                reuse(pe, u_ready[1 - h], i + h)
                for j in range(NR):
                    cut = slice(j * P, (j + 1) * P)
                    nc.tensor.matmul(ob[:, j, :], xT[h][:, cut], m.W0f[:, :], start=True, stop=False)
                    nc.tensor.matmul(ob[:, j, :], r1[h][:, cut], m.MG1[:, P:2 * P], start=False, stop=False)
                    nc.tensor.matmul(ob[:, j, :], r2[h][:, cut], m.MG2[:, P:2 * P], start=False, stop=False)
                    last = nc.tensor.matmul(ob[:, j, :], r3[h][:, cut], m.G3[:, :], start=False, stop=True)
                last.then_inc(o_done[h], 1)

            def edge_turn(i, h):
                pe.wait_ge(gathered[h], 64 * (i + 1))
                reuse(pe, agg_ready[1 - h], i + h)
                reuse(pe, xdT_ready[1 - h], i + h)
                for j in range(ER):
                    nc.tensor.transpose(e0[:, 0, j * P:(j + 1) * P], gs[h][:, j, :], m.ident[:, :])
                for j in range(ER):
                    last = nc.tensor.transpose(e0[:, 1, j * P:(j + 1) * P], gd[h][:, j, :], m.ident[:, :])
                last.then_inc(te_done[h], 1)

            def edge_layer(i, h):
                pe.wait_ge(z_ready[h], i + 1)
                reuse(pe, slot_ready[1 - h], i + h)
                nc.tensor.matmul(e1[:, 0, :], m.W1_0[:, :], z[h][:, :], start=True, stop=True
                                 ).then_inc(le_done[h], 1)

            def edge_rows_out(i, h):
                pe.wait_ge(re_ready[h], i + 1)
                nc.tensor.matmul(e1[:, 1, :], m.MG1[:, 0:P], re[h][:, :], start=True, stop=True
                                 ).then_inc(me_done[h], 1)
                pe.wait_ge(xdT_ready[h], i + 1)
                reuse(pe, rows_out[1 - h], i + h)
                for j in range(ER):
                    cut = slice(j * P, (j + 1) * P)
                    nc.tensor.matmul(e2[:, j, :], re[h][:, cut], m.MG1[:, :], start=True, stop=True,
                                     skip_group_check=True)
                    last = nc.tensor.matmul(e2[:, j, P:2 * P], xdT[h][:, cut], m.W0f[:, :], start=False,
                                            stop=True, skip_group_check=True)
                last.then_inc(rows_done[h], 1)

            def step(i, turn_next=True):
                first_product(i, 0)
                first_product(i, 1)
                edge_turn(i, 0)
                y_rows(i, 0, r1_ready, y2_out, i, m.MG1[:, 0:P], r1, y1_done)
                y_rows(i, 1, r1_ready, y2_out, i, m.MG1[:, 0:P], r1, y1_done)
                y_turn(i, 0, y1_out, y1s, l2_done)
                edge_turn(i, 1)
                y_turn(i, 1, y1_out, y1s, l2_done)
                edge_layer(i, 0)
                y_rows(i, 0, r2_ready, y1_out, i + 1, m.MG2[:, 0:P], r2, y2_done)
                y_rows(i, 1, r2_ready, y1_out, i + 1, m.MG2[:, 0:P], r2, y2_done)
                y_turn(i, 0, y2_out, y2s, l3_done)
                edge_rows_out(i, 0)
                y_turn(i, 1, y2_out, y2s, l3_done)
                edge_layer(i, 1)
                out_rows(i, 0)
                if turn_next:
                    node_turn(i + 1, 0)
                edge_rows_out(i, 1)
                if turn_next:
                    node_turn(i + 1, 1)
                out_rows(i, 1)

            node_turn(0, 0)
            node_turn(0, 1)
            step(0)
            with pe.Fori(1, STEPS - 1) as i:
                step(i)
            step(STEPS - 1, turn_next=False)

        @block.scalar
        def _(act):
            def turn_out(i, h):
                act.wait_ge(t_done[h], i + 1)
                reuse(act, o_done[h], i)
                nc.scalar.activation(xT[h][:, :], chain[h][:, :], ACT.Copy).then_inc(xT_ready[h], 1)

            def relu(i, h, done, scale, bias, dst, ready):
                act.wait_ge(done[h], i + 1)
                nc.scalar.activation(dst[h][:, :], chain[h][:, :], ACT.Relu, bias=bias, scale=scale
                                     ).then_inc(ready[h], 1)

            def y_out(i, h, done, stored, dst, copied):
                act.wait_ge(done[h], i + 1)
                reuse(act, stored[h], 16 * i)
                nc.scalar.activation(dst[h][:, :], yb[h][:, :], ACT.Copy).then_inc(copied[h], 1)

            def edge_turn_out(i, h):
                act.wait_ge(te_done[h], i + 1)
                reuse(act, rows_done[h], i)
                reuse(act, z_ready[h], i)
                nc.scalar.activation(xdT[h][:, :], e0[:, 1, :], ACT.Copy).then_inc(xdT_ready[h], 1)

            def edge_relu(i, h):
                act.wait_ge(le_done[h], i + 1)
                reuse(act, rows_done[h], i)
                nc.scalar.activation(re[h][:, :], e1[:, 0, :], ACT.Relu, bias=m.b1[:, 0:1]
                                     ).then_inc(re_ready[h], 1)

            def edge_out(i, h):
                act.wait_ge(me_done[h], i + 1)
                nc.scalar.activation(m.slots[:, bass.DynSlice((2 * i + h) * ET, ET)], e1[:, 1, :],
                                     ACT.Identity, bias=m.c[:, 0:1]).then_inc(slot_ready[h], 1)
                act.wait_ge(rows_done[h], i + 1)
                reuse(act, rows_stored[h], 32 * i)
                nc.scalar.activation(rows_s[h][:, :, :], e2[:, :, :], ACT.Copy).then_inc(rows_out[h], 1)

            def root(i, h, n):
                act.wait_ge(mv_ready[n][h], NR * (i + 1))
                reuse(act, rstd_ready[n][h], i)
                nc.scalar.activation(std[h][:, n, :], mv[h][:, n, :, 1], ACT.Sqrt, bias=m.eps[:, 0:1]
                                     ).then_inc(std_ready[n][h], 1)

            def step(i, norms=True, turn_next=True):
                relu(i, 0, l1_done, m.scale[:, 0:1], m.b1[:, 0:1], r1, r1_ready)
                relu(i, 1, l1_done, m.scale[:, 0:1], m.b1[:, 0:1], r1, r1_ready)
                if norms:
                    root(i - 1, 0, 0)
                    root(i - 1, 1, 0)
                edge_turn_out(i, 0)
                y_out(i, 0, y1_done, y1_stored, y1s, y1_out)
                y_out(i, 1, y1_done, y1_stored, y1s, y1_out)
                relu(i, 0, l2_done, m.scale[:, 1:2], m.beta[:, 0:1], r2, r2_ready)
                edge_turn_out(i, 1)
                relu(i, 1, l2_done, m.scale[:, 1:2], m.beta[:, 0:1], r2, r2_ready)
                edge_relu(i, 0)
                y_out(i, 0, y2_done, y2_stored, y2s, y2_out)
                y_out(i, 1, y2_done, y2_stored, y2s, y2_out)
                relu(i, 0, l3_done, m.scale[:, 2:3], m.beta[:, 1:2], r3, r3_ready)
                edge_out(i, 0)
                if norms:
                    root(i - 1, 0, 1)
                    root(i - 1, 1, 1)
                relu(i, 1, l3_done, m.scale[:, 2:3], m.beta[:, 1:2], r3, r3_ready)
                edge_relu(i, 1)
                if turn_next:
                    turn_out(i + 1, 0)
                edge_out(i, 1)
                if turn_next:
                    turn_out(i + 1, 1)

            turn_out(0, 0)
            turn_out(0, 1)
            step(0, norms=False)
            step(1)
            with act.Fori(2, STEPS - 1) as i:
                step(i)
            step(STEPS - 1, turn_next=False)
            for n in range(2):
                for h in range(2):
                    root(STEPS - 1, h, n)

        @block.vector
        def _(dve):
            nc.vector.memset(agg[1][:, :], 0.0).then_inc(carry_ready, 1)
            dve.wait_ge(carry_ready, 1)

            def mask(i):
                dve.wait_ge(dst_loaded, 16 * (i + 1))
                nc.vector.tensor_tensor(m.same[:, bass.DynSlice(i * 2 * ET, 2 * ET)], dst_wide[:, 1:2 * ET + 1],
                                        dst_wide[:, 0:2 * ET], ALU.is_equal).then_inc(mask_ready, 1)
                dve.wait_ge(mask_ready, i + 1)

            def sums(i, h):
                dve.wait_ge(xdT_ready[h], i + 1)
                reuse(dve, agg_ready[1 - h], i + h)
                nc.vector.tensor_tensor_scan(agg[h][:, :], m.same[:, bass.DynSlice((2 * i + h) * ET, ET)],
                                             e0[:, 0, :], agg[1 - h][:, ET - 1:ET], ALU.mult, ALU.add
                                             ).then_inc(agg_ready[h], 1)
                dve.wait_ge(agg_ready[h], i + 1)
                reuse(dve, le_done[h], i)
                nc.vector.scalar_tensor_tensor(out=z[h][:, :], in0=xdT[h][:, :], scalar=m.scale[:, 0:1],
                                               in1=agg[h][:, :], op0=ALU.mult, op1=ALU.add
                                               ).then_inc(z_ready[h], 1)

            def moments(i, h, n, src, src_ready):
                dve.wait_ge(src_ready[h], i + 1)
                for j in range(NR):
                    nc.vector.bn_stats(stats[h][:, n, j, :], src[h][:, j, :]).then_inc(stats_ready[n][h], 1)
                dve.wait_ge(stats_ready[n][h], NR * (i + 1))
                settle(dve, passed_dve)
                for j in range(NR):
                    nc.vector.bn_aggr(mv[h][:, n, j, :], stats[h][:, n, j, :]).then_inc(mv_ready[n][h], 1)

            def inverse(i, h, n):
                dve.wait_ge(std_ready[n][h], i + 1)
                nc.vector.reciprocal(rstd[h][:, n, :], std[h][:, n, :]).then_inc(rstd_ready[n][h], 1)

            def normed(i, h, n, dst, stored, ready):
                dve.wait_ge(rstd_ready[n][h], i + 1)
                reuse(dve, stored[h], 16 * i)
                for j in range(NR):
                    last = nc.vector.tensor_scalar(dst[h][:, j, :], u[h][:, j, :], mv[h][:, n, j, 0:1],
                                                   rstd[h][:, n, j:j + 1], ALU.subtract, ALU.mult)
                last.then_inc(ready[h], 1)

            def first_norm(i, h):
                inverse(i, h, 0)
                normed(i, h, 0, x1s, x1_stored, x1_ready)

            def add_bias(i):
                for h in range(2):
                    dve.wait_ge(x1_ready[h], i + 1)
                    nc.vector.tensor_tensor(u[h][:, :, :], x1s[h][:, :, :], m.bo[:, :, :], ALU.add
                                            ).then_inc(v_ready[h], 1)
                    moments(i, h, 1, u, v_ready)

            def second_norm(i):
                for h in range(2):
                    inverse(i, h, 1)
                for h in range(2):
                    normed(i, h, 1, fins, fin_stored, fin_ready)

            def add_constant(i, h):
                dve.wait_ge(o_done[h], i + 1)
                reuse(dve, fin_ready[h], i)
                nc.vector.tensor_tensor(u[h][:, :, :], ob[:, :, :], m.cf[:, :, :], ALU.add
                                        ).then_inc(u_ready[h], 1)
                moments(i, h, 0, u, u_ready)

            def step(i, norms=True):
                mask(i)
                sums(i, 0)
                if norms:
                    first_norm(i - 1, 0)
                    first_norm(i - 1, 1)
                sums(i, 1)
                if norms:
                    add_bias(i - 1)
                    second_norm(i - 1)
                add_constant(i, 0)
                add_constant(i, 1)

            step(0, norms=False)
            step(1)
            with dve.Fori(2, STEPS) as i:
                step(i)
            first_norm(STEPS - 1, 0)
            first_norm(STEPS - 1, 1)
            add_bias(STEPS - 1)
            second_norm(STEPS - 1)

        @block.gpsimd
        def _(pool):
            def gather(i):
                for h in range(2):
                    reuse(pool, te_done[h], i)
                nc.gpsimd.tensor_copy(stage[:, 0:CHUNK], m.src_idx[:, bass.DynSlice(i * CHUNK, CHUNK)]
                                      ).then_inc(staged, 1)
                nc.gpsimd.tensor_copy(stage[:, CHUNK:2 * CHUNK], m.dst_idx[:, bass.DynSlice(i * CHUNK, CHUNK)]
                                      ).then_inc(staged, 1)
                pool.wait_ge(staged, 2 * (i + 1))
                settle(pool, passed_pool)
                for h in range(2):
                    for j in range(ER):
                        for c, g in ((0, gs), (CHUNK, gd)):
                            col = c + h * ER + j
                            nc.gpsimd.indirect_dma_start(
                                out=g[h][:, j, :], out_offset=None, in_=a["x"],
                                in_offset=bass.IndirectOffsetOnAxis(ap=stage[:, col:col + 1], axis=0),
                            ).then_inc(gathered[h], 16)

            def put_slots(n, q):
                reuse(pool, slots_put[q], 16 * CHUNK * ((n - q) // 2))
                nc.gpsimd.tensor_copy(to_put[q][:, :], m.slot_to[:, bass.DynSlice(n * CHUNK, CHUNK)]
                                      ).then_inc(slots_staged, 1)
                nc.gpsimd.tensor_copy(put_rows[q][:, :], m.slot_row[:, bass.DynSlice(n * CHUNK, CHUNK)]
                                      ).then_inc(slots_staged, 1)
                pool.wait_ge(slots_staged, 2 * n + 2)
                settle(pool, passed_pool)
                for j in range(CHUNK):
                    nc.gpsimd.indirect_dma_start(
                        out=m.row_of_node, in_=put_rows[q][:, j:j + 1], in_offset=None,
                        out_offset=bass.IndirectOffsetOnAxis(ap=to_put[q][:, j:j + 1], axis=0),
                        bounds_check=N - 1, oob_is_err=False,
                    ).then_inc(slots_put[q], 16)

            def find_rows(n, q):
                reuse(pool, found_kept, n - 1)
                nc.gpsimd.tensor_copy(to_find[q][:, :], m.src_idx[:, bass.DynSlice(n * CHUNK, CHUNK)]
                                      ).then_inc(finds_staged, 1)
                pool.wait_ge(finds_staged, n + 1)
                settle(pool, passed_pool)
                for j in range(CHUNK):
                    nc.gpsimd.indirect_dma_start(
                        out=found[q][:, j:j + 1], out_offset=None, in_=m.row_of_node,
                        in_offset=bass.IndirectOffsetOnAxis(ap=to_find[q][:, j:j + 1], axis=0),
                    ).then_inc(rows_found[q], 16)

            def keep_rows(n, q):
                pool.wait_ge(rows_found[q], 16 * CHUNK * ((n - q) // 2 + 1))
                nc.gpsimd.tensor_copy(m.src_row[:, bass.DynSlice(n * CHUNK, CHUNK)], found[q][:, :]
                                      ).then_inc(found_kept, 1)

            half = STEPS // 2

            def putting_step(i):
                gather(i + 1)
                put_slots(2 * i, 0)
                put_slots(2 * i + 1, 1)

            def finding_step(i, n, first=False):
                gather(i + 1)
                find_rows(n, 0)
                if not first:
                    keep_rows(n - 1, 1)
                find_rows(n + 1, 1)
                keep_rows(n, 0)

            gather(0)
            putting_step(0)
            with pool.Fori(1, half) as i:
                putting_step(i)
            put_slots(2 * half, 0)
            pool.wait_ge(slots_put[0], 16 * CHUNK * (half + 1))
            pool.wait_ge(slots_put[1], 16 * CHUNK * half)
            finding_step(half, 0, first=True)
            with pool.Fori(half + 1, STEPS - 1) as i:
                finding_step(i, 2 * i - 2 * half)
            find_rows(2 * half, 0)
            keep_rows(2 * half - 1, 1)
            keep_rows(2 * half, 0)



def pipeline(eng, units, stages):
    lags = [lag for _, lag in stages]
    first = -(-(max(lags) + RING) // RING)
    last = (units + min(lags)) // RING

    def single(s):
        for stage, lag in stages:
            if 0 <= s - lag < units:
                stage(s - lag, (s - lag) % RING)

    for s in range(min(0, min(lags)), RING * first):
        single(s)
    with eng.Fori(first, last) as i:
        for r in range(RING):
            for stage, lag in stages:
                stage(RING * i + r - lag, (r - lag) % RING)
    for s in range(RING * last, units + max(lags)):
        single(s)


def edge_layer(nc, m, l):
    final = l == 2
    src_table = m.y2_table if final else m.y1_table
    with ExitStack() as ctx:
        sem, ring_of_sems = sem_maker(nc, ctx, f"layer{l}")

        def ring(name, shape, dt=F32):
            return [ctx.enter_context(nc.sbuf_tensor(f"{name}_l{l}{q}", shape, dt)) for q in range(RING)]

        def banks(name, shape):
            return [ctx.enter_context(nc.psum_tensor(f"{name}_l{l}{q}", shape, F32)) for q in range(2)]

        stage = [ctx.enter_context(nc.sbuf_tensor(f"stage_l{l}{p}", [P, 2, ER], I32)) for p in range(RING // 2)]
        gs = ring("gs", [P, ER, P])
        msg = ring("msg", [P, ET])
        agg = ring("agg", [P, ET])
        pre = ring("pre", [P, ET])
        re = ring("re", [P, ET])
        skip_in = ring("skip_in", [P, ER, P])
        y_out = ring("y_out", [P, ER, P])
        s_out = ring("s_out", [P, ER, P])
        stats = ring("stats", [P, ER, 6])
        mv = ring("mv", [P, ER, 2])
        std = ring("std", [P, ER])
        rstd = ring("rstd", [P, ER])
        shift = ring("shift", [P, ER])
        pt = banks("pt", [P, ET])
        pm = banks("pm", [P, 512])
        pr = banks("pr", [P, ER, 2 * P])

        gathered = ring_of_sems("gathered")
        skip_loaded = ring_of_sems("skip_loaded")
        stored = ring_of_sems("stored")
        staged = sem("staged")
        t_done = sem("t_done")
        msg_ready = sem("msg_ready")
        agg_ready = sem("agg_ready")
        pre_ready = sem("pre_ready")
        re_ready = sem("re_ready")
        m_done = sem("m_done")
        slot_ready = sem("slot_ready")
        rows_done = sem("rows_done")
        y_ready = sem("y_ready")
        sum_ready = sem("sum_ready")
        part_ready = sem("part_ready")
        shift_ready = sem("shift_ready")
        stats_ready = sem("stats_ready")
        mv_ready = sem("mv_ready")
        std_ready = sem("std_ready")
        rstd_ready = sem("rstd_ready")
        x1_ready = sem("x1_ready")
        x1_turned = sem("x1_turned")
        carry_ready = sem("carry_ready")
        passed_pool = sem("passed_pool")
        passed_dve = sem("passed_dve")
        block = ctx.enter_context(nc.Block())

        @block.sync
        def _(sp):
            def load_skip(n, q):
                reuse(sp, sum_ready, n - RING + 1)
                sp.dma_start(skip_in[q][:, :, :], edge_rows(m.skip_rows, n * ET)).then_inc(skip_loaded[q], 16)

            def store(n, q):
                if final:
                    sp.wait_ge(x1_ready, n + 1)
                    sp.dma_start(edge_rows(m.x1_table, n * ET + N), s_out[q][:, :, :]).then_inc(stored[q], 16)
                else:
                    sp.wait_ge(y_ready, n + 1)
                    sp.dma_start(edge_rows(m.y2_table, n * ET + N), y_out[q][:, :, :]).then_inc(stored[q], 16)
                    sp.wait_ge(sum_ready, n + 1)
                    sp.dma_start(edge_rows(m.skip_rows, n * ET), s_out[q][:, :, :]).then_inc(stored[q], 16)

            pipeline(sp, UNITS, [(load_skip, -1), (store, 5 if final else 4)])
            for q in range(RING):
                sp.wait_ge(stored[q], (16 if final else 32) * uses(q))

        @block.gpsimd
        def _(pool):
            def gather(n, q):
                reuse(pool, t_done, n - RING + 1)
                if q % 2 == 0:
                    reuse(pool, gathered[q + 1], 32 * (use(n, q) - 1))
                    settle(pool, passed_pool)
                    nc.gpsimd.tensor_copy(stage[q // 2][:, :, :],
                                          m.src_row[:, bass.DynSlice(n * ER, 2 * ER)]
                                          .rearrange("p (u j) -> p u j", u=2)).then_inc(staged, 2)
                    pool.wait_ge(staged, n + 2)
                settle(pool, passed_pool)
                for j in range(ER):
                    nc.gpsimd.indirect_dma_start(
                        out=gs[q][:, j, :], out_offset=None, in_=src_table,
                        in_offset=bass.IndirectOffsetOnAxis(ap=stage[q // 2][:, q % 2, j:j + 1], axis=0),
                    ).then_inc(gathered[q], 16)

            pipeline(pool, UNITS, [(gather, 0)])

        @block.tensor
        def _(pe):
            def turn(n, q):
                pe.wait_ge(gathered[q], 32 * use(n, q))
                reuse(pe, msg_ready, n - 1)
                for j in range(ER):
                    last = nc.tensor.transpose(pt[q % 2][:, j * P:(j + 1) * P], gs[q][:, j, :], m.ident[:, :])
                last.then_inc(t_done, 1)

            def products(n, q):
                pe.wait_ge(re_ready, n + 1)
                reuse(pe, sum_ready, n - 1)
                if final:
                    for j in range(ER):
                        last = nc.tensor.matmul(pr[q % 2][:, j, 0:P], re[q][:, j * P:(j + 1) * P], m.G3[:, :],
                                                start=True, stop=True)
                    last.then_inc(rows_done, 1)
                    return
                reuse(pe, slot_ready, n - 1)
                nc.tensor.matmul(pm[q % 2][:, 0:ET], m.MG2[:, 0:P], re[q][:, :], start=True, stop=True
                                 ).then_inc(m_done, 1)
                for j in range(ER):
                    last = nc.tensor.matmul(pr[q % 2][:, j, :], re[q][:, j * P:(j + 1) * P], m.MG2[:, :],
                                            start=True, stop=True)
                last.then_inc(rows_done, 1)

            def turn_back(n, q):
                pe.wait_ge(x1_ready, n + 1)
                reuse(pe, slot_ready, n - 1)
                for j in range(ER):
                    last = nc.tensor.transpose(pm[q % 2][:, j * P:(j + 1) * P], s_out[q][:, j, :], m.ident[:, :])
                last.then_inc(x1_turned, 1)

            pipeline(pe, UNITS, [(turn, 0), (products, 2)] + [(turn_back, 5)] * final)

        @block.scalar
        def _(act):
            def take_turned(n, q):
                act.wait_ge(t_done, n + 1)
                reuse(act, agg_ready, n - RING + 1)
                nc.scalar.activation(msg[q][:, :], pt[q % 2][:, :], ACT.Identity, bias=m.c[:, l - 1:l]
                                     ).then_inc(msg_ready, 1)

            def relu(n, q):
                act.wait_ge(pre_ready, n + 1)
                reuse(act, rows_done, n - RING + 1)
                nc.scalar.activation(re[q][:, :], pre[q][:, :], ACT.Relu, bias=m.b1[:, l:l + 1]
                                     ).then_inc(re_ready, 1)

            def take(n, q):
                act.wait_ge(m_done, n + 1)
                nc.scalar.activation(m.slots[:, bass.DynSlice(n * ET, ET)], pm[q % 2][:, 0:ET],
                                     ACT.Identity, bias=m.c[:, 1:2]).then_inc(slot_ready, 1)
                act.wait_ge(rows_done, n + 1)
                reuse(act, stored[q], 32 * (use(n, q) - 1))
                nc.scalar.activation(y_out[q][:, :, :], pr[q % 2][:, :, 0:P], ACT.Copy).then_inc(y_ready, 1)

            def root(n, q):
                act.wait_ge(mv_ready, ER * n + ER)
                reuse(act, rstd_ready, n - RING + 1)
                nc.scalar.activation(std[q][:, :], mv[q][:, :, 1], ACT.Sqrt, bias=m.eps[:, 0:1]
                                     ).then_inc(std_ready, 1)

            def norm(n, q):
                act.wait_ge(shift_ready, n + 1)
                reuse(act, stored[q], 16 * (use(n, q) - 1))
                for j in range(ER):
                    last = nc.scalar.activation(s_out[q][:, j, :], y_out[q][:, j, :], ACT.Identity,
                                                bias=shift[q][:, j:j + 1], scale=rstd[q][:, j:j + 1])
                last.then_inc(x1_ready, 1)

            pipeline(act, UNITS, [(take_turned, 0)] + ([(relu, 1), (root, 3), (norm, 4)] if final else
                                                       [(relu, 1), (take, 2)]))

        @block.vector
        def _(dve):
            nc.vector.memset(agg[RING - 1][:, :], 0.0).then_inc(carry_ready, 1)
            dve.wait_ge(carry_ready, 1)

            def sums(n, q):
                dve.wait_ge(msg_ready, n + 1)
                reuse(dve, agg_ready, n)
                nc.vector.tensor_tensor_scan(agg[q][:, :], m.same[:, bass.DynSlice(n * ET, ET)],
                                             msg[q][:, :], agg[q - 1][:, ET - 1:ET], ALU.mult, ALU.add
                                             ).then_inc(agg_ready, 1)

            def add_own(n, q):
                dve.wait_ge(agg_ready, n + 1)
                reuse(dve, re_ready, n - RING + 1)
                nc.vector.scalar_tensor_tensor(out=pre[q][:, :], in0=m.slots[:, bass.DynSlice(n * ET, ET)],
                                               scalar=m.scale[:, l:l + 1], in1=agg[q][:, :],
                                               op0=ALU.mult, op1=ALU.add).then_inc(pre_ready, 1)

            def add_skip(n, q):
                dve.wait_ge(rows_done, n + 1)
                dve.wait_ge(skip_loaded[q], 16 * use(n, q))
                if final:
                    reuse(dve, x1_ready, n - RING + 1)
                    nc.vector.tensor_tensor(y_out[q][:, :, :], pr[q % 2][:, :, 0:P], skip_in[q][:, :, :], ALU.add
                                            ).then_inc(sum_ready, 1)
                    return
                dve.wait_ge(y_ready, n + 1)
                reuse(dve, stored[q], 32 * (use(n, q) - 1))
                nc.vector.tensor_tensor(s_out[q][:, :, :], pr[q % 2][:, :, P:2 * P], skip_in[q][:, :, :],
                                        ALU.add).then_inc(part_ready, 1)

            def add_constant(n, q):
                dve.wait_ge(part_ready, n + 1)
                nc.vector.tensor_tensor(s_out[q][:, :, :], s_out[q][:, :, :], m.cf[:, 0:ER, :], ALU.add
                                        ).then_inc(sum_ready, 1)

            def moments(n, q):
                dve.wait_ge(sum_ready, n + 1)
                for j in range(ER):
                    nc.vector.bn_stats(stats[q][:, j, :], y_out[q][:, j, :]).then_inc(stats_ready, 1)

            def gather_moments(n, q):
                dve.wait_ge(stats_ready, ER * n + ER)
                settle(dve, passed_dve)
                for j in range(ER):
                    nc.vector.bn_aggr(mv[q][:, j, :], stats[q][:, j, :]).then_inc(mv_ready, 1)

            def inverse(n, q):
                dve.wait_ge(std_ready, n + 1)
                reuse(dve, x1_ready, n - RING + 1)
                nc.vector.reciprocal(rstd[q][:, :], std[q][:, :]).then_inc(rstd_ready, 1)

            def shifts(n, q):
                dve.wait_ge(rstd_ready, n + 1)
                nc.vector.scalar_tensor_tensor(out=shift[q][:, :], in0=mv[q][:, :, 0], scalar=-1.0,
                                               in1=rstd[q][:, :], op0=ALU.mult, op1=ALU.mult
                                               ).then_inc(shift_ready, 1)

            def keep_ends(n, q):
                dve.wait_ge(x1_turned, n + 1)
                nc.vector.scalar_tensor_tensor(out=m.slots[:, bass.DynSlice(n * ET, ET)],
                                               in0=m.same[:, bass.DynSlice(n * ET + 1, ET)], scalar=0.0,
                                               in1=pm[q % 2][:, 0:ET], op0=ALU.is_equal, op1=ALU.mult
                                               ).then_inc(slot_ready, 1)

            if final:
                pipeline(dve, UNITS, [(sums, 1), (add_skip, 3), (add_own, 1), (moments, 3), (inverse, 4),
                                      (gather_moments, 3), (shifts, 4), (keep_ends, 6)])
            else:
                pipeline(dve, UNITS, [(sums, 1), (add_skip, 3), (add_own, 1), (add_constant, 3)])



def attention(nc, m, a, out):
    with ExitStack() as ctx:
        sem, ring_of_sems = sem_maker(nc, ctx, "attn")

        def ring(name, shape, dt=F32, size=RING):
            return [ctx.enter_context(nc.sbuf_tensor(f"{name}_at{q}", shape, dt)) for q in range(size)]

        def bank(name, shape):
            return ctx.enter_context(nc.psum_tensor(f"{name}_at", shape, F32))

        stage = ring("stage", [P, 2, ER], I32, size=RING // 2)
        to_stage = ring("to_stage", [P, 2, ER], I32, size=RING // 2)
        gs = ring("gs", [P, ER, P])
        ein = ring("ein", [P, ER, ED])
        ends = ring("ends", [P, ET])
        goes_on = ring("goes_on", [P, ET], U8)
        xs = ring("xs", [P, ET], size=2)
        eT = ring("eT", [ED, ET], size=2)
        xd = ring("xd", [P, ET])
        qh = ring("qh", [P, ET], size=2)
        v = ring("v", [P, ET])
        prod = ring("prod", [P, ET], size=2)
        sc = ring("sc", [H, ET], size=2)
        pen = ring("pen", [H, ET], size=2)
        mx = ring("mx", [H, ET + 1], size=2)
        tmp = ring("tmp", [H, ET], size=2)
        arg = ring("arg", [H, 2, ET], size=2)
        ex = ring("ex", [H, 2, ET], size=2)
        den = ring("den", [H, ET], size=2)
        rden = ring("rden", [P, ER, H], size=2)
        al = ring("al", [P, ER, P], size=2)
        va = ring("va", [P, ET], size=2)
        u = ring("u", [P, ER, P], size=2)
        fin = ring("fin", [P, ER, P])
        stats = ring("stats", [P, ER, 6])
        mv = ring("mv", [P, ER, 2])
        vare = ring("vare", [P, ER])
        rstd = ring("rstd", [P, ER])
        shift = ring("shift", [P, ER])
        far = ctx.enter_context(nc.sbuf_tensor("far", [H, 1], F32))
        turned = bank("turned", [P, 512])
        qk = [bank(f"qk{q}", [P, 512]) for q in range(2)]
        vs = [bank(f"vs{q}", [P, 512]) for q in range(2)]
        spread = bank("spread", [P, 512])
        rows = [bank(f"rows{q}", [P, ER, P]) for q in range(2)]

        gathered = ring_of_sems("gathered")
        e_loaded = ring_of_sems("e_loaded")
        slots_in = ring_of_sems("slots_in")
        scattered = ring_of_sems("scattered")
        staged = sem("staged")
        to_staged = sem("to_staged")
        init = sem("init")
        e_clear = sem("e_clear")
        t_done = sem("t_done")
        xs_ready = sem("xs_ready")
        eT_ready = sem("eT_ready")
        xd_ready = sem("xd_ready")
        qk_done = sem("qk_done")
        v_done = sem("v_done")
        q_ready = sem("q_ready")
        v_ready = sem("v_ready")
        prod_ready = sem("prod_ready")
        sc_done = sem("sc_done")
        sc_ready = sem("sc_ready")
        pen_ready = sem("pen_ready")
        tail_ready = sem("tail_ready")
        mx_ready = sem("mx_ready")
        tmp_ready = sem("tmp_ready")
        arg_ready = sem("arg_ready")
        ex_ready = sem("ex_ready")
        den_ready = sem("den_ready")
        den_turned = sem("den_turned")
        rden_ready = sem("rden_ready")
        al_ready = sem("al_ready")
        spread_done = sem("spread_done")
        va_ready = sem("va_ready")
        o_done = sem("o_done")
        u_ready = sem("u_ready")
        stats_ready = sem("stats_ready")
        mv_ready = sem("mv_ready")
        var_ready = sem("var_ready")
        rstd_ready = sem("rstd_ready")
        shift_ready = sem("shift_ready")
        fin_ready = sem("fin_ready")
        passed_pool = sem("passed_pool")
        passed_dve = sem("passed_dve")
        passed_sp = sem("passed_sp")
        block = ctx.enter_context(nc.Block())

        def first_edge(n):
            return (UNITS - 1) * ET - n * ET

        @block.sync
        def _(sp):
            def load(n, q):
                first = first_edge(n)
                reuse(sp, xd_ready, n - RING + 1)
                reuse(sp, pen_ready, n - RING + 1)
                settle(sp, passed_sp)
                sp.dma_start(ends[q][:, :], m.slots[:, bass.DynSlice(first, ET)]).then_inc(slots_in[q], 16)
                sp.dma_start(goes_on[q][:, :], m.same[:, bass.DynSlice(first + 1, ET)]
                             ).then_inc(slots_in[q], 16)
                reuse(sp, t_done, n - RING + 1)
                settle(sp, passed_sp)
                if isinstance(n, int) and n == 0:
                    rest = E - (EP - P)
                    assert 0 < rest < P
                    sp.wait_ge(e_clear, 1)
                    sp.dma_start(ein[0][:, 0, :], a["edge"][EP - ET:EP - P, :]).then_inc(e_loaded[0], 16)
                    sp.dma_start(ein[0][0:rest, 1, :], a["edge"][EP - P:E, :]).then_inc(e_loaded[0], 16)
                else:
                    sp.dma_start(ein[q][:, :, :], edge_rows(a["edge"], first)).then_inc(e_loaded[q], 16)

            pipeline(sp, UNITS, [(load, -1)])

        @block.gpsimd
        def _(pool):
            def gather(n, q):
                reuse(pool, t_done, n - RING + 1)
                if q % 2 == 0:
                    reuse(pool, gathered[q + 1], 32 * (use(n, q) - 1))
                    settle(pool, passed_pool)
                    nc.gpsimd.tensor_copy(stage[q // 2][:, :, :],
                                          m.src_row[:, bass.DynSlice((UNITS - 2) * ER - n * ER, 2 * ER)]
                                          .rearrange("p (u j) -> p u j", u=2)).then_inc(staged, 2)
                    pool.wait_ge(staged, n + 2)
                settle(pool, passed_pool)
                for j in range(ER):
                    nc.gpsimd.indirect_dma_start(
                        out=gs[q][:, j, :], out_offset=None, in_=m.x1_table,
                        in_offset=bass.IndirectOffsetOnAxis(ap=stage[q // 2][:, 1 - q % 2, j:j + 1], axis=0),
                    ).then_inc(gathered[q], 16)

            def root(n, q):
                pool.wait_ge(var_ready, n + 1)
                reuse(pool, fin_ready, n - RING + 1)
                nc.gpsimd.tensor_tensor(rstd[q][:, :], vare[q][:, :], m.minus_half[:, 0:ER], ALU.pow
                                        ).then_inc(rstd_ready, 1)

            def scatter(n, q):
                if q % 2 == 0:
                    reuse(pool, scattered[q], 32 * (use(n, q) - 1))
                    reuse(pool, scattered[q + 1], 32 * (use(n, q) - 1))
                    settle(pool, passed_pool)
                    nc.gpsimd.tensor_copy(to_stage[q // 2][:, :, :],
                                          m.final_to[:, bass.DynSlice((UNITS - 2) * ER - n * ER, 2 * ER)]
                                          .rearrange("p (u j) -> p u j", u=2)).then_inc(to_staged, 2)
                    pool.wait_ge(to_staged, n + 2)
                pool.wait_ge(fin_ready, n + 1)
                settle(pool, passed_pool)
                for j in range(ER):
                    nc.gpsimd.indirect_dma_start(
                        out=out, in_=fin[q][:, j, :], in_offset=None,
                        out_offset=bass.IndirectOffsetOnAxis(ap=to_stage[q // 2][:, 1 - q % 2, j:j + 1], axis=0),
                        bounds_check=N - 1, oob_is_err=False,
                    ).then_inc(scattered[q], 16)

            pipeline(pool, UNITS, [(scatter, 5), (gather, -2), (root, 3)])
            for q in range(RING):
                pool.wait_ge(scattered[q], 32 * uses(q))

        @block.tensor
        def _(pe):
            def turn_sums(n, q):
                pe.wait_ge(den_ready, n + 1)
                reuse(pe, va_ready, n)
                for j in range(ER):
                    last = nc.tensor.matmul(spread[:, ET + j * H:ET + (j + 1) * H],
                                            den[q % 2][:, j * P:(j + 1) * P], m.ident[0:H, 0:H],
                                            start=True, stop=True)
                last.then_inc(den_turned, 1)

            def spread_weights(n, q):
                pe.wait_ge(al_ready, n + 1)
                for j in range(ER):
                    last = nc.tensor.matmul(spread[:, j * P:(j + 1) * P],
                                            al[q % 2][:, j, :], m.ident[:, :], start=True, stop=True)
                last.then_inc(spread_done, 1)

            def scores(n, q):
                pe.wait_ge(prod_ready, n + 1)
                pe.wait_ge(eT_ready, n + 1)
                pe.wait_ge(v_ready, n + 1)
                nc.tensor.matmul(vs[q % 2][0:H, ET:2 * ET], m.head_sum[:, :], prod[q % 2][:, :],
                                 start=True, stop=False)
                nc.tensor.matmul(vs[q % 2][0:H, ET:2 * ET], m.Wb8[:, :], eT[q % 2][:, :], start=False, stop=True
                                 ).then_inc(sc_done, 1)

            def turn(n, q):
                pe.wait_ge(gathered[q], 32 * use(n, q))
                pe.wait_ge(e_loaded[q], 16 * use(n, q) + (16 if q == 0 else 0))
                reuse(pe, eT_ready, n)
                for j in range(ER):
                    nc.tensor.transpose(turned[:, j * P:(j + 1) * P], gs[q][:, j, :], m.ident[:, :])
                for j in range(ER):
                    last = nc.tensor.transpose(turned[0:ED, ET + j * P:ET + (j + 1) * P], ein[q][:, j, :],
                                               m.ident[:, :])
                last.then_inc(t_done, 1)

            def project(n, q):
                pe.wait_ge(xd_ready, n + 1)
                reuse(pe, prod_ready, n - 1)
                nc.tensor.matmul(qk[q % 2][:, ET:2 * ET], m.Wk[:, :], xd[q][:, :], start=True, stop=True)
                pe.wait_ge(xs_ready, n + 1)
                nc.tensor.matmul(qk[q % 2][:, 0:ET], m.Wq[:, :], xs[q % 2][:, :], start=True, stop=True
                                 ).then_inc(qk_done, 1)
                reuse(pe, sc_ready, n - 1)
                nc.tensor.matmul(vs[q % 2][:, 0:ET], m.Wv[:, :], xd[q][:, :], start=True, stop=True
                                 ).then_inc(v_done, 1)

            def out_rows(n, q):
                pe.wait_ge(va_ready, n + 1)
                reuse(pe, u_ready, n - 1)
                for j in range(ER):
                    cut = slice(j * P, (j + 1) * P)
                    nc.tensor.matmul(rows[q % 2][:, j, :], xd[q][:, cut], m.ident[:, :], start=True, stop=False)
                    last = nc.tensor.matmul(rows[q % 2][:, j, :], va[q % 2][:, cut], m.Wo[:, :],
                                            start=False, stop=True)
                last.then_inc(o_done, 1)

            pipeline(pe, UNITS, [(out_rows, 3), (scores, 1), (turn_sums, 2), (turn, 0), (project, 0), (spread_weights, 2)])

        @block.scalar
        def _(act):
            def take_turned(n, q):
                act.wait_ge(t_done, n + 1)
                reuse(act, qk_done, n - 1)
                nc.scalar.activation(xs[q % 2][:, :], turned[:, 0:ET], ACT.Copy).then_inc(xs_ready, 1)
                reuse(act, sc_done, n - 1)
                nc.scalar.activation(eT[q % 2][:, :], turned[0:ED, ET:2 * ET], ACT.Copy).then_inc(eT_ready, 1)

            def take_projected(n, q):
                act.wait_ge(qk_done, n + 1)
                reuse(act, prod_ready, n - 1)
                nc.scalar.activation(qh[q % 2][:, :], qk[q % 2][:, 0:ET], ACT.Identity, bias=m.bqkv[:, 0:1]
                                     ).then_inc(q_ready, 1)
                act.wait_ge(v_done, n + 1)
                reuse(act, va_ready, n - RING + 1)
                nc.scalar.activation(v[q][:, :], vs[q % 2][:, 0:ET], ACT.Identity, bias=m.bqkv[:, 2:3]
                                     ).then_inc(v_ready, 1)

            def penalty(n, q):
                act.wait_ge(slots_in[q], 32 * use(n, q))
                act.wait_ge(init, 4)
                reuse(act, tmp_ready, n - 1)
                nc.scalar.activation(pen[q % 2][:, :], goes_on[q][0:H, :], ACT.Identity, bias=far[:, 0:1], scale=FAR
                                     ).then_inc(pen_ready, 1)

            def take_scores(n, q):
                act.wait_ge(sc_done, n + 1)
                reuse(act, arg_ready, n - 1)
                nc.scalar.activation(sc[q % 2][:, :], vs[q % 2][0:H, ET:2 * ET], ACT.Identity, bias=m.bb8[:, 0:1]
                                     ).then_inc(sc_ready, 1)

            def exps(n, q):
                act.wait_ge(arg_ready, n + 1)
                reuse(act, den_ready, n - 1)
                nc.scalar.activation(ex[q % 2][:, :, :], arg[q % 2][:, :, :], ACT.Exp).then_inc(ex_ready, 1)

            def norm(n, q):
                act.wait_ge(shift_ready, n + 1)
                reuse(act, scattered[q], 32 * (use(n, q) - 1))
                for j in range(ER):
                    last = nc.scalar.activation(fin[q][:, j, :], u[q % 2][:, j, :], ACT.Identity,
                                                bias=shift[q][:, j:j + 1], scale=rstd[q][:, j:j + 1])
                last.then_inc(fin_ready, 1)

            pipeline(act, UNITS, [(take_scores, 1), (take_turned, 0), (penalty, 0), (norm, 4), (take_projected, 0),
                                  (exps, 1)])

        @block.vector
        def _(dve):
            nc.vector.memset(ein[0][:, :, :], 0.0).then_inc(e_clear, 1)
            nc.vector.memset(xd[RING - 1][:, :], 0.0).then_inc(init, 1)
            nc.vector.memset(mx[1][:, :], 0.0).then_inc(init, 1)
            nc.vector.memset(den[1][:, :], 1.0).then_inc(init, 1)
            nc.vector.memset(far[:, :], -FAR).then_inc(init, 1)
            dve.wait_ge(init, 4)

            def sums(n, q):
                dve.wait_ge(ex_ready, n + 1)
                reuse(dve, den_ready, n)
                reuse(dve, den_turned, n - 1)
                nc.vector.tensor_tensor_scan(den[q % 2][:, ::-1], ex[q % 2][:, 0, ::-1], ex[q % 2][:, 1, ::-1],
                                             den[(q - 1) % 2][:, 0:1], ALU.mult, ALU.add).then_inc(den_ready, 1)

            sums_by_edge = spread[:, ET:ET + ER * H]

            def inverse(n, q):
                dve.wait_ge(den_turned, n + 1)
                reuse(dve, al_ready, n - 1)
                nc.vector.reciprocal(rden[q % 2].rearrange("p j h -> p (j h)"), sums_by_edge).then_inc(rden_ready, 1)

            def weights(n, q):
                dve.wait_ge(rden_ready, n + 1)
                reuse(dve, spread_done, n - 1)
                each = [P, ER * H, HD]
                nc.vector.tensor_tensor(al[q % 2].rearrange("p j (h d) -> p (j h) d", h=H),
                                        sums_by_edge.unsqueeze(2).to_broadcast(each),
                                        rden[q % 2].rearrange("p j h -> p (j h)").unsqueeze(2).to_broadcast(each),
                                        ALU.mult).then_inc(al_ready, 1)

            def products(n, q):
                dve.wait_ge(q_ready, n + 1)
                reuse(dve, sc_done, n - 1)
                nc.vector.scalar_tensor_tensor(out=prod[q % 2][:, :], in0=qk[q % 2][:, ET:2 * ET],
                                               scalar=m.bqkv[:, 1:2], in1=qh[q % 2][:, :],
                                               op0=ALU.add, op1=ALU.mult).then_inc(prod_ready, 1)

            def spread_features(n, q):
                dve.wait_ge(slots_in[q], 32 * use(n, q))
                reuse(dve, xd_ready, n)
                reuse(dve, o_done, n - RING + 1)
                nc.vector.tensor_tensor_scan(xd[q][:, ::-1], goes_on[q][:, ::-1], ends[q][:, ::-1],
                                             xd[q - 1][:, 0:1], ALU.mult, ALU.add).then_inc(xd_ready, 1)

            def weigh(n, q):
                dve.wait_ge(spread_done, n + 1)
                dve.wait_ge(v_ready, n + 1)
                reuse(dve, o_done, n - 1)
                nc.vector.tensor_tensor(va[q % 2][:, :], spread[:, 0:ET], v[q][:, :], ALU.mult
                                        ).then_inc(va_ready, 1)

            def last_maximum(n, q):
                reuse(dve, mx_ready, n)
                reuse(dve, arg_ready, n - 1)
                nc.vector.tensor_copy(mx[q % 2][:, ET:ET + 1], mx[(q - 1) % 2][:, 0:1]).then_inc(tail_ready, 1)

            def maxima(n, q):
                dve.wait_ge(tail_ready, n + 1)
                dve.wait_ge(pen_ready, n + 1)
                dve.wait_ge(sc_ready, n + 1)
                nc.vector.tensor_tensor_scan(mx[q % 2][:, 0:ET][:, ::-1], pen[q % 2][:, ::-1], sc[q % 2][:, ::-1],
                                             mx[q % 2][:, ET:ET + 1], ALU.add, ALU.max).then_inc(mx_ready, 1)

            def exponents(n, q):
                dve.wait_ge(mx_ready, n + 1)
                nc.vector.tensor_tensor(tmp[q % 2][:, :], mx[q % 2][:, 1:ET + 1], pen[q % 2][:, :], ALU.add
                                        ).then_inc(tmp_ready, 1)
                reuse(dve, ex_ready, n - 1)
                nc.vector.tensor_tensor(arg[q % 2][:, 1, :], sc[q % 2][:, :], mx[q % 2][:, 0:ET], ALU.subtract)
                dve.wait_ge(tmp_ready, n + 1)
                nc.vector.tensor_tensor(arg[q % 2][:, 0, :], tmp[q % 2][:, :], mx[q % 2][:, 0:ET], ALU.subtract
                                        ).then_inc(arg_ready, 1)

            def add_bias(n, q):
                dve.wait_ge(o_done, n + 1)
                reuse(dve, fin_ready, n - 1)
                nc.vector.tensor_tensor(u[q % 2][:, :, :], rows[q % 2][:, :, :], m.bo[:, 0:ER, :], ALU.add
                                        ).then_inc(u_ready, 1)

            def moments(n, q):
                dve.wait_ge(u_ready, n + 1)
                for j in range(ER):
                    nc.vector.bn_stats(stats[q][:, j, :], u[q % 2][:, j, :]).then_inc(stats_ready, 1)

            def gather_moments(n, q):
                dve.wait_ge(stats_ready, ER * n + ER)
                settle(dve, passed_dve)
                for j in range(ER):
                    nc.vector.bn_aggr(mv[q][:, j, :], stats[q][:, j, :]).then_inc(mv_ready, 1)

            def guard(n, q):
                dve.wait_ge(mv_ready, ER * n + ER)
                reuse(dve, rstd_ready, n - RING + 1)
                nc.vector.tensor_scalar(vare[q][:, :], mv[q][:, :, 1], LN_EPS, None, ALU.add
                                        ).then_inc(var_ready, 1)

            def shifts(n, q):
                dve.wait_ge(rstd_ready, n + 1)
                reuse(dve, fin_ready, n - RING + 1)
                nc.vector.scalar_tensor_tensor(out=shift[q][:, :], in0=mv[q][:, :, 0], scalar=-1.0,
                                               in1=rstd[q][:, :], op0=ALU.mult, op1=ALU.mult
                                               ).then_inc(shift_ready, 1)

            pipeline(dve, UNITS, [(shifts, 4), (products, 1), (sums, 2), (last_maximum, 1), (spread_features, 0),
                                  (add_bias, 3), (inverse, 2), (moments, 3), (weights, 2), (gather_moments, 3),
                                  (maxima, 1), (guard, 3), (exponents, 1), (weigh, 2)])


def program(nc, a, out):
    with ExitStack() as ctx:
        m = lay_out(nc, ctx)
        prepare(nc, m, a)
        nodes_and_first_layer(nc, m, a, out)
        edge_layer(nc, m, 1)
        edge_layer(nc, m, 2)
        attention(nc, m, a, out)


_INS = {"x": "x", "src": "src", "dst": "dst", "edge_attr_64": "edge",
        "L0_gnn_eps": "eps", "L0_gnn_W1": "W1", "L0_gnn_b1": "b1", "L0_gnn_W2": "W2", "L0_gnn_b2": "b2",
        "L0_gnn_Wf": "Wf", "L0_gnn_bf": "bf",
        "L1_gnn_Wq": "Wq", "L1_gnn_bq": "bq", "L1_gnn_Wk": "Wk", "L1_gnn_bk": "bk", "L1_gnn_Wv": "Wv",
        "L1_gnn_bv": "bv", "L1_gnn_Wb": "Wb", "L1_gnn_bb": "bb", "L1_gnn_Wo": "Wo", "L1_gnn_bo": "bo"}


def kernel(**inputs):
    import numpy as _np
    import concourse.bacc as _bacc
    from concourse import mybir as _mybir
    from concourse.bass_utils import run_bass_kernel_spmd as _run

    nc = _bacc.Bacc("TRN2", target_bir_lowering=False, num_devices=1)
    arrays, args = {}, {}
    for name, short in _INS.items():
        v = _np.ascontiguousarray(inputs[name])
        arrays[f"in_{name}_dram"] = v
        args[short] = nc.dram_tensor(f"in_{name}_dram", v.shape, _mybir.dt.from_np(v.dtype),
                                     kind="ExternalInput").ap()
    out = nc.dram_tensor("out_0_dram", (N, D), _mybir.dt.float32, kind="ExternalOutput").ap()
    program(nc, args, out)
    r = _run(nc, [arrays], core_ids=[0])
    return r.results[0]["out_0_dram"]
```
